# Optimizing a Trainium2 kernel written in Bass

```python
import numpy as np
import jax
import jax.numpy as jnp

def _softmax(x, axis=-1):
    return jax.nn.softmax(x, axis=axis)

def _gelu(x):
    return jax.nn.gelu(x, approximate=True)

def _silu(x):
    return jax.nn.silu(x)

def _sigmoid(x):
    return jax.nn.sigmoid(x)

def _layernorm(x, axis=-1, eps=1e-05):
    m = jnp.mean(x, axis=axis, keepdims=True)
    v = jnp.var(x, axis=axis, keepdims=True)
    return (x - m) / jnp.sqrt(v + eps)

def _scatter_add(tgt, idx, src, axis=0):
    return tgt.at[idx].add(src)

def _segment_sum(src, seg, n):
    return jax.ops.segment_sum(src, seg, n)
kernel_name = 'mk_metaformer_d2_conv_nhwc256_r4_b4b6c2'

def setup_inputs(seed: int=0):
    np.random.seed(seed)
    _w = jnp.asarray

    def _rec_inputs():
        import jax
        import jax.numpy as jnp
        _gk = jax.random.key(seed)
        x = -0.0002928 + 1 * jax.random.normal(jax.random.fold_in(_gk, 1), (4, 16, 16, 64), jnp.float32)
        return x
    x = _rec_inputs()

    def _L0_conv_setup():
        import jax, jax.numpy as jnp
        import numpy as np
        from jax import lax
        N, H, W, C = (4, 16, 16, 64)
        G, K = (8, 3)
        Cg = C // G
        PAD, STRIDE, DIL = (1, 1, 1)
        OFFSET_SCALE = 1.0
        P = K * K

        def _bilinear_sample(img, grid):
            B, Cc, Hi, Wi = img.shape
            x = ((grid[..., 0] + 1.0) * Wi - 1.0) * 0.5
            y = ((grid[..., 1] + 1.0) * Hi - 1.0) * 0.5
            x0 = jnp.floor(x)
            y0 = jnp.floor(y)
            fx = x - x0
            fy = y - y0
            x0i = x0.astype(jnp.int32)
            y0i = y0.astype(jnp.int32)
            flat = img.reshape(B, Cc, Hi * Wi)
            gather = jax.vmap(lambda f, i: f[:, i])

            def corner(xc, yc, w):
                valid = (xc >= 0) & (xc < Wi) & (yc >= 0) & (yc < Hi)
                idx = jnp.clip(yc, 0, Hi - 1) * Wi + jnp.clip(xc, 0, Wi - 1)
                return gather(flat, idx) * (w * valid)[:, None]
            out = corner(x0i, y0i, (1.0 - fx) * (1.0 - fy))
            out = out + corner(x0i + 1, y0i, fx * (1.0 - fy))
            out = out + corner(x0i, y0i + 1, (1.0 - fx) * fy)
            out = out + corner(x0i + 1, y0i + 1, fx * fy)
            return out
        key = jax.random.key(seed)
        ks = jax.random.split(key, 12)
        s = 1.0 / np.sqrt(C)
        return {'x': jax.random.normal(ks[0], (N, H, W, C), jnp.float32), 'in_w': jax.random.normal(ks[1], (C, C), jnp.float32) * s, 'in_b': jnp.zeros((C,), jnp.float32), 'out_w': jax.random.normal(ks[2], (C, C), jnp.float32) * s, 'out_b': jnp.zeros((C,), jnp.float32), 'off_w': jax.random.normal(ks[3], (C, G * P * 2), jnp.float32) * 0.02, 'off_b': jax.random.normal(ks[4], (G * P * 2,), jnp.float32) * 0.1, 'mask_w': jax.random.normal(ks[5], (C, G * P), jnp.float32) * 0.02, 'mask_b': jnp.zeros((G * P,), jnp.float32), 'dw_k': jax.random.normal(ks[6], (C, 1, K, K), jnp.float32) * (1.0 / K), 'bn_g': 1.0 + 0.1 * jax.random.normal(ks[7], (C,), jnp.float32), 'bn_b': 0.1 * jax.random.normal(ks[8], (C,), jnp.float32), 'bn_m': 0.1 * jax.random.normal(ks[9], (C,), jnp.float32), 'bn_v': 1.0 + 0.1 * jax.random.uniform(ks[10], (C,), jnp.float32)}
    _L0_conv_all = _L0_conv_setup()
    _L0_conv_in = {k: v for k, v in _L0_conv_all.items() if k in ('in_w', 'in_b', 'out_w', 'out_b', 'off_w', 'off_b', 'mask_w', 'mask_b', 'dw_k', 'bn_g', 'bn_b', 'bn_m', 'bn_v')}
    del _L0_conv_all

    def _L0_ffn_setup():
        import jax, jax.numpy as jnp
        import numpy as np
        B, T, D, H, E = (16, 1024, 64, 128, 8)
        key = jax.random.key(seed)
        ks = jax.random.split(key, 5)
        x = jax.random.normal(ks[0], (B, T, D), dtype=jnp.float32)
        gate_w = jax.random.normal(ks[1], (D, E), dtype=jnp.float32) * 0.02
        gate_b = jnp.zeros((E,), dtype=jnp.float32)
        W1 = jax.random.normal(ks[2], (E, D, H), dtype=jnp.float32) * 0.02
        b1 = jnp.zeros((E, H), dtype=jnp.float32)
        W2 = jax.random.normal(ks[3], (E, H, D), dtype=jnp.float32) * 0.02
        b2 = jnp.zeros((E, D), dtype=jnp.float32)
        return {'x': x, 'gate_w': gate_w, 'gate_b': gate_b, 'W1': W1, 'b1': b1, 'W2': W2, 'b2': b2}
    _L0_ffn_all = _L0_ffn_setup()
    _L0_ffn_in = {k: v for k, v in _L0_ffn_all.items() if k in ('gate_w', 'gate_b', 'W1', 'b1', 'W2', 'b2')}
    del _L0_ffn_all

    def _L1_conv_setup():
        import jax, jax.numpy as jnp
        import numpy as np
        K = 3
        G = 4

        def conv_same(x, w, b):
            return jax.lax.conv_general_dilated(x, w, (1, 1), 'SAME', dimension_numbers=('NHWC', 'HWIO', 'NHWC')) + b

        def depthwise_same(x, w, b):
            c = x.shape[-1]
            return jax.lax.conv_general_dilated(x, w, (1, 1), 'SAME', dimension_numbers=('NHWC', 'HWIO', 'NHWC'), feature_group_count=c) + b

        def kernel_grid(k, dtype):
            off = (k - 1) / 2.0
            lin = jnp.linspace(-off, off, k).astype(dtype)
            xg, yg = jnp.meshgrid(lin, lin)
            return jnp.stack([xg, yg], axis=-1).reshape(-1, 2)

        def sample_with_offsets(x, offsets, k):
            B, H, W, C = x.shape
            dt = x.dtype
            gy, gx = jnp.meshgrid(jnp.arange(H, dtype=dt), jnp.arange(W, dtype=dt), indexing='ij')
            grid = jnp.stack([gx, gy], axis=-1)[None, :, :, None, :]
            off = offsets.reshape(B, H, W, k * k, 2)
            kg = kernel_grid(k, dt).reshape(1, 1, 1, k * k, 2)
            loc = grid + kg + off
            lx = jnp.clip(loc[..., 0], 0.0, W - 1.0)
            ly = jnp.clip(loc[..., 1], 0.0, H - 1.0)
            x0 = jnp.clip(jnp.floor(lx), 0.0, W - 1.0)
            y0 = jnp.clip(jnp.floor(ly), 0.0, H - 1.0)
            x1 = jnp.clip(x0 + 1.0, 0.0, W - 1.0)
            y1 = jnp.clip(y0 + 1.0, 0.0, H - 1.0)
            wa = (x1 - lx) * (y1 - ly)
            wb = (x1 - lx) * (ly - y0)
            wc = (lx - x0) * (y1 - ly)
            wd = (lx - x0) * (ly - y0)
            flat = x.reshape(B, H * W, C)
            N = H * W * k * k

            def gather(yi, xi):
                idx = (yi * W + xi).astype(jnp.int32).reshape(B, N)
                return jnp.take_along_axis(flat, idx[..., None], axis=1)
            Ia = gather(y0, x0)
            Ib = gather(y1, x0)
            Ic = gather(y0, x1)
            Id = gather(y1, x1)
            w_ = lambda w: w.reshape(B, N, 1)
            interp = w_(wa) * Ia + w_(wb) * Ib + w_(wc) * Ic + w_(wd) * Id
            return interp.reshape(B, H, W, k * k * C)
        key = jax.random.key(seed)
        ks = jax.random.split(key, 6)
        B, H, W, C = (4, 24, 24, 64)
        Cg = C // G
        K2C = K * K * Cg
        GF = 64 // G
        x = jax.random.normal(ks[0], (B, H, W, C), dtype=jnp.float32)
        w_init = jax.random.normal(ks[1], (1, 1, C, C), dtype=jnp.float32) / np.sqrt(C)
        b_init = jnp.zeros((C,), dtype=jnp.float32)
        w_off = jax.random.normal(ks[2], (G, K, K, Cg, 2 * K * K), dtype=jnp.float32) * 0.01
        b_off = jnp.zeros((G, 2 * K * K), dtype=jnp.float32)
        w_dw = jax.random.normal(ks[3], (G, K, K, 1, K2C), dtype=jnp.float32) / 3.0
        b_dw = jnp.zeros((G, K2C), dtype=jnp.float32)
        w_pw = jax.random.normal(ks[4], (G, 1, 1, K2C, GF), dtype=jnp.float32) / np.sqrt(K2C)
        b_pw = jnp.zeros((G, GF), dtype=jnp.float32)
        return {'x': x, 'w_init': w_init, 'b_init': b_init, 'w_off': w_off, 'b_off': b_off, 'w_dw': w_dw, 'b_dw': b_dw, 'w_pw': w_pw, 'b_pw': b_pw}
    _L1_conv_all = _L1_conv_setup()
    _L1_conv_in = {k: v for k, v in _L1_conv_all.items() if k in ('w_init', 'b_init', 'w_off', 'b_off', 'w_dw', 'b_dw', 'w_pw', 'b_pw')}
    del _L1_conv_all

    def _L1_ffn_setup():
        import math
        import jax, jax.numpy as jnp
        import numpy as np
        CAPACITY_FACTOR = 1.25
        key = jax.random.key(seed)
        ks = jax.random.split(key, 5)
        B, L, D, F, E = (8, 2048, 64, 256, 8)
        h = jax.random.normal(ks[0], (B, L, D), dtype=jnp.float32)
        gate_w = jax.random.normal(ks[1], (D, E), dtype=jnp.float32) * 0.02
        gate_b = jnp.zeros((E,), dtype=jnp.float32)
        w1 = jax.random.normal(ks[2], (E, D, F), dtype=jnp.float32) * (1.0 / math.sqrt(D))
        b1 = jnp.zeros((E, F), dtype=jnp.float32)
        w2 = jax.random.normal(ks[3], (E, F, D), dtype=jnp.float32) * (1.0 / math.sqrt(F))
        b2 = jnp.zeros((E, D), dtype=jnp.float32)
        return {'h': h, 'gate_w': gate_w, 'gate_b': gate_b, 'w1': w1, 'b1': b1, 'w2': w2, 'b2': b2}
    _L1_ffn_all = _L1_ffn_setup()
    _L1_ffn_in = {k: v for k, v in _L1_ffn_all.items() if k in ('gate_w', 'gate_b', 'w1', 'b1', 'w2', 'b2')}
    del _L1_ffn_all
    return {'x': x, 'L0_conv_in_w': _L0_conv_in['in_w'], 'L0_conv_in_b': _L0_conv_in['in_b'], 'L0_conv_out_w': _L0_conv_in['out_w'], 'L0_conv_out_b': _L0_conv_in['out_b'], 'L0_conv_off_w': _L0_conv_in['off_w'], 'L0_conv_off_b': _L0_conv_in['off_b'], 'L0_conv_mask_w': _L0_conv_in['mask_w'], 'L0_conv_mask_b': _L0_conv_in['mask_b'], 'L0_conv_dw_k': _L0_conv_in['dw_k'], 'L0_conv_bn_g': _L0_conv_in['bn_g'], 'L0_conv_bn_b': _L0_conv_in['bn_b'], 'L0_conv_bn_m': _L0_conv_in['bn_m'], 'L0_conv_bn_v': _L0_conv_in['bn_v'], 'L0_ffn_gate_w': _L0_ffn_in['gate_w'], 'L0_ffn_gate_b': _L0_ffn_in['gate_b'], 'L0_ffn_W1': _L0_ffn_in['W1'], 'L0_ffn_b1': _L0_ffn_in['b1'], 'L0_ffn_W2': _L0_ffn_in['W2'], 'L0_ffn_b2': _L0_ffn_in['b2'], 'L1_conv_w_init': _L1_conv_in['w_init'], 'L1_conv_b_init': _L1_conv_in['b_init'], 'L1_conv_w_off': _L1_conv_in['w_off'], 'L1_conv_b_off': _L1_conv_in['b_off'], 'L1_conv_w_dw': _L1_conv_in['w_dw'], 'L1_conv_b_dw': _L1_conv_in['b_dw'], 'L1_conv_w_pw': _L1_conv_in['w_pw'], 'L1_conv_b_pw': _L1_conv_in['b_pw'], 'L1_ffn_gate_w': _L1_ffn_in['gate_w'], 'L1_ffn_gate_b': _L1_ffn_in['gate_b'], 'L1_ffn_w1': _L1_ffn_in['w1'], 'L1_ffn_b1': _L1_ffn_in['b1'], 'L1_ffn_w2': _L1_ffn_in['w2'], 'L1_ffn_b2': _L1_ffn_in['b2']}

def reference(x, L0_conv_in_w, L0_conv_in_b, L0_conv_out_w, L0_conv_out_b, L0_conv_off_w, L0_conv_off_b, L0_conv_mask_w, L0_conv_mask_b, L0_conv_dw_k, L0_conv_bn_g, L0_conv_bn_b, L0_conv_bn_m, L0_conv_bn_v, L0_ffn_gate_w, L0_ffn_gate_b, L0_ffn_W1, L0_ffn_b1, L0_ffn_W2, L0_ffn_b2, L1_conv_w_init, L1_conv_b_init, L1_conv_w_off, L1_conv_b_off, L1_conv_w_dw, L1_conv_b_dw, L1_conv_w_pw, L1_conv_b_pw, L1_ffn_gate_w, L1_ffn_gate_b, L1_ffn_w1, L1_ffn_b1, L1_ffn_w2, L1_ffn_b2):
    import jax
    import jax.numpy as jnp

    def _L0_conv_ref(x, in_w, in_b, out_w, out_b, off_w, off_b, mask_w, mask_b, dw_k, bn_g, bn_b, bn_m, bn_v):
        import jax, jax.numpy as jnp
        import numpy as np
        from jax import lax
        N, H, W, C = (4, 16, 16, 64)
        G, K = (8, 3)
        Cg = C // G
        PAD, STRIDE, DIL = (1, 1, 1)
        OFFSET_SCALE = 1.0
        P = K * K

        def _bilinear_sample(img, grid):
            B, Cc, Hi, Wi = img.shape
            x = ((grid[..., 0] + 1.0) * Wi - 1.0) * 0.5
            y = ((grid[..., 1] + 1.0) * Hi - 1.0) * 0.5
            x0 = jnp.floor(x)
            y0 = jnp.floor(y)
            fx = x - x0
            fy = y - y0
            x0i = x0.astype(jnp.int32)
            y0i = y0.astype(jnp.int32)
            flat = img.reshape(B, Cc, Hi * Wi)
            gather = jax.vmap(lambda f, i: f[:, i])

            def corner(xc, yc, w):
                valid = (xc >= 0) & (xc < Wi) & (yc >= 0) & (yc < Hi)
                idx = jnp.clip(yc, 0, Hi - 1) * Wi + jnp.clip(xc, 0, Wi - 1)
                return gather(flat, idx) * (w * valid)[:, None]
            out = corner(x0i, y0i, (1.0 - fx) * (1.0 - fy))
            out = out + corner(x0i + 1, y0i, fx * (1.0 - fy))
            out = out + corner(x0i, y0i + 1, (1.0 - fx) * fy)
            out = out + corner(x0i + 1, y0i + 1, fx * fy)
            return out
        xp = x @ in_w + in_b
        x1 = jnp.transpose(x, (0, 3, 1, 2))
        x1 = lax.conv_general_dilated(x1, dw_k, (1, 1), [(PAD, PAD), (PAD, PAD)], feature_group_count=C)
        x1 = bn_g[:, None, None] * (x1 - bn_m[:, None, None]) * lax.rsqrt(bn_v + 1e-05)[:, None, None] + bn_b[:, None, None]
        x1 = jax.nn.silu(x1)
        x1 = jnp.transpose(x1, (0, 2, 3, 1))
        offset = x1 @ off_w + off_b
        mask = jax.nn.softmax((x1 @ mask_w + mask_b).reshape(N, H, W, G, P), -1)
        Hi, Wi = (H + 2 * PAD, W + 2 * PAD)
        xpad = jnp.pad(xp, ((0, 0), (PAD, PAD), (PAD, PAD), (0, 0)))
        base = DIL * (K - 1) // 2 + 0.5
        ref_y = (base + jnp.arange(H, dtype=jnp.float32) * STRIDE) / Hi
        ref_x = (base + jnp.arange(W, dtype=jnp.float32) * STRIDE) / Wi
        ref = jnp.stack(jnp.meshgrid(ref_x, ref_y, indexing='xy'), -1)
        g1 = jnp.arange(K, dtype=jnp.float32) * DIL - DIL * (K - 1) // 2
        gx = jnp.repeat(g1 / Wi, K)
        gy = jnp.tile(g1 / Hi, K)
        grid = jnp.stack([gx, gy], -1)
        norm = jnp.array([Wi, Hi], jnp.float32)
        loc = ref[None, :, :, None, None, :] + grid[None, None, None, None, :, :] * OFFSET_SCALE + offset.reshape(N, H, W, G, P, 2) * (OFFSET_SCALE / norm)
        sgrid = 2.0 * loc - 1.0
        img = xpad.reshape(N, Hi * Wi, G, Cg).transpose(0, 2, 3, 1).reshape(N * G, Cg, Hi, Wi)
        sg = sgrid.reshape(N, H * W, G, P, 2).transpose(0, 2, 1, 3, 4).reshape(N * G, H * W, P, 2)
        samples = _bilinear_sample(img, sg)
        m = mask.reshape(N, H * W, G, P).transpose(0, 2, 1, 3).reshape(N * G, 1, H * W, P)
        out = (samples * m).sum(-1)
        out = out.reshape(N, C, H * W).transpose(0, 2, 1).reshape(N, H, W, C)
        return out @ out_w + out_b

    def _L0_ffn_ref(x, gate_w, gate_b, W1, b1, W2, b2):
        import jax, jax.numpy as jnp
        import numpy as np
        B, T, D, H, E = (16, 1024, 64, 128, 8)
        Bb, Tt, Dd = x.shape
        Ee = gate_w.shape[1]
        xf = x.reshape(-1, Dd)
        N = xf.shape[0]
        logits = xf @ gate_w + gate_b
        probs = jax.nn.softmax(logits, axis=-1)
        top2_vals, top2_idx = jax.lax.top_k(probs, 2)
        cw = jnp.zeros((N, Ee), dtype=xf.dtype).at[jnp.arange(N)[:, None], top2_idx].add(top2_vals)

        def step(acc, params):
            w1, bb1, w2, bb2, we = params
            h = jax.nn.gelu(xf @ w1 + bb1, approximate=False)
            y = h @ w2 + bb2
            return (acc + we[:, None] * y, None)
        out, _ = jax.lax.scan(step, jnp.zeros_like(xf), (W1, b1, W2, b2, cw.T))
        return out.reshape(Bb, Tt, Dd)

    def _L1_conv_ref(x, w_init, b_init, w_off, b_off, w_dw, b_dw, w_pw, b_pw):
        import jax, jax.numpy as jnp
        import numpy as np
        K = 3
        G = 4

        def conv_same(x, w, b):
            return jax.lax.conv_general_dilated(x, w, (1, 1), 'SAME', dimension_numbers=('NHWC', 'HWIO', 'NHWC')) + b

        def depthwise_same(x, w, b):
            c = x.shape[-1]
            return jax.lax.conv_general_dilated(x, w, (1, 1), 'SAME', dimension_numbers=('NHWC', 'HWIO', 'NHWC'), feature_group_count=c) + b

        def kernel_grid(k, dtype):
            off = (k - 1) / 2.0
            lin = jnp.linspace(-off, off, k).astype(dtype)
            xg, yg = jnp.meshgrid(lin, lin)
            return jnp.stack([xg, yg], axis=-1).reshape(-1, 2)

        def sample_with_offsets(x, offsets, k):
            B, H, W, C = x.shape
            dt = x.dtype
            gy, gx = jnp.meshgrid(jnp.arange(H, dtype=dt), jnp.arange(W, dtype=dt), indexing='ij')
            grid = jnp.stack([gx, gy], axis=-1)[None, :, :, None, :]
            off = offsets.reshape(B, H, W, k * k, 2)
            kg = kernel_grid(k, dt).reshape(1, 1, 1, k * k, 2)
            loc = grid + kg + off
            lx = jnp.clip(loc[..., 0], 0.0, W - 1.0)
            ly = jnp.clip(loc[..., 1], 0.0, H - 1.0)
            x0 = jnp.clip(jnp.floor(lx), 0.0, W - 1.0)
            y0 = jnp.clip(jnp.floor(ly), 0.0, H - 1.0)
            x1 = jnp.clip(x0 + 1.0, 0.0, W - 1.0)
            y1 = jnp.clip(y0 + 1.0, 0.0, H - 1.0)
            wa = (x1 - lx) * (y1 - ly)
            wb = (x1 - lx) * (ly - y0)
            wc = (lx - x0) * (y1 - ly)
            wd = (lx - x0) * (ly - y0)
            flat = x.reshape(B, H * W, C)
            N = H * W * k * k

            def gather(yi, xi):
                idx = (yi * W + xi).astype(jnp.int32).reshape(B, N)
                return jnp.take_along_axis(flat, idx[..., None], axis=1)
            Ia = gather(y0, x0)
            Ib = gather(y1, x0)
            Ic = gather(y0, x1)
            Id = gather(y1, x1)
            w_ = lambda w: w.reshape(B, N, 1)
            interp = w_(wa) * Ia + w_(wb) * Ib + w_(wc) * Ic + w_(wd) * Id
            return interp.reshape(B, H, W, k * k * C)
        B, H, W, C = x.shape
        Cg = C // G
        x = conv_same(x, w_init, b_init)
        xg = x.reshape(B, H, W, G, Cg)
        outs = []
        for g in range(G):
            xi = xg[:, :, :, g, :]
            offsets = conv_same(xi, w_off[g], b_off[g])
            sampled = sample_with_offsets(xi, offsets, K)
            h = depthwise_same(sampled, w_dw[g], b_dw[g])
            outs.append(conv_same(h, w_pw[g], b_pw[g]))
        return jnp.concatenate(outs, axis=-1)

    def _L1_ffn_ref(h, gate_w, gate_b, w1, b1, w2, b2):
        import math
        import jax, jax.numpy as jnp
        import numpy as np
        CAPACITY_FACTOR = 1.25
        B, L, D = h.shape
        E = gate_w.shape[1]
        T = B * L
        C = max(1, math.ceil(CAPACITY_FACTOR * T / E))
        x = h.reshape(T, D)
        logits = x @ gate_w + gate_b
        probs = jax.nn.softmax(logits, axis=-1)
        idx = jnp.argmax(probs, axis=-1)
        prb = jnp.take_along_axis(probs, idx[:, None], axis=1)[:, 0]
        one_hot = jax.nn.one_hot(idx, E, dtype=jnp.float32)
        pos = (jnp.cumsum(one_hot, axis=0) * one_hot).sum(-1).astype(jnp.int32) - 1
        kept = pos < C
        pos_safe = jnp.where(kept, pos, C)
        buf = jnp.zeros((E, C, D), dtype=h.dtype).at[idx, pos_safe].set(x, mode='drop')
        hmid = jax.nn.relu(jnp.einsum('ecd,edf->ecf', buf, w1) + b1[:, None, :])
        ybuf = jnp.einsum('ecf,efd->ecd', hmid, w2) + b2[:, None, :]
        pos_g = jnp.minimum(pos, C - 1)
        y_tok = ybuf[idx, pos_g] * (prb * kept)[:, None]
        y = y_tok.reshape(B, L, D)
        y = jnp.nan_to_num(y, nan=0.0, posinf=10000.0, neginf=-10000.0)
        return y

    def _gn(v, G=32, eps=1e-05):
        B_, H_, W_, C_ = v.shape
        g = v.reshape(B_, H_, W_, G, C_ // G)
        m = jnp.mean(g, axis=(1, 2, 4), keepdims=True)
        s = jnp.var(g, axis=(1, 2, 4), keepdims=True)
        return ((g - m) / jnp.sqrt(s + eps)).reshape(v.shape)

    def _ln_c(v, eps=1e-06):
        m = jnp.mean(v, axis=-1, keepdims=True)
        s = jnp.var(v, axis=-1, keepdims=True)
        return (v - m) / jnp.sqrt(s + eps)

    def _ln_t(v, eps=1e-05):
        m = jnp.mean(v, axis=-1, keepdims=True)
        s = jnp.var(v, axis=-1, keepdims=True)
        return (v - m) / jnp.sqrt(s + eps)

    def _to_tokens(v):
        B_, H_, W_, C_ = v.shape
        return v.reshape(B_, H_ * W_, C_)

    def _from_tokens(t, like):
        return t.reshape(like.shape)
    x = x + _L0_conv_ref(_ln_c(x), L0_conv_in_w, L0_conv_in_b, L0_conv_out_w, L0_conv_out_b, L0_conv_off_w, L0_conv_off_b, L0_conv_mask_w, L0_conv_mask_b, L0_conv_dw_k, L0_conv_bn_g, L0_conv_bn_b, L0_conv_bn_m, L0_conv_bn_v)
    t = _to_tokens(x)
    t = t + _L0_ffn_ref(_ln_t(t), L0_ffn_gate_w, L0_ffn_gate_b, L0_ffn_W1, L0_ffn_b1, L0_ffn_W2, L0_ffn_b2)
    x = _from_tokens(t, x)
    x = x + _L1_conv_ref(_ln_c(x), L1_conv_w_init, L1_conv_b_init, L1_conv_w_off, L1_conv_b_off, L1_conv_w_dw, L1_conv_b_dw, L1_conv_w_pw, L1_conv_b_pw)
    t = _to_tokens(x)
    t = t + _L1_ffn_ref(_ln_t(t), L1_ffn_gate_w, L1_ffn_gate_b, L1_ffn_w1, L1_ffn_b1, L1_ffn_w2, L1_ffn_b2)
    x = _from_tokens(t, x)
    return x

_drawn_inputs = setup_inputs


def setup_inputs(seed=0):
    import zlib

    import numpy as np

    out = dict(_drawn_inputs(seed))
    spreads = {'L0_conv_in_b': (0.0, 0.1),
     'L0_conv_out_b': (0.0, 0.1),
     'L0_ffn_gate_b': (0.0, 0.288),
     'L0_ffn_b1': (0.0, 0.8),
     'L0_ffn_b2': (0.0, 0.283),
     'L1_conv_b_init': (0.0, 0.1),
     'L1_conv_b_off': (0.0, 0.1),
     'L1_conv_b_dw': (0.0, 0.1),
     'L1_conv_b_pw': (0.0, 0.1),
     'L1_ffn_gate_b': (0.0, 0.1),
     'L1_ffn_b1': (0.0, 0.8),
     'L1_ffn_b2': (0.0, 0.705)}
    factors = {'L0_conv_bn_g': 5.45,
     'L0_conv_bn_b': 5.539,
     'L0_conv_bn_m': 4.988,
     'L0_conv_bn_v': 8.0,
     'L0_ffn_W1': 8.0,
     'L0_ffn_W2': 7.506}
    for name, (base, spread) in spreads.items():
        noise = np.random.default_rng([zlib.crc32(name.encode()), seed]).standard_normal(out[name].shape)
        drawn = base * np.exp(spread * noise) if base else spread * noise
        out[name] = jnp.asarray(drawn.astype(out[name].dtype))
    for name, factor in factors.items():
        out[name] = (out[name] * factor).astype(out[name].dtype)
    return out
```

```python
from contextlib import ExitStack

import concourse.bass as bass
from concourse import mybir

F32 = mybir.dt.float32
I32 = mybir.dt.int32
ALU = mybir.AluOpType
ACT = mybir.ActivationFunctionType
AX = mybir.AxisListType

B, H, W, C = 4, 16, 16, 64
P = 128
J = B * H * W // P
HC = J
K = 9
G0, C0 = 8, 8
G1, C1 = 4, 16
GP0, GP1 = G0 * K, G1 * K
E, F0, F1 = 8, 128, 256
CAP = -(-5 * B * H * W // (4 * E))
WIN0 = 2
R0 = 1 + WIN0
R1 = 2
D0, D1 = 2 * WIN0 + 1, 3
N0, N1 = 2 * R0 + 1, 2 * R1 + 1
RB = 15
NB = 2 * RB + 1
BIGV = 3.4028234663852886e38


def V(t, p0, off, dims):
    if isinstance(t, tuple):
        t, off = t[0], t[1] + off
    pitch = 1
    for s in t.shape[1:]:
        pitch *= s
    return bass.AP(tensor=t, offset=p0 * pitch + off,
                   ap=[[dims[0][0] * pitch, dims[0][1]]] + [list(d) for d in dims[1:]])


def program(nc, a, out):
    ctx = ExitStack()
    with ctx:
        def sb(name, *shape, dt=F32):
            return ctx.enter_context(nc.sbuf_tensor(name, list(shape), dt))

        sems = {}

        def sem(name):
            if name not in sems:
                sems[name] = ctx.enter_context(nc.semaphore(name))
            return sems[name]

        def scratch(name, reach):
            return nc.dram_tensor(name, [B, H + 2 * reach, W + 2 * reach, C], F32)
        pad0, pad1 = scratch("pad0", R0), scratch("pad1", R1)
        wide = scratch("wide", RB)

        ps = ctx.enter_context(nc.psum_tensor("ps", [P, 8, 512], F32))

        def bank(i, p0, p1, *dims, off=0):
            return V(ps, p0, 512 * i + off, [[1, p1 - p0], *dims])

        x0 = sb("x0", P, J, C)
        x1 = sb("x1", P, J, C)
        x2 = sb("x2", P, J, C)
        x3 = x1
        xn = sb("xn", P, J, 2, C)
        xT = sb("xT", C + 1, J, P)
        stats = sb("stats", P, J, 6)
        aggr = sb("aggr", P, J, 2)
        veps = sb("veps", P, J)
        rstd = sb("rstd", P, J)
        mhalf = sb("mhalf", P, J)
        ident = sb("ident", P, P)
        tri = sb("tri", P, P)
        img = sb("img", P, J, C)
        zero = sb("zero", P, 1058)
        o_tok = sb("o_tok", P, J, C)
        pidx = sb("pidx", P, 4, dt=I32)
        pf = sb("pf", P, 4)
        gsel = sb("gsel", P, G1)
        e4 = sb("e4", P, G1)
        jneg = sb("jneg", P, J, E)
        cval = sb("cval", P, 8)
        flagf = sb("flagf", P, 4)
        flagi = sb("flagi", 1, 4, dt=I32)
        w_in = sb("w_in", C + 1, C)
        w_out = sb("w_out", C + 1, C)
        w_om = sb("w_om", P, 3 * GP0)
        b_om = sb("b_om", P, 3 * GP0)
        w_dc = sb("w_dc", P, K + 4)
        bn = sb("bn", P, 8)
        w_g0 = sb("w_g0", C + 1, E)
        w_10 = sb("w_10", C + 1, E * F0)
        w_20 = sb("w_20", F0, E * C)
        b_20 = sb("b_20", E, C)
        w_i1 = sb("w_i1", C + 1, 2, C)
        w_of = sb("w_of", P, 2, 54)
        w_ob = sb("w_ob", P, 2, 3, 72)
        b_of = sb("b_of", 72, 1)
        w_dp = sb("w_dp", P, 5, K + C1 + 1)
        w_pb = sb("w_pb", P, 5, C)
        w_cv = sb("w_cv", P, 5, K, C)
        b_pw = sb("b_pw", C, 1)
        b_cv = sb("b_cv", C, 1)
        w_g1 = sb("w_g1", C + 1, E)
        w_11 = sb("w_11", C + 1, E * F1)
        w_21 = sb("w_21", P, 2 * E, C)
        b_21 = sb("b_21", E, C)
        lg = sb("lg", P, J, E)
        lgw = sb("lgw", P, J, E)
        t1 = sb("t1", P, J, E)
        t2 = sb("t2", P, J, E)
        oh1 = sb("oh1", P, J, E)
        oh2 = sb("oh2", P, J, E)
        ex = sb("ex", P, J, E)
        cw = sb("cw", P, J, E)
        m1 = sb("m1", P, J)
        m2 = sb("m2", P, J)
        den = sb("den", P, J)
        cum = sb("cum", P, J, E)
        cwT = sb("cwT", E, J, P)
        ysum = sb("ysum", P, J, C)
        nmask = sb("nmask", P, J * C, dt=I32)
        big1e4 = sb("big1e4", P, 3, 1)
        NP0 = (H + 2) * (W + 2)
        cm = sb("cm", P, 1736)
        cpad, dwc, x1T, cpad1 = (cm, 0), (cm, 2 * NP0), (cm, 2 * NP0 + 2 * H * (W + 2)), (cm, 0)
        ox = sb("ox", P, J * GP0)
        oy = sb("oy", P, J * GP0)
        ml = sb("ml", P, J * GP0)
        m64 = sb("m64", P, J * G0)
        r64 = sb("r64", P, J * G0)
        abx = sb("abx", P, J * GP0)
        aby = sb("aby", P, J * GP0)
        NPR = 4
        BIG = 19248
        big = sb("big", P, BIG)
        ring = sb("ring", P, 4608)
        base1 = sb("base1", P, J * 2 * GP1)
        loc1, u1 = abx, aby
        val1 = sb("val1", P, J * 2 * GP1)
        fslab = sb("fslab", P, (HC + 2 * RB) * C)
        offT = fslab[0:72, 0:B * H * W]
        fy = sb("fy", P, J * GP0)
        fx = sb("fx", P, J * GP0)
        fcnt = sb("fcnt", P, 2)

        def bigv(off, *dims, p=P):
            return V(big, 0, off, [[1, p], *dims])
        SLAB0 = (HC + 2 * R0) * C
        SLAB1 = (HC + 2 * R1) * C
        TX, TY = N0 * SLAB0, N0 * SLAB0 + D0 * J * GP0
        AW = 0
        NA = J * G0 * N0 * N0
        AW = TY + D0 * J * GP0
        assert AW + NA <= BIG
        AD = N1 * SLAB1
        T1 = AD + 9 * J * GP1
        SM = T1 + 3 * J * 2 * GP1
        ST = SM + J * K * C
        STN = B * NP0
        assert ST + 5 * STN <= BIG, ST + 5 * STN

        block = ctx.enter_context(nc.Block())

        def sample_product(eng, V, big, ring, slot, py, d, size, ad):
            dy, dx = divmod(d, 3)
            return eng.tensor_tensor(
                V(ring, 0, slot * 1536, [[1, P], [512, 3], [C1, J * G1], [1, C1]]),
                bigv((py + dy) * size + dx * C, [C, 3], [C1, J * G1], [1, C1]),
                bigv(ad + d * J * GP1 + 3 * py, [1, 3], [K, J * G1], [0, C1]), ALU.mult)

        @block.sync
        def _(sp):
            def load(dst, name, s="wts"):
                sp.dma_start(dst, a[name]).then_inc(sem(s), 16)

            sp.dma_start(x0[:, :, :], a["x"].rearrange("b (r q) w c -> (b r q w) c", r=H)
                         .rearrange("(p j) c -> p j c", j=J)).then_inc(sem("x_in"), 16)
            for hf in range(2):
                sp.dma_start(w_dc[C * hf:C * hf + C, :], a["dc"]).then_inc(sem("w_conv0"), 16)
            load(w_in[:, :], "w_in", "w_proj0")
            for hf in range(2):
                sp.dma_start(w_om[C * hf:C * hf + C, :], a["om"]).then_inc(sem("w_offm"), 16)
            sp.dma_start(b_om[:, :], V2(a["omb"], [[0, P], [1, 3 * GP0]])).then_inc(sem("w_offm"), 16)

            sp.wait_ge(sem("zero_set"), 1)
            for pad, reach in ((pad0, R0), (pad1, R1)):
                n = B * (H + 2 * reach) * (W + 2 * reach) * C // P
                sp.dma_start(V2(pad, [[n, P], [1, n]]), zero[:, 0:n]).then_inc(sem("pad_zeroed"), 16)
            load(w_out[:, :], "w_out", "w_o0")
            load(w_g0[:, :], "w_g0", "w_ffn0")
            load(w_10[:, :], "w_10", "w_ffn0")
            load(w_20[:, :], "w_20", "w_ffn0")
            load(b_20[:, :], "b_20", "w_ffn0")
            for i in range(2):
                load(w_i1[:, i, :], "w_i1", "w_i1")
            load(w_of[:, 0, :], "w_of_a", "w_of")
            load(w_of[0:C, 1, :], "w_of_b", "w_of")
            load(b_of[:, :], "b_of", "w_of")
            sp.dma_start(w_dp[:, 0:4, :], a["w_dp_a"].rearrange("(t q) n -> q t n", t=4)).then_inc(sem("w_dp"), 16)
            load(w_dp[0:C, 4, :], "w_dp_b", "w_dp")
            load(b_pw[:, :], "b_pw", "w_dp")
            load(w_g1[:, :], "w_g1", "w_ffn1")
            load(w_11[:, :], "w_11", "w_ffn1")
            sp.dma_start(w_21[:, :, :], a["w_21"].rearrange("(t q) n -> q t n", q=P)).then_inc(sem("w_ffn1"), 16)
            load(b_21[:, :], "b_21", "w_ffn1")

            def image_out(pad, reach, ready, stored):
                wd = W + 2 * reach
                sp.wait_ge(sem(ready), 1)
                for b in range(B):
                    dst = V2(pad, [[wd * C, H], [HC * C, 2], [1, HC * C]],
                             off=((b * (H + 2 * reach) + reach) * wd + reach) * C)
                    sp.dma_start(dst, V(img, 32 * b, 0, [[2, H], [1, 2], [1, HC * C]])
                                 if False else img[32 * b:32 * b + 32, :, :]).then_inc(sem(stored), 16)

            def slabs_in(pad, reach, stored, arrived):
                wd = W + 2 * reach
                n = 2 * reach + 1
                size = (HC + 2 * reach) * C
                sp.wait_ge(sem(stored), 16 * B)
                for b in range(B):
                    for h in range(2):
                        src = V2(pad, [[wd * C, H], [wd * C, n], [1, size]],
                                 off=(b * (H + 2 * reach) * wd + HC * h) * C)
                        dst = V(big, 32 * b + h, 0, [[2, H], [size, n], [1, size]])
                        sp.dma_start(dst, src).then_inc(sem(arrived), 16)

            def general_loads(tag):
                wd = W + 2 * RB
                flag = sp.value_load(flagi[0:1, tag:tag + 1], min_val=0, max_val=1)
                with sp.If(flag > 0):
                    n = B * (H + 2 * RB) * wd * C // P
                    sp.dma_start(V2(wide, [[n, P], [n // 4, 4], [1, n // 4]]),
                                 V(zero, 0, 0, [[1, P], [0, 4], [1, n // 4]])).then_inc(sem(f"wide_zero{tag}"), 16)
                    sp.wait_ge(sem(f"wide_zero{tag}"), 16)
                    for b in range(B):
                        dst = V2(wide, [[wd * C, H], [HC * C, 2], [1, HC * C]],
                                 off=((b * (H + 2 * RB) + RB) * wd + RB) * C)
                        sp.dma_start(dst, img[32 * b:32 * b + 32, :, :]).then_inc(sem(f"wide_img{tag}"), 16)
                    sp.wait_ge(sem(f"wide_img{tag}"), 16 * B)
                    with sp.Fori(1, NB + 1) as i:
                        sp.wait_ge(sem(f"fslab_used{tag}"), i)
                        for b in range(B):
                            rows = wide.ap()[b, bass.ds(i - 1, H), :, :].rearrange("r w c -> r (w c)")
                            for h in range(2):
                                sp.dma_start(V(fslab, 32 * b + h, 0, [[2, H], [1, (HC + 2 * RB) * C]]),
                                             rows[:, HC * h * C:(HC * h + HC + 2 * RB) * C]
                                             ).then_inc(sem(f"fslab_in{tag}"), 16)
                with sp.Else():
                    sp.nop()

            sp.wait_ge(sem("pad_zeroed"), 32)
            image_out(pad0, R0, "img0", "pad0_stored")
            slabs_in(pad0, R0, "pad0_stored", "slab0")
            sp.wait_ge(sem("flag0"), 1)
            general_loads(0)
            sp.wait_ge(sem("img1"), 1)
            image_out(pad1, R1, "img1", "pad1_stored")
            slabs_in(pad1, R1, "pad1_stored", "slab1")
            sp.wait_ge(sem("flag1"), 1)
            general_loads(1)
            sp.wait_ge(sem("x4"), 1)
            sp.dma_start(out.rearrange("b r w c -> (b r w) c").rearrange("(p j) c -> p j c", j=J),
                         x0[:, :, :]).then_inc(sem("stored"), 16)
            sp.wait_ge(sem("stored"), 16)

        @block.gpsimd
        def _(pool):
            gp = nc.gpsimd
            n = [0]

            def step(ins):
                n[0] += 1
                ins.then_inc(sem("pool_step"), 1)
                pool.wait_ge(sem("pool_step"), n[0])

            gp.memset(mhalf[:, :], -0.5).then_inc(sem("mhalf"), 1)
            gp.memset(V(cpad, 0, 0, [[1, P], [1, 2 * NP0]]), 0.0).then_inc(sem("cpad_zero"), 1)
            step(gp.memset(ident[:, :], 0.0))
            gp.affine_select(out=ident[:, :], in_=ident[:, :], compare_op=ALU.not_equal, fill=1.0, base=0,
                             pattern=[[-1, P]], channel_multiplier=1).then_inc(sem("ident"), 1)
            gp.memset(zero[:, :], 0.0).then_inc(sem("zero_set"), 1)

            def inv_std(k, eps):
                pool.wait_ge(sem("mhalf"), 1)
                pool.wait_ge(sem("var"), k)
                gp.tensor_tensor(rstd[:, :], veps[:, :], mhalf[:, :], ALU.pow).then_inc(sem("rstd"), 1)
            inv_std(1, 0)
            pool.wait_ge(sem("bnv"), 1)
            gp.tensor_tensor(bn[:, 1:2], bn[:, 0:1], mhalf[:, 0:1], ALU.pow).then_inc(sem("bnr"), 1)
            for k in range(D0):
                last = gp.memset(cval[:, k:k + 1], float(WIN0 - k))
            last.then_inc(sem("cval"), 1)
            gp.memset(bigv(AW, [1, NA]), 0.0).then_inc(sem("A_zero"), 1)

            for c in range(1, D0 * D0, 2):
                i = c // 2
                dy, dx = divmod(c, D0)
                pool.wait_ge(sem("tenty"), dy + 1)
                pool.wait_ge(sem("tentx"), dx + 1)
                if i >= 2:
                    pool.wait_ge(sem("poolw_used"), i - 1)
                gp.tensor_tensor(ring[:, 576 * (i % 2):576 * (i % 2) + 576],
                                 bigv(TY + dy * J * GP0, [1, J * GP0]), bigv(TX + dx * J * GP0, [1, J * GP0]),
                                 ALU.mult).then_inc(sem("poolw"), 1)
            pool.wait_ge(sem("slab0"), 128)
            pool.wait_ge(sem("A_done"), 1)
            order = [w for w in range(N0 * N0) if OWNER(w) == "pool"]
            for i, w in enumerate(order):
                if i >= 2:
                    pool.wait_ge(sem("acc0"), PE_COUNT(order[i - 2]))
                wy, wx = divmod(w, N0)
                gp.tensor_tensor(V(ring, 0, 2304 + 512 * (i % 2), [[1, P], [C0, J * G0], [1, C0]]),
                                 bigv(wy * SLAB0 + wx * C, [C0, J * G0], [1, C0]),
                                 bigv(AW + wx * N0 + wy, [N0 * N0, J * G0], [0, C0]),
                                 ALU.mult).then_inc(sem("pool_pr0"), 1)
            inv_std(2, 0)
            gp.memset(V(cpad1, 0, 0, [[1, P], [1, B * NP0]]), 0.0).then_inc(sem("cpad1_zero"), 1)
            gp.iota(pidx[:, 0:1], [[0, 1]], base=0, channel_multiplier=1).then_inc(sem("pidx"), 1)
            gp.iota(e4[:, :], [[1, G1]], base=0, channel_multiplier=0,
                    allow_small_or_imprecise_dtypes=True).then_inc(sem("pidx"), 1)
            for g in range(G1):
                gp.iota(V(base1, 0, g * K, [[1, P], [2 * GP1, J], [3, 3], [1, 3]]),
                        [[1, J], [0, 3], [1, 3]], base=-1, channel_multiplier=0,
                        allow_small_or_imprecise_dtypes=True)
                last = gp.iota(V(base1, 0, GP1 + g * K, [[1, P], [2 * GP1, J], [3, 3], [1, 3]]),
                               [[0, J], [1, 3], [0, 3]], base=-1, channel_multiplier=0,
                               allow_small_or_imprecise_dtypes=True)
            last.then_inc(sem("pidx"), 1)
            step(gp.memset(tri[:, :], 1.0))
            gp.affine_select(out=tri[:, :], in_=tri[:, :], compare_op=ALU.is_gt, fill=0.0, base=0,
                             pattern=[[1, P]], channel_multiplier=-1).then_inc(sem("tri"), 1)
            gp.memset(big1e4[:, 0, :], 1.0e4)
            gp.memset(big1e4[:, 1, :], -1.0e4)
            gp.memset(big1e4[:, 2, :], 0.0).then_inc(sem("limits"), 1)
            inv_std(3, 0)
            pool.wait_ge(sem("w_of"), 48)
            pool.wait_ge(sem("w_dp"), 48)
            pool.wait_ge(sem("gsel"), 1)
            for kt, rows in ((0, P), (1, C)):
                gp.tensor_tensor(V(w_ob, 0, kt * 216, [[1, rows], [36, 6], [9, G1], [1, 9]]),
                                 V(w_of, 0, kt * 54, [[1, rows], [9, 6], [0, G1], [1, 9]]),
                                 V(gsel, 0, 0, [[1, rows], [0, 6], [1, G1], [0, 9]]), ALU.mult
                                 ).then_inc(sem("w_ob"), 1)
            for kt in range(5):
                rows = P if kt < 4 else C
                gp.tensor_tensor(V(w_pb, 0, kt * C, [[1, rows], [C1, G1], [1, C1]]),
                                 V(w_dp, 0, kt * 26 + K, [[1, rows], [0, G1], [1, C1]]),
                                 V(gsel, 0, 0, [[1, rows], [1, G1], [0, C1]]), ALU.mult).then_inc(sem("w_pb"), 1)
            pool.wait_ge(sem("w_pb"), 5)
            for kt in range(5):
                rows = P if kt < 4 else C
                gp.tensor_tensor(V(w_cv, 0, kt * K * C, [[1, rows], [C, K], [1, C]]),
                                 V(w_dp, 0, kt * 26, [[1, rows], [1, K], [0, C]]),
                                 V(w_pb, 0, kt * C, [[1, rows], [0, K], [1, C]]), ALU.mult).then_inc(sem("w_cv"), 1)
            gp.memset(bigv(ST, [1, 5 * STN]), 0.0).then_inc(sem("st_zero"), 1)
            pool.wait_ge(sem("slab1"), 128)
            pool.wait_ge(sem("pairs"), 9)
            k = 0
            for c in range(27):
                if not POOL1(c):
                    continue
                py, d = divmod(c, 9)
                if k >= 1:
                    pool.wait_ge(sem("pool_pr1_used"), k)
                sample_product(gp, V, big, ring, 0, py, d, SLAB1, AD).then_inc(sem("pool_pr1"), 1)
                k += 1
            inv_std(4, 0)

        @block.scalar
        def _(act):
            sc = nc.scalar

            def copy_T(k, src_bank, m=C):
                act.wait_ge(sem("xT_ps"), k)
                if k == 1:
                    act.wait_ge(sem("ones_row"), 1)
                sc.copy(xT[0:m, :, :], bank(src_bank, 0, m, [1, J * P])).then_inc(sem("xT"), 1)

            def gate_exp(k):
                act.wait_ge(sem("gate_in"), k)
                sc.activation(ex[:, :, :], lgw[:, :, :], ACT.Exp).then_inc(sem("gate_ex"), 1)

            copy_T(1, 0)
            act.wait_ge(sem("img0_ps"), 1)
            sc.copy(img[:, :, :], bank(2, 0, P, [1, 512])).then_inc(sem("img0"), 1)
            act.wait_ge(sem("bn"), 1)
            act.wait_ge(sem("dwc"), 1)
            sc.activation(V(x1T, 0, 0, [[1, P], [256, 2], [16, 16], [1, 16]]),
                          V(dwc, 0, 0, [[1, P], [288, 2], [18, 16], [1, 16]]), ACT.Silu,
                          bias=bn[:, 3:4], scale=bn[:, 2:3]).then_inc(sem("x1T"), 1)
            act.wait_ge(sem("offx"), 1)
            act.wait_ge(sem("cval"), 1)
            for k in range(D0):
                if k:
                    act.wait_ge(sem("tentx"), k)
                sc.activation(abx[:, :], ox[:, :], ACT.Abs, bias=cval[:, k:k + 1]).then_inc(sem("abx"), 1)
                act.wait_ge(sem("abx"), k + 1)
                sc.activation(bigv(TX + k * J * GP0, [1, J * GP0]), abx[:, :], ACT.Relu, bias=1.0,
                              scale=-1.0).then_inc(sem("tentx"), 1)
                if k == 0:
                    act.wait_ge(sem("mask_in"), 1)
                    sc.activation(ml[:, :], ml[:, :], ACT.Exp).then_inc(sem("mask_e"), 1)
            copy_T(2, 0)
            copy_T(3, 0)
            gate_exp(1)
            for hf in range(2):
                for e in range(E):
                    i = hf * E + e
                    act.wait_ge(sem("h0_ps"), i + 1)
                    if hf == 1 and e == 0:
                        act.wait_ge(sem("y0_ps"), 4)
                    sc.activation(bigv(e * 512, [1, 512]), bank(i % 2, 0, F0, [1, 512]), ACT.Gelu
                                  ).then_inc(sem("h0"), 1)
                if hf == 0:
                    act.wait_ge(sem("cwT_ps"), 1)
                    sc.copy(cwT[:, :, :], bank(6, 0, E, [1, J * P])).then_inc(sem("cwT"), 1)
            copy_T(4, 0)
            act.wait_ge(sem("img1_ps"), 1)
            sc.copy(img[:, :, :], bank(2, 0, P, [1, 512])).then_inc(sem("img1"), 1)
            act.wait_ge(sem("w_of"), 48)
            act.wait_ge(sem("offT_ps"), 1)
            sc.activation(offT, bank(0, 0, 72, [1, 1024]), ACT.Identity, bias=b_of[:, 0:1]
                          ).then_inc(sem("offT"), 1)
            act.wait_ge(sem("st_zero"), 1)
            for kt in range(5):
                rows = P if kt < 4 else C
                act.wait_ge(sem("st_ps"), kt + 1)
                for b in range(B):
                    sc.copy(V(big, 0, ST + kt * STN + b * NP0 + W + 2 + 1,
                              [[1, rows], [1, J], [W + 2, H], [HC, 2]]),
                            bank(2 * (kt % 2), 0, rows, [P, J], [2, H], [1, 2], off=32 * b)
                            ).then_inc(sem("st"), 1)
            act.wait_ge(sem("b_cv"), 1)
            act.wait_ge(sem("conv_ps"), 1)
            sc.activation(xT[0:C, :, :], bank(4, 0, C, [1, 1024]), ACT.Identity, bias=b_cv[:, 0:1]
                          ).then_inc(sem("convT"), 1)
            copy_T(5, 0)
            gate_exp(2)
            for hf in range(2):
                for f in range(2 * E):
                    i = hf * 2 * E + f
                    act.wait_ge(sem("h1_ps"), i + 1)
                    if hf == 1 and f == 0:
                        act.wait_ge(sem("y1_ps"), 4)
                    sc.activation(bigv(f * 512, [1, 512]), bank(i % 2, 0, P, [1, 512]), ACT.Relu
                                  ).then_inc(sem("h1"), 1)
                if hf == 0:
                    act.wait_ge(sem("cwT_ps"), 2)
                    sc.copy(cwT[:, :, :], bank(6, 0, E, [1, J * P])).then_inc(sem("cwT"), 1)

        @block.tensor
        def _(pe):
            mm, tr = nc.tensor.matmul, nc.tensor.transpose

            def xn_transposes(k, first_bank=0):
                pe.wait_ge(sem("xn"), k)
                pe.wait_ge(sem("ident"), 1)
                for j in range(J):
                    last = tr(bank(first_bank + j // 4, 0, C, [1, P], off=(j % 4) * P), xn[:, j, 0, :], ident[:, :])
                last.then_inc(sem("xT_ps"), 1)

            def project(w, first_bank, width, done, slot=C):
                for j in range(J):
                    last = mm(bank(first_bank, 0, P, [1, width], off=j * slot), xT[:, j, :], w,
                              start=True, stop=True)
                last.then_inc(sem(done), 1)

            pe.wait_ge(sem("xn"), 1)
            pe.wait_ge(sem("ident"), 1)
            for j in range(J):
                last = tr(bank(j // 4, 0, P, [1, P], off=(j % 4) * P), xn[:, j, :, :], ident[:, :])
            last.then_inc(sem("xT_ps"), 1)
            pe.wait_ge(sem("xT"), 1)
            pe.wait_ge(sem("w_proj0"), 16)
            project(w_in[:, :], 2, C, "img0_ps")
            pe.wait_ge(sem("x1T"), 1)
            pe.wait_ge(sem("w_offm"), 48)
            for j in range(J):
                for hf in range(2):
                    p0 = C * hf
                    last = mm(bank(4 + j // 2, p0, p0 + C, [1, 3 * GP0], off=256 * (j % 2)),
                              V(x1T, p0, j, [[1, C], [J, C]]), w_om[p0:p0 + C, :], start=True, stop=True)
            last.then_inc(sem("om_ps"), 1)
            seen = {"pool": 0, "dve": 0}
            first = True
            for w in PE_ORDER:
                who = OWNER(w)
                i = seen[who]
                seen[who] += 1
                pe.wait_ge(sem("pool_pr0" if who == "pool" else "dve_pr0"), i + 1)
                src = (V(ring, 0, 2304 + 512 * (i % 2), [[1, P], [1, 512]]) if who == "pool" else
                       V(ring, 0, 512 * (i % 3), [[1, P], [1, 512]]))
                mm(bank(3, 0, P, [1, 512]), ident[:, :], src, start=first, stop=(w == PE_ORDER[-1])
                   ).then_inc(sem("acc0"), 1)
                first = False
            pe.wait_ge(sem("off_max"), 1)
            tr(bank(2, 0, 1, [1, P]), flagf[:, 0:1], ident[:, :]).then_inc(sem("off_maxT"), 1)
            pe.wait_ge(sem("o_tok"), 1)
            for j in range(J):
                last = tr(bank(j // 4, 0, C, [1, P], off=(j % 4) * P), o_tok[:, j, :], ident[:, :])
            last.then_inc(sem("xT_ps"), 1)
            pe.wait_ge(sem("xT"), 2)
            pe.wait_ge(sem("w_o0"), 16)
            project(w_out[:, :], 2, C, "x1_ps")

            def experts(tag, n, w1, w2, b2, k):
                for hf in range(2):
                    for f in range(n):
                        i = hf * n + f
                        if i >= 2:
                            pe.wait_ge(sem(f"h{tag}"), i - 1)
                        mm(bank(i % 2, 0, P, [1, 512]), w1[:, P * f:P * f + P],
                           xT[:, 4 * hf:4 * hf + 4, :], start=True, stop=True).then_inc(sem(f"h{tag}_ps"), 1)
                    if hf == 0:
                        pe.wait_ge(sem("cw"), k)
                        for j in range(J):
                            last = tr(bank(6 + j // 4, 0, E, [1, P], off=(j % 4) * P), cw[:, j, :], ident[:, :])
                        last.then_inc(sem("cwT_ps"), 1)
                        pe.wait_ge(sem("cwT"), k)
                        for j in range(J):
                            last = mm(bank(5, 0, P, [1, C], off=C * j), cwT[:, j, :], b2[:, :], start=True, stop=True)
                        last.then_inc(sem("yb_ps"), 1)
                    pe.wait_ge(sem(f"h{tag}"), (hf + 1) * n)
                    for jj in range(4):
                        i = 4 * hf + jj
                        if i >= 2:
                            pe.wait_ge(sem(f"y{tag}_used"), i - 1)
                        per = n // E
                        for e in range(E):
                            for f in range(per):
                                ft = e * per + f
                                last = mm(bank(2 + i % 2, 0, P, [1, C], off=e * C),
                                          bigv(ft * 512 + jj * P, [1, P]), w2(ft), start=(f == 0), stop=(f == per - 1),
                                          skip_group_check=True)
                        last.then_inc(sem(f"y{tag}_ps"), 1)

            xn_transposes(2)
            pe.wait_ge(sem("xT"), 3)
            pe.wait_ge(sem("w_ffn0"), 64)
            project(w_g0[:, :], 4, E, "gate_ps", slot=E)
            experts(0, E, w_10, lambda f: w_20[:, C * f:C * f + C], b_20, 1)

            xn_transposes(3)
            pe.wait_ge(sem("xT"), 4)
            pe.wait_ge(sem("w_i1"), 32)
            project(w_i1[:, 0, :], 2, C, "img1_ps")
            for n in range(2):
                last = mm(bank(4 + n, 0, P, [1, 512]), w_i1[:, :, :], xT[:, 4 * n:4 * n + 4, :], start=True, stop=True)
            last.then_inc(sem("imgT_ps"), 1)
            pe.wait_ge(sem("w_ob"), 2)
            pe.wait_ge(sem("cpad1"), 1)
            for n in range(2):
                k = 0
                for kt, rows, dy in ((0, P, 0), (1, C, 2)):
                    for kx in range(3):
                        last = mm(bank(n, 0, 72, [1, 512]), V(w_ob, 0, kt * 216 + kx * 72, [[1, rows], [1, 72]]),
                                  V(cpad1, 0, 2 * n * NP0 + dy * (W + 2) + kx,
                                    [[1, rows], [NP0, 2], [W + 2, H], [1, W]]),
                                  start=(k == 0), stop=(k == 5))
                        k += 1
            last.then_inc(sem("offT_ps"), 1)
            pe.wait_ge(sem("offT"), 1)
            for j in range(J):
                last = tr(bank(2 + j // 4, 0, P, [1, 72], off=(j % 4) * P), V(fslab, 0, j, [[1, 72], [J, P]]),
                          ident[0:72, 0:72])
            last.then_inc(sem("off1_ps"), 1)
            pe.wait_ge(sem("off_max"), 2)
            tr(bank(6, 0, 1, [1, P]), flagf[:, 1:2], ident[:, :]).then_inc(sem("off_maxT"), 1)
            pe.wait_ge(sem("w_pb"), 5)
            for kt in range(5):
                rows = P if kt < 4 else C
                last = mm(bank(7, 0, C, [1, 1]), w_pb[0:rows, kt, :], w_dp[0:rows, kt, K + C1:K + C1 + 1],
                          start=(kt == 0), stop=(kt == 4))
            last.then_inc(sem("b_cv_ps"), 1)
            pe.wait_ge(sem("w_cv"), 5)
            for kt in range(5):
                rows = P if kt < 4 else C
                pe.wait_ge(sem("sampled"), SM_READY[kt])
                if kt >= 2:
                    pe.wait_ge(sem("st"), 4 * (kt - 1))
                if kt == 0:
                    pe.wait_ge(sem("off1"), 1)
                for j in range(J):
                    last = tr(bank(2 * (kt % 2) + j // 4, 0, rows, [1, P], off=(j % 4) * P),
                              bigv(SM + j * K * C + kt * P, [1, rows]), ident[:, :])
                last.then_inc(sem("st_ps"), 1)
                pe.wait_ge(sem("st"), 4 * (kt + 1))
                for n in range(2):
                    for tap in range(K):
                        ky, kx = divmod(tap, 3)
                        last = mm(bank(4 + n, 0, C, [1, 512]), w_cv[0:rows, kt, tap, :],
                                  V(big, 0, ST + kt * STN + 2 * n * NP0 + ky * (W + 2) + kx,
                                    [[1, rows], [NP0, 2], [W + 2, H], [1, W]]),
                                  start=(kt == 0 and tap == 0), stop=(kt == 4 and tap == K - 1))
            last.then_inc(sem("conv_ps"), 1)
            pe.wait_ge(sem("convT"), 1)
            for j in range(J):
                last = tr(bank(2, 0, P, [1, C], off=j * C), V(xT, 0, j, [[1, C], [J, P]]), ident[0:C, 0:C])
            last.then_inc(sem("x3_ps"), 1)

            xn_transposes(4)
            pe.wait_ge(sem("xT"), 5)
            pe.wait_ge(sem("w_ffn1"), 64)
            project(w_g1[:, :], 4, E, "gate_ps", slot=E)
            pe.wait_ge(sem("tri"), 1)
            pe.wait_ge(sem("tot"), 1)
            mm(bank(5, 0, P, [1, E]), tri[:, :], cum[:, J - 1, :], start=True, stop=True).then_inc(sem("before"), 1)
            experts(1, 2 * E, w_11, lambda f: w_21[:, f, :], b_21, 2)

        @block.vector
        def _(dve):
            v = nc.vector
            n = [0]

            def step(ins):
                n[0] += 1
                ins.then_inc(sem("dve_step"), 1)
                dve.wait_ge(sem("dve_step"), n[0])

            def layernorm(k, src, eps, dup):
                for j in range(J):
                    last = v.bn_stats(stats[:, j, :], src[:, j, :])
                step(last)
                for j in range(J):
                    last = v.bn_aggr(aggr[:, j, :], stats[:, j, :])
                step(last)
                v.tensor_scalar(veps[:, :], aggr[:, :, 1], eps, None, ALU.add).then_inc(sem("var"), 1)
                dve.wait_ge(sem("rstd"), k)
                for j in range(J):
                    last = v.tensor_scalar(xn[:, j, 0:dup, :], V(src, 0, j * C, [[1, P], [0, dup], [1, C]]),
                                           aggr[:, j, 0:1], rstd[:, j:j + 1], ALU.subtract, ALU.mult)
                last.then_inc(sem("xn"), 1)

            def off_flag(tag, src, width, limit, op):
                step(v.tensor_reduce(flagf[:, tag:tag + 1], src, AX.X, ALU.max, apply_absolute_value=True))
                v.tensor_copy(flagf[:, 2:3], flagf[:, tag:tag + 1]).then_inc(sem("off_max"), 1)
                return limit, op

            def flag_finish(tag, src_bank, limit, op):
                dve.wait_ge(sem("off_maxT"), tag + 1)
                step(v.tensor_reduce(flagf[0:1, 2:3], bank(src_bank, 0, 1, [1, P]), AX.X, ALU.max))
                v.tensor_scalar(flagi[0:1, tag:tag + 1], flagf[0:1, 2:3], limit, None, op).then_inc(sem(f"flag{tag}"), 1)
                dve.wait_ge(sem(f"flag{tag}"), 1)

            v.memset(xT[C:C + 1, :, :], 1.0).then_inc(sem("ones_row"), 1)
            dve.wait_ge(sem("x_in"), 16)
            layernorm(1, x0, 1e-6, 2)
            dve.wait_ge(sem("w_conv0"), 32)
            v.tensor_scalar(bn[:, 0:1], w_dc[:, K + 3:K + 4], 1e-5, None, ALU.add).then_inc(sem("bnv"), 1)
            dve.wait_ge(sem("xT_ps"), 1)
            dve.wait_ge(sem("cpad_zero"), 1)
            dve.wait_ge(sem("xT"), 1)
            for hf in range(2):
                for b in range(2):
                    last = v.tensor_copy(V(cpad, C * hf, b * NP0 + W + 2 + 1, [[1, C], [1, J], [W + 2, H], [HC, 2]]),
                                         bank(0, C * hf, C * hf + C, [P, J], [2, H], [1, 2],
                                              off=32 * (2 * hf + b)))
            step(last)
            n_dw = 15 * (W + 2) + W
            for tap in range(K):
                ky, kx = divmod(tap, 3)
                src = V(cpad, 0, ky * (W + 2) + kx, [[1, P], [NP0, 2], [1, n_dw]])
                dst = V(dwc, 0, 0, [[1, P], [H * (W + 2), 2], [1, n_dw]])
                if tap == 0:
                    step(v.tensor_scalar(dst, src, w_dc[:, 0:1], None, ALU.mult))
                elif tap < K - 1:
                    step(v.scalar_tensor_tensor(dst, src, w_dc[:, tap:tap + 1], dst, ALU.mult, ALU.add))
                else:
                    v.scalar_tensor_tensor(dst, src, w_dc[:, tap:tap + 1], dst, ALU.mult, ALU.add).then_inc(sem("dwc"), 1)
            dve.wait_ge(sem("bnr"), 1)
            step(v.tensor_tensor(bn[:, 2:3], w_dc[:, K:K + 1], bn[:, 1:2], ALU.mult))
            step(v.tensor_tensor(bn[:, 4:5], w_dc[:, K + 2:K + 3], bn[:, 2:3], ALU.mult))
            v.tensor_tensor(bn[:, 3:4], w_dc[:, K + 1:K + 2], bn[:, 4:5], ALU.subtract).then_inc(sem("bn"), 1)
            dve.wait_ge(sem("om_ps"), 1)
            dve.wait_ge(sem("w_offm"), 48)
            for i, (dst, signal) in enumerate(((ox, "offx"), (ml, "ml"), (oy, "offy"))):
                c0 = {0: 0, 1: 2, 2: 1}[i] * GP0
                v.tensor_tensor(V(dst, 0, 0, [[1, P], [GP0, J], [1, GP0]]),
                                bank(4, 0, P, [256, J], [1, GP0], off=c0),
                                V(b_om, 0, c0, [[1, P], [0, J], [1, GP0]]), ALU.add).then_inc(sem(signal), 1)
            dve.wait_ge(sem("ml"), 1)
            step(v.tensor_reduce(m64[:, :], V(ml, 0, 0, [[1, P], [K, J * G0], [1, K]]), AX.X, ALU.max))
            v.tensor_tensor(V(ml, 0, 0, [[1, P], [K, J * G0], [1, K]]), V(ml, 0, 0, [[1, P], [K, J * G0], [1, K]]),
                            V(m64, 0, 0, [[1, P], [1, J * G0], [0, K]]), ALU.subtract).then_inc(sem("mask_in"), 1)
            dve.wait_ge(sem("offy"), 1)
            step(v.tensor_tensor(fy[:, 0:GP0 * J], ox[:, :], ox[:, :], ALU.mult))
            step(v.tensor_tensor(fx[:, 0:GP0 * J], oy[:, :], oy[:, :], ALU.mult))
            step(v.tensor_tensor(fy[:, 0:GP0 * J], fy[:, 0:GP0 * J], fx[:, 0:GP0 * J], ALU.max))
            v.tensor_reduce(flagf[:, 0:1], fy[:, 0:GP0 * J], AX.X, ALU.max).then_inc(sem("off_max"), 1)
            dve.wait_ge(sem("mask_e"), 1)
            step(v.tensor_reduce(m64[:, :], V(ml, 0, 0, [[1, P], [K, J * G0], [1, K]]), AX.X, ALU.add))
            step(v.reciprocal(r64[:, :], m64[:, :]))
            for k in range(D0):
                d = float(k - WIN0)
                step(v.tensor_scalar(aby[:, :], oy[:, :], -1.0, 1.0 + d, ALU.mult, ALU.add))
                step(v.scalar_tensor_tensor(aby[:, :], oy[:, :], 1.0 - d, aby[:, :], ALU.add, ALU.min))
                v.scalar_tensor_tensor(bigv(TY + k * J * GP0, [1, J * GP0]), aby[:, :], 0.0, ml[:, :],
                                       ALU.max, ALU.mult).then_inc(sem("tenty"), 1)
                dve.wait_ge(sem("tenty"), k + 1)
            dve.wait_ge(sem("A_zero"), 1)
            dve.wait_ge(sem("tenty"), D0)
            for c in range(D0 * D0):
                dy, dx = divmod(c, D0)
                if c % 2:
                    dve.wait_ge(sem("poolw"), c // 2 + 1)
                    src = V(ring, 0, 576 * ((c // 2) % 2), [[1, P], [K, J * G0], [3, 3], [1, 3]])
                else:
                    dve.wait_ge(sem("tentx"), dx + 1)
                    step(v.tensor_tensor(ring[:, 1152:1728], bigv(TY + dy * J * GP0, [1, J * GP0]),
                                         bigv(TX + dx * J * GP0, [1, J * GP0]), ALU.mult))
                    src = V(ring, 0, 1152, [[1, P], [K, J * G0], [3, 3], [1, 3]])
                dst = bigv(AW + dx * N0 + dy, [N0 * N0, J * G0], [N0, 3], [1, 3])
                add = v.tensor_tensor(dst, dst, src, ALU.add)
                if c % 2:
                    add.then_inc(sem("poolw_used"), 1)
                    dve.wait_ge(sem("poolw_used"), c // 2 + 1)
                elif c < D0 * D0 - 1:
                    step(add)
                else:
                    add.then_inc(sem("A_done"), 1)
            dve.wait_ge(sem("A_done"), 1)
            dve.wait_ge(sem("slab0"), 128)
            order = [w for w in range(N0 * N0) if OWNER(w) == "dve"]
            own = [w for w in range(N0 * N0) if OWNER(w) == "sum"]
            acc = V(ring, 0, 3328, [[1, P], [1, 512]])

            def product(w, dst_off):
                wy, wx = divmod(w, N0)
                return v.tensor_tensor(V(ring, 0, dst_off, [[1, P], [C0, J * G0], [1, C0]]),
                                       bigv(wy * SLAB0 + wx * C, [C0, J * G0], [1, C0]),
                                       bigv(AW + wx * N0 + wy, [N0 * N0, J * G0], [0, C0]), ALU.mult)
            todo = list(order)
            k = 0
            for i, w in enumerate(own):
                if i == 0:
                    step(product(w, 3328))
                else:
                    step(product(w, 3840))
                    step(v.tensor_tensor(acc, acc, V(ring, 0, 3840, [[1, P], [1, 512]]), ALU.add))
                while todo and k * len(own) <= i * len(order):
                    if k >= 3:
                        dve.wait_ge(sem("acc0"), PE_COUNT(order[k - 3]))
                    product(todo.pop(0), 512 * (k % 3)).then_inc(sem("dve_pr0"), 1)
                    k += 1
            while todo:
                dve.wait_ge(sem("acc0"), PE_COUNT(order[k - 3]))
                product(todo.pop(0), 512 * (k % 3)).then_inc(sem("dve_pr0"), 1)
                k += 1
            flag_finish(0, 2, float(WIN0 * WIN0), ALU.is_ge)
            dve.wait_ge(sem("acc0"), len(PE_ORDER))
            step(v.tensor_tensor(acc, acc, bank(3, 0, P, [1, 512]), ALU.add))

            def tent_loop(tag, width, xs, ys, prepare, consume):
                prepare()
                m = [0]

                def fstep(ins):
                    m[0] += 1
                    ins.then_inc(sem("general_step"), 1)
                    dve.wait_ge(sem("general_step"), m[0])

                def tent(dst, src, count):
                    fstep(v.tensor_scalar(dst, src, count, None, ALU.subtract))
                    fstep(v.scalar_tensor_tensor(dst, dst, -1.0, dst, ALU.mult, ALU.min))
                    fstep(v.tensor_scalar(dst, dst, 1.0, 0.0, ALU.add, ALU.max))

                v.memset(fcnt[:, 0:1], float(-RB)).then_inc(sem(f"general_start{tag}"), 1)
                dve.wait_ge(sem(f"general_start{tag}"), 1)
                dve.sem_inc(sem(f"fslab_used{tag}"), 1)
                with dve.Fori(1, NB + 1) as i:
                    dve.sem_clear(sem("general_step"))
                    m[0] = 0
                    dve.wait_ge(sem(f"fslab_in{tag}"), i * 128)
                    tent(fy[:, 0:width], ys, fcnt[:, 0:1])
                    fstep(v.memset(fcnt[:, 1:2], float(-RB)))
                    with dve.Fori(0, NB) as k:
                        dve.sem_clear(sem("general_step"))
                        m[0] = 0
                        tent(fx[:, 0:width], xs, fcnt[:, 1:2])
                        fstep(v.tensor_tensor(fx[:, 0:width], fx[:, 0:width], fy[:, 0:width], ALU.mult))
                        consume(fstep, fslab[:, bass.ds(k * C, HC * C)])
                        fstep(v.tensor_scalar(fcnt[:, 1:2], fcnt[:, 1:2], 1.0, None, ALU.add))
                    dve.sem_clear(sem("general_step"))
                    m[0] = 0
                    fstep(v.tensor_scalar(fcnt[:, 0:1], fcnt[:, 0:1], 1.0, None, ALU.add))
                    dve.sem_inc(sem(f"fslab_used{tag}"), 1)

            flag = dve.value_load(flagi[0:1, 0:1], min_val=0, max_val=1)
            with dve.If(flag > 0):
                def prepare0():
                    for ap_, px in ((ox, True), (oy, False)):
                        for t in range(3):
                            o = (3 * t if px else t)
                            vw = V(ap_, 0, o, [[1, P], [K, J * G0], [1 if px else 3, 3]])
                            v.tensor_scalar(vw, vw, float(t - 1), None, ALU.add).then_inc(sem("general_prep0"), 1)
                    v.memset(acc, 0.0).then_inc(sem("general_prep0"), 1)
                    dve.wait_ge(sem("general_prep0"), 7)

                def consume0(istep, slab):
                    istep(v.tensor_tensor(fx[:, :], fx[:, :], ml[:, :], ALU.mult))
                    istep(v.tensor_reduce(m64[:, :], V(fx, 0, 0, [[1, P], [K, J * G0], [1, K]]), AX.X, ALU.add))
                    istep(v.tensor_tensor(V(ring, 0, 3840, [[1, P], [C0, J * G0], [1, C0]]),
                                          slab.rearrange("p (g c) -> p g c", c=C0),
                                          V(m64, 0, 0, [[1, P], [1, J * G0], [0, C0]]), ALU.mult))
                    istep(v.tensor_tensor(acc, acc, V(ring, 0, 3840, [[1, P], [1, 512]]), ALU.add))
                tent_loop(0, J * GP0, ox[:, :], oy[:, :], prepare0, consume0)
            with dve.Else():
                dve.nop()
            v.tensor_tensor(o_tok[:, :, :].rearrange("p j (g c) -> p (j g) c", c=C0),
                            V(ring, 0, 3328, [[1, P], [C0, J * G0], [1, C0]]),
                            V(r64, 0, 0, [[1, P], [1, J * G0], [0, C0]]), ALU.mult).then_inc(sem("o_tok"), 1)
            dve.wait_ge(sem("x1_ps"), 1)
            step(v.tensor_tensor(x1[:, :, :], x0[:, :, :], bank(2, 0, P, [1, 512]), ALU.add))

            JE3 = [[8, J], [1, 8]]

            def je(t):
                return t[:, :, :]

            def bc(t):
                return V(t, 0, 0, [[1, P], [1, J], [0, E]])

            def first_of_max(src, m, dst):
                step(v.tensor_reduce(m[:, :], je(src), AX.X, ALU.max))
                step(v.tensor_tensor(je(t1), je(src), bc(m), ALU.is_equal))
                step(v.tensor_tensor(je(t1), je(t1), je(jneg), ALU.mult))
                step(v.tensor_reduce(den[:, :], je(t1), AX.X, ALU.max))
                step(v.tensor_tensor(je(dst), je(t1), bc(den), ALU.is_equal))

            def weighted_sum(tag, first_bank):
                for i in range(J):
                    dve.wait_ge(sem(f"y{tag}_ps"), i + 1)
                    v.tensor_tensor(V(ring, 0, (i % 2) * E * C, [[1, P], [C, E], [1, C]]), bank(2 + i % 2, 0, P, [C, E], [1, C]),
                                    V(cw, 0, i * E, [[1, P], [1, E], [0, C]]), ALU.mult
                                    ).then_inc(sem(f"y{tag}_used"), 1)
                    dve.wait_ge(sem(f"y{tag}_used"), i + 1)
                    step(v.tensor_reduce(ysum[:, i, :], V(ring, 0, (i % 2) * E * C, [[1, P], [1, C], [C, E]]),
                                         AX.X, ALU.add))

            for e in range(E):
                last = v.memset(jneg[:, :, e:e + 1], float(E - e))
            step(last)
            layernorm(2, x1, 1e-5, 1)
            dve.wait_ge(sem("gate_ps"), 1)
            step(v.tensor_copy(je(lg), bank(4, 0, P, [E, J], [1, E])))
            first_of_max(lg, m1, oh1)
            v.tensor_tensor(je(lgw), je(lg), bc(m1), ALU.subtract).then_inc(sem("gate_in"), 1)
            step(v.tensor_scalar(je(t2), je(oh1), -BIGV, None, ALU.mult))
            step(v.tensor_tensor(je(t2), je(lg), je(t2), ALU.add))
            first_of_max(t2, m2, oh2)
            step(v.tensor_tensor(je(oh1), je(oh1), je(oh2), ALU.add))
            dve.wait_ge(sem("gate_ex"), 1)
            step(v.tensor_reduce(den[:, :], je(ex), AX.X, ALU.add))
            step(v.reciprocal(m2[:, :], den[:, :]))
            step(v.tensor_tensor(je(t1), je(oh1), je(ex), ALU.mult))
            v.tensor_tensor(je(cw), je(t1), bc(m2), ALU.mult).then_inc(sem("cw"), 1)
            dve.wait_ge(sem("cw"), 1)
            dve.wait_ge(sem("pidx"), 3)
            step(v.tensor_scalar(pidx[:, 1:2], pidx[:, 0:1], 1, 1, ALU.bitwise_and, ALU.bitwise_and))
            step(v.tensor_scalar(pidx[:, 2:3], pidx[:, 0:1], 1, 15, ALU.logical_shift_right, ALU.bitwise_and))
            step(v.tensor_scalar(pidx[:, 3:4], pidx[:, 0:1], 4, 3, ALU.logical_shift_right, ALU.bitwise_and))
            step(v.tensor_copy(pf[:, :], pidx[:, :]))
            step(v.tensor_scalar(pf[:, 1:2], pf[:, 1:2], float(HC), None, ALU.mult))
            v.tensor_scalar(gsel[:, :], e4[:, :], pf[:, 3:4], None, ALU.is_equal).then_inc(sem("gsel"), 1)
            for c0, col in ((0, 1), (GP1, 2)):
                vw = V(base1, 0, c0, [[1, P], [2 * GP1, J], [1, GP1]])
                step(v.tensor_scalar(vw, vw, pf[:, col:col + 1], None, ALU.add))
            weighted_sum(0, 2)
            dve.wait_ge(sem("yb_ps"), 1)
            step(v.tensor_tensor(ysum[:, :, :], ysum[:, :, :], bank(5, 0, P, [C, J], [1, C]), ALU.add))
            step(v.tensor_tensor(x2[:, :, :], x1[:, :, :], ysum[:, :, :], ALU.add))

            layernorm(3, x2, 1e-6, 1)
            dve.wait_ge(sem("imgT_ps"), 1)
            dve.wait_ge(sem("cpad1_zero"), 1)
            for hf in range(2):
                for b in range(B):
                    last = v.tensor_copy(
                        V(cpad1, C * hf, b * NP0 + (W + 2) * (1 - hf) + 1, [[1, C], [1, J], [W + 2, H], [HC, 2]]),
                        bank(4, C * hf, C * hf + C, [P, J], [2, H], [1, 2], off=32 * b))
            last.then_inc(sem("cpad1"), 1)
            dve.wait_ge(sem("off1_ps"), 1)
            FU = [[1, P], [1, J * 2 * GP1]]
            step(v.tensor_tensor(V(loc1, 0, 0, [[1, P], [2 * GP1, J], [1, 2 * GP1]]),
                                 bank(2, 0, P, [P, J], [1, 2 * GP1]),
                                 V(base1, 0, 0, [[1, P], [2 * GP1, J], [1, 2 * GP1]]), ALU.add))
            step(v.tensor_scalar(val1[:, :], loc1[:, :], W - 1.0, None, ALU.is_lt))
            step(v.tensor_scalar(loc1[:, :], loc1[:, :], 0.0, W - 1.0, ALU.max, ALU.min))
            v.tensor_tensor(u1[:, :], loc1[:, :], base1[:, :], ALU.subtract).then_inc(sem("off1"), 1)
            dve.wait_ge(sem("off1"), 1)
            step(v.tensor_reduce(flagf[:, 1:2], u1[:, :], AX.X, ALU.max, apply_absolute_value=True))
            v.tensor_copy(flagf[:, 3:4], flagf[:, 1:2]).then_inc(sem("off_max"), 1)
            NT = J * 2 * GP1
            step(v.tensor_scalar(loc1[:, :], u1[:, :], -1.0, 0.0, ALU.mult, ALU.max))
            v.scalar_tensor_tensor(bigv(T1 + 2 * NT, [1, NT]), u1[:, :], 0.0, val1[:, :], ALU.max, ALU.mult)
            step(v.tensor_tensor(bigv(T1, [1, NT]), loc1[:, :], val1[:, :], ALU.mult))
            step(v.tensor_scalar(loc1[:, :], u1[:, :], -1.0, 1.0, ALU.mult, ALU.add))
            step(v.scalar_tensor_tensor(loc1[:, :], u1[:, :], 1.0, loc1[:, :], ALU.add, ALU.min))
            step(v.tensor_tensor(bigv(T1 + NT, [1, NT]), loc1[:, :], val1[:, :], ALU.mult))
            for d in range(9):
                dy, dx = divmod(d, 3)
                v.tensor_tensor(bigv(AD + d * J * GP1, [GP1, J], [1, GP1]),
                                bigv(T1 + dy * NT + GP1, [2 * GP1, J], [1, GP1]),
                                bigv(T1 + dx * NT, [2 * GP1, J], [1, GP1]), ALU.mult).then_inc(sem("pairs"), 1)
            dve.wait_ge(sem("pairs"), 9)
            flag_finish(1, 6, 1.0, ALU.is_gt)
            dve.wait_ge(sem("slab1"), 128)
            def rv(slot):
                return V(ring, 0, slot * 1536, [[1, P], [512, 3], [C, J], [1, C]])

            k = 0
            for c in range(27):
                py, d = divmod(c, 9)
                smp = bigv(SM + py * 3 * C, [C, 3], [K * C, J], [1, C])
                if POOL1(c):
                    k += 1
                    dve.wait_ge(sem("pool_pr1"), k)
                    ins = v.tensor_tensor(smp, smp, rv(0), ALU.add)
                    ins.then_inc(sem("pool_pr1_used"), 1)
                    dve.wait_ge(sem("pool_pr1_used"), k)
                else:
                    step(sample_product(v, V, big, ring, 1 + d % 2, py, d, SLAB1, AD))
                    if d == 1:
                        step(v.tensor_tensor(smp, rv(1), rv(2), ALU.add))
                    elif d > 1:
                        step(v.tensor_tensor(smp, smp, rv(1 + d % 2), ALU.add))
            flag = dve.value_load(flagi[0:1, 1:2], min_val=0, max_val=1)
            with dve.If(flag > 0):
                U = V(u1, 0, 0, [[1, P], [2 * GP1, J], [1, GP1]])

                def prepare1():
                    for c0 in (0, GP1):
                        for t in range(3):
                            for g in range(G1):
                                o = c0 + g * K + (t if c0 == 0 else 3 * t)
                                vw = V(u1, 0, o, [[1, P], [2 * GP1, J], [3 if c0 == 0 else 1, 3]])
                                v.tensor_scalar(vw, vw, float(t - 1), None, ALU.add).then_inc(sem("general_prep1"), 1)
                    dve.wait_ge(sem("general_prep1"), 24)
                    for c0, dst in ((0, ox), (GP1, oy)):
                        v.tensor_copy(V(dst, 0, 0, [[1, P], [GP1, J], [1, GP1]]),
                                      V(u1, 0, c0, [[1, P], [2 * GP1, J], [1, GP1]])).then_inc(sem("general_prep1"), 1)
                    v.tensor_tensor(V(ml, 0, 0, [[1, P], [GP1, J], [1, GP1]]),
                                    V(val1, 0, 0, [[1, P], [2 * GP1, J], [1, GP1]]),
                                    V(val1, 0, GP1, [[1, P], [2 * GP1, J], [1, GP1]]), ALU.mult
                                    ).then_inc(sem("general_prep1"), 1)
                    v.memset(bigv(SM, [1, J * K * C]), 0.0).then_inc(sem("general_prep1"), 1)
                    dve.wait_ge(sem("general_prep1"), 28)

                def consume1(istep, slab):
                    istep(v.tensor_tensor(fx[:, 0:J * GP1], fx[:, 0:J * GP1], ml[:, 0:J * GP1], ALU.mult))
                    for p in range(K):
                        istep(v.tensor_tensor(V(ring, 0, 0, [[1, P], [C1, J * G1], [1, C1]]),
                                              slab.rearrange("p (g c) -> p g c", c=C1),
                                              V(fx, 0, p, [[1, P], [K, J * G1], [0, C1]]), ALU.mult))
                        smp = bigv(SM + p * C, [K * C, J], [1, C])
                        istep(v.tensor_tensor(smp, smp, V(ring, 0, 0, [[1, P], [C, J], [1, C]]), ALU.add))
                tent_loop(1, J * GP1, ox[:, 0:J * GP1], oy[:, 0:J * GP1], prepare1, consume1)
            with dve.Else():
                dve.nop()
            v.tensor_copy(flagf[:, 2:3], bigv(SM, [1, 1])).then_inc(sem("sampled"), 1)
            dve.wait_ge(sem("b_cv_ps"), 1)
            v.tensor_tensor(b_cv[:, :], b_pw[:, :], bank(7, 0, C, [1, 1]), ALU.add).then_inc(sem("b_cv"), 1)
            dve.wait_ge(sem("off1"), 1)
            dve.wait_ge(sem("x3_ps"), 1)
            step(v.tensor_tensor(x3[:, :, :], x2[:, :, :], bank(2, 0, P, [1, 512]), ALU.add))

            layernorm(4, x3, 1e-5, 1)
            dve.wait_ge(sem("gate_ps"), 2)
            step(v.tensor_copy(je(lg), bank(4, 0, P, [E, J], [1, E])))
            first_of_max(lg, m1, oh1)
            v.tensor_tensor(je(lgw), je(lg), bc(m1), ALU.subtract).then_inc(sem("gate_in"), 1)
            step(v.tensor_copy(cum[:, 0, :], oh1[:, 0, :]))
            for j in range(1, J - 1):
                step(v.tensor_tensor(cum[:, j, :], cum[:, j - 1, :], oh1[:, j, :], ALU.add))
            v.tensor_tensor(cum[:, J - 1, :], cum[:, J - 2, :], oh1[:, J - 1, :], ALU.add).then_inc(sem("tot"), 1)
            dve.wait_ge(sem("before"), 1)
            step(v.tensor_tensor(je(t2), je(cum), bank(5, 0, P, [0, J], [1, E]), ALU.add))
            step(v.scalar_tensor_tensor(je(t2), je(t2), float(CAP), je(oh1), ALU.is_le, ALU.mult))
            dve.wait_ge(sem("gate_ex"), 2)
            step(v.tensor_reduce(den[:, :], je(ex), AX.X, ALU.add))
            step(v.reciprocal(m2[:, :], den[:, :]))
            v.tensor_tensor(je(cw), je(t2), bc(m2), ALU.mult).then_inc(sem("cw"), 1)
            dve.wait_ge(sem("cw"), 2)
            weighted_sum(1, 2)
            dve.wait_ge(sem("yb_ps"), 2)
            step(v.tensor_tensor(ysum[:, :, :], ysum[:, :, :], bank(5, 0, P, [C, J], [1, C]), ALU.add))
            dve.wait_ge(sem("limits"), 1)
            ys = V(ysum, 0, 0, [[1, P], [1, J * C]])
            for op, limit, col in ((ALU.is_gt, BIGV, 0), (ALU.is_lt, -BIGV, 1), (None, None, 2)):
                if op is None:
                    step(v.tensor_tensor(nmask[:, :], ys, ys, ALU.not_equal))
                else:
                    step(v.tensor_scalar(nmask[:, :], ys, limit, None, op))
                step(v.copy_predicated(ys, nmask[:, :], V(big1e4, 0, col, [[1, P], [0, J * C]])))
            v.tensor_tensor(x0[:, :, :], x3[:, :, :], ysum[:, :, :], ALU.add).then_inc(sem("x4"), 1)


def V2(t, dims, off=0):
    if isinstance(t, bass.AP):
        return bass.AP(tensor=t.tensor, offset=t.offset + off, ap=[list(d) for d in dims])
    return bass.AP(tensor=t, offset=off, ap=[list(d) for d in dims])


def OWNER(w):
    return ("pool", "sum", "dve", "pool", "sum", "pool", "sum")[w % 7]


PE_ORDER = [w for w in range(N0 * N0) if OWNER(w) != "sum"]


def PE_COUNT(w):
    return PE_ORDER.index(w) + 1


def POOL1(c):
    return c % 9 in (2, 5, 8)


SM_READY = [1, 1, 1, 1, 1]

_ORDER = ["x", "dc", "w_in", "om", "omb", "w_out", "w_g0", "w_10", "w_20", "b_20", "w_i1", "w_of_a", "w_of_b",
          "b_of", "w_dp_a", "w_dp_b", "b_pw", "w_g1", "w_11", "w_21", "b_21"]


def kernel(**inputs):
    import numpy as np
    import concourse.bacc as _bacc
    from concourse.bass_utils import run_bass_kernel_spmd as _run

    i = {k: np.asarray(v) for k, v in inputs.items()}

    def rows(*parts):
        return np.concatenate(parts, axis=0)

    om = i["L0_conv_off_w"].reshape(C, GP0, 2).transpose(0, 2, 1).reshape(C, 2 * GP0)
    omb = i["L0_conv_off_b"].reshape(GP0, 2).transpose(1, 0).reshape(2 * GP0)
    w_of = i["L1_conv_w_off"].reshape(G1, 3, 3, C1, K, 2).transpose(1, 0, 3, 2, 5, 4).reshape(3 * C, 54)
    b_of = i["L1_conv_b_off"].reshape(G1, K, 2).transpose(2, 0, 1).reshape(72, 1)
    w_dw = i["L1_conv_w_dw"].reshape(G1, K, K, C1).transpose(2, 0, 3, 1).reshape(K * C, K)
    w_pw = i["L1_conv_w_pw"].reshape(G1, K, C1, C1).transpose(1, 0, 2, 3).reshape(K * C, C1)
    b_dw = i["L1_conv_b_dw"].reshape(G1, K, C1).transpose(1, 0, 2).reshape(K * C, 1)
    w_dp = np.concatenate([w_dw, w_pw, b_dw], axis=1)
    data = {
        "x": i["x"],
        "dc": np.concatenate([i["L0_conv_dw_k"].reshape(C, K)] +
                             [i["L0_conv_bn_" + s].reshape(C, 1) for s in "gbmv"], axis=1),
        "w_in": rows(i["L0_conv_in_w"], i["L0_conv_in_b"][None]),
        "om": np.concatenate([om, i["L0_conv_mask_w"]], axis=1),
        "omb": np.concatenate([omb, i["L0_conv_mask_b"]]),
        "w_out": rows(i["L0_conv_out_w"], i["L0_conv_out_b"][None]),
        "w_g0": rows(i["L0_ffn_gate_w"], i["L0_ffn_gate_b"][None]),
        "w_10": rows(i["L0_ffn_W1"].transpose(1, 0, 2).reshape(C, E * F0), i["L0_ffn_b1"].reshape(1, E * F0)),
        "w_20": i["L0_ffn_W2"].transpose(1, 0, 2).reshape(F0, E * C),
        "b_20": i["L0_ffn_b2"],
        "w_i1": rows(i["L1_conv_w_init"].reshape(C, C), i["L1_conv_b_init"][None]),
        "w_of_a": w_of[:P], "w_of_b": w_of[P:],
        "b_of": b_of,
        "w_dp_a": w_dp[:4 * P], "w_dp_b": w_dp[4 * P:],
        "b_pw": i["L1_conv_b_pw"].reshape(C, 1),
        "w_g1": rows(i["L1_ffn_gate_w"], i["L1_ffn_gate_b"][None]),
        "w_11": rows(i["L1_ffn_w1"].transpose(1, 0, 2).reshape(C, E * F1), i["L1_ffn_b1"].reshape(1, E * F1)),
        "w_21": i["L1_ffn_w2"].reshape(E * F1, C),
        "b_21": i["L1_ffn_b2"],
    }
    nc = _bacc.Bacc("TRN2", target_bir_lowering=False, num_devices=1)
    arrays, aps = {}, {}
    for name in _ORDER:
        v = np.ascontiguousarray(data[name])
        arrays[f"in_{name}_dram"] = v
        aps[name] = nc.dram_tensor(f"in_{name}_dram", v.shape, F32, kind="ExternalInput").ap()
    out = nc.dram_tensor("out_0_dram", (B, H, W, C), F32, kind="ExternalOutput").ap()
    program(nc, aps, out)
    r = _run(nc, [arrays], core_ids=[0])
    return r.results[0]["out_0_dram"]
```

```python
from contextlib import ExitStack

import concourse.bass as bass
from concourse import mybir

F32 = mybir.dt.float32
I32 = mybir.dt.int32
U32 = mybir.dt.uint32
ALU = mybir.AluOpType
ACT = mybir.ActivationFunctionType
AX = mybir.AxisListType

B, H, W, C = 4, 16, 16, 64
P = 128
J = B * H * W // P
HC = J
K = 9
G0, C0 = 8, 8
G1, C1 = 4, 16
GP0, GP1 = G0 * K, G1 * K
E, F0, F1 = 8, 128, 256
T = B * H * W
CAP = -(-5 * B * H * W // (4 * E))
SLOTS = E * CAP
ST_N = SLOTS // P
QE = CAP // ST_N
WIN0 = 2
R0 = 1 + WIN0
R1 = 2
D0, D1 = 2 * WIN0 + 1, 3
N0, N1 = 2 * R0 + 1, 2 * R1 + 1
HB = -(-2 * E // 3)
RB = 15
NB = 2 * RB + 1
BIGV = 3.4028234663852886e38


def V(t, p0, off, dims):
    if isinstance(t, tuple):
        t, off = t[0], t[1] + off
    pitch = 1
    for s in t.shape[1:]:
        pitch *= s
    return bass.AP(tensor=t, offset=p0 * pitch + off,
                   ap=[[dims[0][0] * pitch, dims[0][1]]] + [list(d) for d in dims[1:]])


def program(nc, a, out):
    ctx = ExitStack()
    with ctx:
        def sb(name, *shape, dt=F32):
            return ctx.enter_context(nc.sbuf_tensor(name, list(shape), dt))

        sems = {}

        def sem(name):
            if name not in sems:
                sems[name] = ctx.enter_context(nc.semaphore(name))
            return sems[name]

        def scratch(name, reach):
            return nc.dram_tensor(name, [B, H + 2 * reach, W + 2 * reach, C], F32)
        pad0, pad1 = scratch("pad0", R0), scratch("pad1", R1)
        wide = scratch("wide", RB)
        slots_in = nc.dram_tensor("slots_in", [SLOTS + T, C], F32)
        slots_out = nc.dram_tensor("slots_out", [SLOTS, C], F32)

        ps = ctx.enter_context(nc.psum_tensor("ps", [P, 8, 512], F32))

        def bank(i, p0, p1, *dims, off=0):
            return V(ps, p0, 512 * i + off, [[1, p1 - p0], *dims])

        x0 = sb("x0", P, J, C)
        x1 = sb("x1", P, J, C)
        x2 = sb("x2", P, J, C)
        x3 = x1
        xn = sb("xn", P, J, 2, C)
        xT = sb("xT", C + 1, J, P)
        stats = sb("stats", P, J, 6)
        aggr = sb("aggr", P, J, 2)
        veps = sb("veps", P, J)
        rstd = sb("rstd", P, J)
        mhalf = sb("mhalf", P, J)
        ident = sb("ident", P, P)
        tri = sb("tri", P, P)
        img = sb("img", P, J, C)
        zero = sb("zero", P, 1058)
        o_tok = sb("o_tok", P, J, C)
        pidx = sb("pidx", P, 4, dt=I32)
        pf = sb("pf", P, 4)
        gsel = sb("gsel", P, G1)
        e4 = sb("e4", P, G1)
        jneg = sb("jneg", P, J, E)
        cval = sb("cval", P, 8)
        flagf = sb("flagf", P, 4)
        flagi = sb("flagi", 1, 4, dt=I32)
        w_in = sb("w_in", C + 1, C)
        w_out = sb("w_out", C + 1, C)
        w_om = sb("w_om", P, 3 * GP0)
        b_om = sb("b_om", P, 3 * GP0)
        w_dc = sb("w_dc", P, K + 4)
        bn = sb("bn", P, 8)
        w_g0 = sb("w_g0", C + 1, E)
        w_10 = sb("w_10", C + 1, E * F0)
        w_20 = sb("w_20", F0, E * C)
        b_20 = sb("b_20", E, C)
        w_i1 = sb("w_i1", C + 1, 2, C)
        w_of = sb("w_of", P, 2, 54)
        w_ob = sb("w_ob", P, 2, 3, 72)
        b_of = sb("b_of", 72, 1)
        w_dp = sb("w_dp", P, 5, K + C1 + 1)
        w_pb = sb("w_pb", P, 5, C)
        w_cv = sb("w_cv", P, 5, 3, 3, C)
        two = sb("two", P, C)
        b_pw = sb("b_pw", C, 1)
        b_cv = sb("b_cv", C, 1)
        w_g1 = sb("w_g1", C + 1, E)
        w_11 = sb("w_11", C + 1, E * F1)
        w_21 = sb("w_21", P, 2 * E, C)
        b_21 = sb("b_21", E, C)
        lg = sb("lg", P, J, E)
        lgw = sb("lgw", P, J, E)
        t1 = sb("t1", P, J, E)
        t2 = sb("t2", P, J, E)
        oh1 = sb("oh1", P, J, E)
        oh2 = sb("oh2", P, J, E)
        ex = sb("ex", P, J, E)
        cw = sb("cw", P, J, E)
        m1 = sb("m1", P, J)
        m2 = sb("m2", P, J)
        den = sb("den", P, J)
        cum = sb("cum", P, J, E)
        cwT = sb("cwT", E, J, P)
        ysum = sb("ysum", P, J, C)
        trash = sb("trash", P, J)
        slot = sb("slot", P, J)
        posf = sb("posf", P, J)
        lost = sb("lost", P, J)
        wtok = sb("wtok", P, J)
        idx_in = sb("idx_in", P, J, dt=U32)
        idx_out = sb("idx_out", P, J, dt=U32)
        nmask = sb("nmask", P, J * C, dt=I32)
        big1e4 = sb("big1e4", P, 3, 1)
        NP0 = (H + 2) * (W + 2)
        cm = sb("cm", P, 1736)
        cpad, dwc, x1T, cpad1 = (cm, 0), (cm, 2 * NP0), (cm, 2 * NP0 + 2 * H * (W + 2)), (cm, 0)
        ox = sb("ox", P, J * GP0)
        oy = sb("oy", P, J * GP0)
        ml = sb("ml", P, J * GP0)
        m64 = sb("m64", P, J * G0)
        r64 = sb("r64", P, J * G0)
        abx = sb("abx", P, J * GP0)
        aby = sb("aby", P, J * GP0)
        NPR = 4
        BIG = 19248
        big = sb("big", P, BIG)
        ring = sb("ring", P, 5120)
        base1 = sb("base1", P, J * 2 * GP1)
        loc1, u1 = abx, aby
        val1 = sb("val1", P, J * 2 * GP1)
        fslab = sb("fslab", P, (HC + 2 * RB) * C)
        offT = fslab[0:72, 0:B * H * W]
        convT_of = (ring, 0)
        convT = ring[:, 0:B * H * W]
        fy = sb("fy", P, J * GP0)
        fx = sb("fx", P, J * GP0)
        fcnt = sb("fcnt", P, 2)

        def bigv(off, *dims, p=P):
            return V(big, 0, off, [[1, p], *dims])
        SLAB0 = (HC + 2 * R0) * C
        SLAB1 = (HC + 2 * R1) * C
        TX, TY = N0 * SLAB0, N0 * SLAB0 + D0 * J * GP0
        AW = 0
        NA = J * G0 * N0 * N0
        AW = TY + D0 * J * GP0
        assert AW + NA <= BIG
        AD = N1 * SLAB1
        T1 = AD + 9 * J * GP1
        SM = T1 + 3 * J * 2 * GP1
        ST = SM + J * K * C
        STN = B * NP0
        XS, XST = 0, ST_N * C
        HS = XST + SLOTS
        YT = HS + 2 * E * CAP
        YS = YT + SLOTS
        YG = YS + ST_N * C
        assert ST + 5 * STN <= BIG, ST + 5 * STN

        block = ctx.enter_context(nc.Block())

        def sample_product(eng, slot, kt, d):
            py, px = divmod(2 * kt, 3)
            dy, dx = divmod(d, 3)
            step = C if px < 2 else SLAB1 - 2 * C
            n = TAPS(kt)
            return eng.tensor_tensor(
                V(ring, 0, slot * 1024, [[1, P], [512, n], [C1, J * G1], [1, C1]]),
                bigv((py + dy) * SLAB1 + (px + dx) * C, [step, n], [C1, J * G1], [1, C1]),
                bigv(AD + d * J * GP1 + 2 * kt, [1, n], [K, J * G1], [0, C1]), ALU.mult)

        @block.sync
        def _(sp):
            def load(dst, name, s="wts"):
                sp.dma_start(dst, a[name]).then_inc(sem(s), 16)

            sp.dma_start(x0[:, :, :], a["x"].rearrange("b (r q) w c -> (b r q w) c", r=H)
                         .rearrange("(p j) c -> p j c", j=J)).then_inc(sem("x_in"), 16)
            for hf in range(2):
                sp.dma_start(w_dc[C * hf:C * hf + C, :], a["dc"]).then_inc(sem("w_conv0"), 16)
            load(w_in[:, :], "w_in", "w_proj0")
            for hf in range(2):
                sp.dma_start(w_om[C * hf:C * hf + C, :], a["om"]).then_inc(sem("w_offm"), 16)
            sp.dma_start(b_om[:, :], V2(a["omb"], [[0, P], [1, 3 * GP0]])).then_inc(sem("w_offm"), 16)

            sp.wait_ge(sem("zero_set"), 1)
            for pad, reach in ((pad0, R0), (pad1, R1)):
                n = B * (H + 2 * reach) * (W + 2 * reach) * C // P
                sp.dma_start(V2(pad, [[n, P], [1, n]]), zero[:, 0:n]).then_inc(sem("pad_zeroed"), 16)
            sp.dma_start(V2(slots_in, [[ST_N * C, P], [1, ST_N * C]]), zero[:, 0:ST_N * C]
                         ).then_inc(sem("slots_zeroed"), 16)
            load(w_out[:, :], "w_out", "w_o0")
            load(w_g0[:, :], "w_g0", "w_ffn0")
            load(w_10[:, :], "w_10", "w_ffn0")
            load(w_20[:, :], "w_20", "w_ffn0")
            load(b_20[:, :], "b_20", "w_ffn0")
            for i in range(2):
                load(w_i1[:, i, :], "w_i1", "w_i1")
            load(w_of[:, 0, :], "w_of_a", "w_of")
            load(w_of[0:C, 1, :], "w_of_b", "w_of")
            load(b_of[:, :], "b_of", "w_of")
            sp.dma_start(w_dp[:, 0:4, :], a["w_dp_a"].rearrange("(t q) n -> q t n", t=4)).then_inc(sem("w_dp"), 16)
            load(w_dp[0:C, 4, :], "w_dp_b", "w_dp")
            load(b_pw[:, :], "b_pw", "w_dp")
            load(w_g1[:, :], "w_g1", "w_ffn1")
            load(w_11[:, :], "w_11", "w_ffn1")
            sp.dma_start(w_21[:, :, :], a["w_21"].rearrange("(t q) n -> q t n", q=P)).then_inc(sem("w_ffn1"), 16)
            load(b_21[:, :], "b_21", "w_ffn1")

            def image_out(pad, reach, ready, stored):
                wd = W + 2 * reach
                sp.wait_ge(sem(ready), 1)
                for b in range(B):
                    dst = V2(pad, [[wd * C, H], [HC * C, 2], [1, HC * C]],
                             off=((b * (H + 2 * reach) + reach) * wd + reach) * C)
                    sp.dma_start(dst, V(img, 32 * b, 0, [[2, H], [1, 2], [1, HC * C]])
                                 if False else img[32 * b:32 * b + 32, :, :]).then_inc(sem(stored), 16)

            def slabs_in(pad, reach, stored, arrived):
                wd = W + 2 * reach
                n = 2 * reach + 1
                size = (HC + 2 * reach) * C
                sp.wait_ge(sem(stored), 16 * B)
                for b in range(B):
                    for h in range(2):
                        src = V2(pad, [[wd * C, H], [wd * C, n], [1, size]],
                                 off=(b * (H + 2 * reach) * wd + HC * h) * C)
                        dst = V(big, 32 * b + h, 0, [[2, H], [size, n], [1, size]])
                        sp.dma_start(dst, src).then_inc(sem(arrived), 16)

            def general_loads(tag):
                wd = W + 2 * RB
                flag = sp.value_load(flagi[0:1, tag:tag + 1], min_val=0, max_val=1)
                with sp.If(flag > 0):
                    n = B * (H + 2 * RB) * wd * C // P
                    sp.dma_start(V2(wide, [[n, P], [n // 4, 4], [1, n // 4]]),
                                 V(zero, 0, 0, [[1, P], [0, 4], [1, n // 4]])).then_inc(sem(f"wide_zero{tag}"), 16)
                    sp.wait_ge(sem(f"wide_zero{tag}"), 16)
                    for b in range(B):
                        dst = V2(wide, [[wd * C, H], [HC * C, 2], [1, HC * C]],
                                 off=((b * (H + 2 * RB) + RB) * wd + RB) * C)
                        sp.dma_start(dst, img[32 * b:32 * b + 32, :, :]).then_inc(sem(f"wide_img{tag}"), 16)
                    sp.wait_ge(sem(f"wide_img{tag}"), 16 * B)
                    with sp.Fori(1, NB + 1) as i:
                        sp.wait_ge(sem(f"fslab_used{tag}"), i)
                        for b in range(B):
                            rows = wide.ap()[b, bass.ds(i - 1, H), :, :].rearrange("r w c -> r (w c)")
                            for h in range(2):
                                sp.dma_start(V(fslab, 32 * b + h, 0, [[2, H], [1, (HC + 2 * RB) * C]]),
                                             rows[:, HC * h * C:(HC * h + HC + 2 * RB) * C]
                                             ).then_inc(sem(f"fslab_in{tag}"), 16)
                with sp.Else():
                    sp.nop()

            sp.wait_ge(sem("pad_zeroed"), 32)
            image_out(pad0, R0, "img0", "pad0_stored")
            slabs_in(pad0, R0, "pad0_stored", "slab0")
            sp.wait_ge(sem("flag0"), 1)
            general_loads(0)
            sp.wait_ge(sem("img1"), 1)
            image_out(pad1, R1, "img1", "pad1_stored")
            slabs_in(pad1, R1, "pad1_stored", "slab1")
            sp.wait_ge(sem("flag1"), 1)
            general_loads(1)
            sp.wait_ge(sem("scattered"), 16 * J)
            sp.dma_start(bigv(XS, [1, ST_N * C]), V2(slots_in, [[ST_N * C, P], [1, ST_N * C]])
                         ).then_inc(sem("slots_loaded"), 16)
            sp.wait_ge(sem("ys"), 1)
            sp.dma_start(V2(slots_out, [[ST_N * C, P], [1, ST_N * C]]), bigv(YS, [1, ST_N * C])
                         ).then_inc(sem("slots_stored"), 16)
            sp.wait_ge(sem("x4"), 1)
            sp.dma_start(out.rearrange("b r w c -> (b r w) c").rearrange("(p j) c -> p j c", j=J),
                         x0[:, :, :]).then_inc(sem("stored"), 16)
            sp.wait_ge(sem("stored"), 16)

        @block.gpsimd
        def _(pool):
            gp = nc.gpsimd
            n = [0]

            def step(ins):
                n[0] += 1
                ins.then_inc(sem("pool_step"), 1)
                pool.wait_ge(sem("pool_step"), n[0])

            gp.memset(mhalf[:, :], -0.5).then_inc(sem("mhalf"), 1)
            gp.memset(V(cpad, 0, 0, [[1, P], [1, 2 * NP0]]), 0.0).then_inc(sem("cpad_zero"), 1)
            step(gp.memset(ident[:, :], 0.0))
            gp.affine_select(out=ident[:, :], in_=ident[:, :], compare_op=ALU.not_equal, fill=1.0, base=0,
                             pattern=[[-1, P]], channel_multiplier=1).then_inc(sem("ident"), 1)
            gp.memset(zero[:, :], 0.0).then_inc(sem("zero_set"), 1)

            def inv_std(k, eps):
                pool.wait_ge(sem("mhalf"), 1)
                pool.wait_ge(sem("var"), k)
                gp.tensor_tensor(rstd[:, :], veps[:, :], mhalf[:, :], ALU.pow).then_inc(sem("rstd"), 1)
            inv_std(1, 0)
            pool.wait_ge(sem("bnv"), 1)
            gp.tensor_tensor(bn[:, 1:2], bn[:, 0:1], mhalf[:, 0:1], ALU.pow).then_inc(sem("bnr"), 1)
            for k in range(D0):
                last = gp.memset(cval[:, k:k + 1], float(WIN0 - k))
            last.then_inc(sem("cval"), 1)
            gp.memset(bigv(AW, [1, NA]), 0.0).then_inc(sem("A_zero"), 1)

            for c in range(1, D0 * D0, 2):
                i = c // 2
                dy, dx = divmod(c, D0)
                pool.wait_ge(sem("tenty"), dy + 1)
                pool.wait_ge(sem("tentx"), dx + 1)
                if i >= 2:
                    pool.wait_ge(sem("poolw_used"), i - 1)
                gp.tensor_tensor(ring[:, 576 * (i % 2):576 * (i % 2) + 576],
                                 bigv(TY + dy * J * GP0, [1, J * GP0]), bigv(TX + dx * J * GP0, [1, J * GP0]),
                                 ALU.mult).then_inc(sem("poolw"), 1)
            pool.wait_ge(sem("slab0"), 128)
            pool.wait_ge(sem("A_done"), 1)
            order = [w for w in range(N0 * N0) if OWNER(w) == "pool"]
            for i, w in enumerate(order):
                if i >= 2:
                    pool.wait_ge(sem("acc0"), PE_COUNT(order[i - 2]))
                wy, wx = divmod(w, N0)
                gp.tensor_tensor(V(ring, 0, 2304 + 512 * (i % 2), [[1, P], [C0, J * G0], [1, C0]]),
                                 bigv(wy * SLAB0 + wx * C, [C0, J * G0], [1, C0]),
                                 bigv(AW + wx * N0 + wy, [N0 * N0, J * G0], [0, C0]),
                                 ALU.mult).then_inc(sem("pool_pr0"), 1)
            inv_std(2, 0)
            gp.memset(V(cpad1, 0, 0, [[1, P], [1, B * NP0]]), 0.0).then_inc(sem("cpad1_zero"), 1)
            gp.iota(pidx[:, 0:1], [[0, 1]], base=0, channel_multiplier=1).then_inc(sem("pidx"), 1)
            gp.iota(e4[:, :], [[1, G1]], base=0, channel_multiplier=0,
                    allow_small_or_imprecise_dtypes=True).then_inc(sem("pidx"), 1)
            gp.iota(trash[:, :], [[1, J]], base=SLOTS, channel_multiplier=J,
                    allow_small_or_imprecise_dtypes=True)
            for g in range(G1):
                gp.iota(V(base1, 0, g * K, [[1, P], [2 * GP1, J], [3, 3], [1, 3]]),
                        [[1, J], [0, 3], [1, 3]], base=-1, channel_multiplier=0,
                        allow_small_or_imprecise_dtypes=True)
                last = gp.iota(V(base1, 0, GP1 + g * K, [[1, P], [2 * GP1, J], [3, 3], [1, 3]]),
                               [[0, J], [1, 3], [0, 3]], base=-1, channel_multiplier=0,
                               allow_small_or_imprecise_dtypes=True)
            last.then_inc(sem("pidx"), 1)
            step(gp.memset(tri[:, :], 1.0))
            gp.affine_select(out=tri[:, :], in_=tri[:, :], compare_op=ALU.is_gt, fill=0.0, base=0,
                             pattern=[[1, P]], channel_multiplier=-1).then_inc(sem("tri"), 1)
            gp.tensor_tensor(two[:, :], ident[:, 0:C], ident[:, C:P], ALU.add).then_inc(sem("two"), 1)
            gp.memset(big1e4[:, 0, :], 1.0e4)
            gp.memset(big1e4[:, 1, :], -1.0e4)
            gp.memset(big1e4[:, 2, :], 0.0).then_inc(sem("limits"), 1)
            inv_std(3, 0)
            pool.wait_ge(sem("w_of"), 48)
            pool.wait_ge(sem("w_dp"), 48)
            pool.wait_ge(sem("gsel"), 1)
            for kt, rows in ((0, P), (1, C)):
                gp.tensor_tensor(V(w_ob, 0, kt * 216, [[1, rows], [36, 6], [9, G1], [1, 9]]),
                                 V(w_of, 0, kt * 54, [[1, rows], [9, 6], [0, G1], [1, 9]]),
                                 V(gsel, 0, 0, [[1, rows], [0, 6], [1, G1], [0, 9]]), ALU.mult
                                 ).then_inc(sem("w_ob"), 1)
            for kt in range(5):
                rows = P if kt < 4 else C
                gp.tensor_tensor(V(w_pb, 0, kt * C, [[1, rows], [C1, G1], [1, C1]]),
                                 V(w_dp, 0, kt * 26 + K, [[1, rows], [0, G1], [1, C1]]),
                                 V(gsel, 0, 0, [[1, rows], [1, G1], [0, C1]]), ALU.mult).then_inc(sem("w_pb"), 1)
            pool.wait_ge(sem("w_pb"), 5)
            for kt in range(5):
                rows = P if kt < 4 else C
                gp.tensor_tensor(V(w_cv, 0, kt * K * C, [[1, rows], [3 * C, 3], [C, 3], [1, C]]),
                                 V(w_dp, 0, kt * 26, [[1, rows], [1, 3], [3, 3], [0, C]]),
                                 V(w_pb, 0, kt * C, [[1, rows], [0, 3], [0, 3], [1, C]]), ALU.mult
                                 ).then_inc(sem("w_cv"), 1)
            gp.memset(bigv(ST, [1, 5 * STN]), 0.0).then_inc(sem("st_zero"), 1)
            pool.wait_ge(sem("slab1"), 128)
            pool.wait_ge(sem("pairs"), 9)
            for kt in range(5):
                for d in POOL_D:
                    k = kt * len(POOL_D) + POOL_D.index(d)
                    if k >= 3:
                        pool.wait_ge(sem("pool_pr1_used"), k - 2)
                    sample_product(gp, k % 3, kt, d).then_inc(sem("pool_pr1"), 1)
            inv_std(4, 0)
            pool.wait_ge(sem("slots_zeroed"), 16)
            pool.wait_ge(sem("idx"), 2)
            pool.wait_ge(sem("xn"), 4)
            for j in range(J):
                gp.indirect_dma_start(out=slots_in.ap(), out_offset=bass.IndirectOffsetOnAxis(
                    ap=idx_in[:, j:j + 1], axis=0), in_=xn[:, j, 0, :], in_offset=None
                ).then_inc(sem("scattered"), 16)
            pool.wait_ge(sem("slots_stored"), 16)
            for j in range(J):
                gp.indirect_dma_start(out=bigv(YG + j * C, [1, C]), out_offset=None, in_=slots_out.ap(),
                                      in_offset=bass.IndirectOffsetOnAxis(ap=idx_out[:, j:j + 1], axis=0)
                                      ).then_inc(sem("gathered"), 16)

        @block.scalar
        def _(act):
            sc = nc.scalar

            def copy_T(k, src_bank, m=C):
                act.wait_ge(sem("xT_ps"), k)
                if k == 1:
                    act.wait_ge(sem("ones_row"), 1)
                sc.copy(xT[0:m, :, :], bank(src_bank, 0, m, [1, J * P])).then_inc(sem("xT"), 1)

            def gate_exp(k):
                act.wait_ge(sem("gate_in"), k)
                sc.activation(ex[:, :, :], lgw[:, :, :], ACT.Exp).then_inc(sem("gate_ex"), 1)

            copy_T(1, 0)
            act.wait_ge(sem("img0_ps"), 1)
            sc.copy(img[:, :, :], bank(2, 0, P, [1, 512])).then_inc(sem("img0"), 1)
            act.wait_ge(sem("bn"), 1)
            act.wait_ge(sem("dwc"), 1)
            sc.activation(V(x1T, 0, 0, [[1, P], [256, 2], [16, 16], [1, 16]]),
                          V(dwc, 0, 0, [[1, P], [288, 2], [18, 16], [1, 16]]), ACT.Silu,
                          bias=bn[:, 3:4], scale=bn[:, 2:3]).then_inc(sem("x1T"), 1)
            act.wait_ge(sem("offx"), 1)
            act.wait_ge(sem("cval"), 1)
            for k in range(D0):
                if k:
                    act.wait_ge(sem("tentx"), k)
                sc.activation(abx[:, :], ox[:, :], ACT.Abs, bias=cval[:, k:k + 1]).then_inc(sem("abx"), 1)
                act.wait_ge(sem("abx"), k + 1)
                sc.activation(bigv(TX + k * J * GP0, [1, J * GP0]), abx[:, :], ACT.Relu, bias=1.0,
                              scale=-1.0).then_inc(sem("tentx"), 1)
                if k == 0:
                    act.wait_ge(sem("mask_in"), 1)
                    sc.activation(ml[:, :], ml[:, :], ACT.Exp).then_inc(sem("mask_e"), 1)
            copy_T(2, 0)
            copy_T(3, 0)
            gate_exp(1)
            for hf in range(2):
                for e in range(E):
                    i = hf * E + e
                    act.wait_ge(sem("h0_ps"), i + 1)
                    if hf == 1 and e == 0:
                        act.wait_ge(sem("y0_ps"), 4)
                    sc.activation(bigv(e * 512, [1, 512]), bank(i % 2, 0, F0, [1, 512]), ACT.Gelu
                                  ).then_inc(sem("h0"), 1)
                if hf == 0:
                    act.wait_ge(sem("cwT_ps"), 1)
                    sc.copy(cwT[:, :, :], bank(6, 0, E, [1, J * P])).then_inc(sem("cwT"), 1)
            copy_T(4, 0)
            act.wait_ge(sem("img1_ps"), 1)
            sc.copy(img[:, :, :], bank(2, 0, P, [1, 512])).then_inc(sem("img1"), 1)
            act.wait_ge(sem("w_of"), 48)
            act.wait_ge(sem("offT_ps"), 1)
            sc.activation(offT, bank(0, 0, 72, [1, 1024]), ACT.Identity, bias=b_of[:, 0:1]
                          ).then_inc(sem("offT"), 1)
            act.wait_ge(sem("st_zero"), 1)
            for kt in range(5):
                rows = P if kt < 4 else C
                act.wait_ge(sem("st_ps"), kt + 1)
                for b in range(B):
                    sc.copy(V(big, 0, ST + kt * STN + b * NP0 + W + 2 + 1,
                              [[1, rows], [1, J], [W + 2, H], [HC, 2]]),
                            bank(2 * (kt % 2), 0, rows, [P, J], [2, H], [1, 2], off=32 * b)
                            ).then_inc(sem("st"), 1)
            act.wait_ge(sem("b_cv"), 1)
            act.wait_ge(sem("conv_ps"), 1)
            sc.activation(convT[0:C, :], bank(4, 0, C, [1, 1024]), ACT.Identity, bias=b_cv[:, 0:1]
                          ).then_inc(sem("convT"), 1)
            copy_T(5, 0)
            gate_exp(2)
            act.wait_ge(sem("cwT_ps"), 2)
            sc.copy(cwT[:, :, :], bank(6, 0, E, [1, J * P])).then_inc(sem("cwT"), 1)
            act.wait_ge(sem("xs_ps"), 1)
            sc.copy(bigv(XST, [1, 1024], p=C), bank(0, 0, C, [1, 1024])).then_inc(sem("xsT"), 1)
            for n in range(HB):
                if n % 2 == 0:
                    act.wait_ge(sem("h1_ps"), n + 1)
                    w = min(3, 2 * E - 3 * n) * CAP
                    sc.activation(bigv(HS + n * 3 * CAP, [1, w]), bank(n, 0, P, [1, w]), ACT.Relu
                                  ).then_inc(sem("h1_act"), 1)

        @block.tensor
        def _(pe):
            mm, tr = nc.tensor.matmul, nc.tensor.transpose

            def xn_transposes(k, first_bank=0):
                pe.wait_ge(sem("xn"), k)
                pe.wait_ge(sem("ident"), 1)
                for j in range(J):
                    last = tr(bank(first_bank + j // 4, 0, C, [1, P], off=(j % 4) * P), xn[:, j, 0, :], ident[:, :])
                last.then_inc(sem("xT_ps"), 1)

            def project(w, first_bank, width, done, slot=C):
                for j in range(J):
                    last = mm(bank(first_bank, 0, P, [1, width], off=j * slot), xT[:, j, :], w,
                              start=True, stop=True)
                last.then_inc(sem(done), 1)

            pe.wait_ge(sem("xn"), 1)
            pe.wait_ge(sem("ident"), 1)
            for j in range(J):
                last = tr(bank(j // 4, 0, P, [1, P], off=(j % 4) * P), xn[:, j, :, :], ident[:, :])
            last.then_inc(sem("xT_ps"), 1)
            pe.wait_ge(sem("xT"), 1)
            pe.wait_ge(sem("w_proj0"), 16)
            project(w_in[:, :], 2, C, "img0_ps")
            pe.wait_ge(sem("x1T"), 1)
            pe.wait_ge(sem("w_offm"), 48)
            for j in range(J):
                for hf in range(2):
                    p0 = C * hf
                    last = mm(bank(4 + j // 2, p0, p0 + C, [1, 3 * GP0], off=256 * (j % 2)),
                              V(x1T, p0, j, [[1, C], [J, C]]), w_om[p0:p0 + C, :], start=True, stop=True)
            last.then_inc(sem("om_ps"), 1)
            seen = {"pool": 0, "dve": 0}
            first = True
            for w in PE_ORDER:
                who = OWNER(w)
                i = seen[who]
                seen[who] += 1
                pe.wait_ge(sem("pool_pr0" if who == "pool" else "dve_pr0"), i + 1)
                src = (V(ring, 0, 2304 + 512 * (i % 2), [[1, P], [1, 512]]) if who == "pool" else
                       V(ring, 0, 512 * (i % 3), [[1, P], [1, 512]]))
                mm(bank(3, 0, P, [1, 512]), ident[:, :], src, start=first, stop=(w == PE_ORDER[-1])
                   ).then_inc(sem("acc0"), 1)
                first = False
            pe.wait_ge(sem("off_max"), 1)
            tr(bank(2, 0, 1, [1, P]), flagf[:, 0:1], ident[:, :]).then_inc(sem("off_maxT"), 1)
            pe.wait_ge(sem("o_tok"), 1)
            for j in range(J):
                last = tr(bank(j // 4, 0, C, [1, P], off=(j % 4) * P), o_tok[:, j, :], ident[:, :])
            last.then_inc(sem("xT_ps"), 1)
            pe.wait_ge(sem("xT"), 2)
            pe.wait_ge(sem("w_o0"), 16)
            project(w_out[:, :], 2, C, "x1_ps")

            def experts(tag, n, w1, w2, b2, k):
                for hf in range(2):
                    for f in range(n):
                        i = hf * n + f
                        if i >= 2:
                            pe.wait_ge(sem(f"h{tag}"), i - 1)
                        mm(bank(i % 2, 0, P, [1, 512]), w1[:, P * f:P * f + P],
                           xT[:, 4 * hf:4 * hf + 4, :], start=True, stop=True).then_inc(sem(f"h{tag}_ps"), 1)
                    if hf == 0:
                        pe.wait_ge(sem("cw"), k)
                        for j in range(J):
                            last = tr(bank(6 + j // 4, 0, E, [1, P], off=(j % 4) * P), cw[:, j, :], ident[:, :])
                        last.then_inc(sem("cwT_ps"), 1)
                        pe.wait_ge(sem("cwT"), k)
                        for j in range(J):
                            last = mm(bank(5, 0, P, [1, C], off=C * j), cwT[:, j, :], b2[:, :], start=True, stop=True)
                        last.then_inc(sem("yb_ps"), 1)
                    pe.wait_ge(sem(f"h{tag}"), (hf + 1) * n)
                    for jj in range(4):
                        i = 4 * hf + jj
                        if i >= 2:
                            pe.wait_ge(sem(f"y{tag}_used"), i - 1)
                        per = n // E
                        for e in range(E):
                            for f in range(per):
                                ft = e * per + f
                                last = mm(bank(2 + i % 2, 0, P, [1, C], off=e * C),
                                          bigv(ft * 512 + jj * P, [1, P]), w2(ft), start=(f == 0), stop=(f == per - 1),
                                          skip_group_check=True)
                        last.then_inc(sem(f"y{tag}_ps"), 1)

            xn_transposes(2)
            pe.wait_ge(sem("xT"), 3)
            pe.wait_ge(sem("w_ffn0"), 64)
            project(w_g0[:, :], 4, E, "gate_ps", slot=E)
            experts(0, E, w_10, lambda f: w_20[:, C * f:C * f + C], b_20, 1)

            xn_transposes(3)
            pe.wait_ge(sem("xT"), 4)
            pe.wait_ge(sem("w_i1"), 32)
            project(w_i1[:, 0, :], 2, C, "img1_ps")
            for n in range(2):
                last = mm(bank(4 + n, 0, P, [1, 512]), w_i1[:, :, :], xT[:, 4 * n:4 * n + 4, :], start=True, stop=True)
            last.then_inc(sem("imgT_ps"), 1)
            pe.wait_ge(sem("w_ob"), 2)
            pe.wait_ge(sem("cpad1"), 1)
            for n in range(2):
                k = 0
                for kt, rows, dy in ((0, P, 0), (1, C, 2)):
                    for kx in range(3):
                        last = mm(bank(n, 0, 72, [1, 512]), V(w_ob, 0, kt * 216 + kx * 72, [[1, rows], [1, 72]]),
                                  V(cpad1, 0, 2 * n * NP0 + dy * (W + 2) + kx,
                                    [[1, rows], [NP0, 2], [W + 2, H], [1, W]]),
                                  start=(k == 0), stop=(k == 5))
                        k += 1
            last.then_inc(sem("offT_ps"), 1)
            pe.wait_ge(sem("offT"), 1)
            for j in range(J):
                last = tr(bank(2 + j // 4, 0, P, [1, 72], off=(j % 4) * P), V(fslab, 0, j, [[1, 72], [J, P]]),
                          ident[0:72, 0:72])
            last.then_inc(sem("off1_ps"), 1)
            pe.wait_ge(sem("off_max"), 2)
            tr(bank(6, 0, 1, [1, P]), flagf[:, 1:2], ident[:, :]).then_inc(sem("off_maxT"), 1)
            pe.wait_ge(sem("w_pb"), 5)
            for kt in range(5):
                rows = P if kt < 4 else C
                last = mm(bank(7, 0, C, [1, 1]), w_pb[0:rows, kt, :], w_dp[0:rows, kt, K + C1:K + C1 + 1],
                          start=(kt == 0), stop=(kt == 4))
            last.then_inc(sem("b_cv_ps"), 1)
            pe.wait_ge(sem("w_cv"), 5)
            for kt in range(5):
                rows = TAPS(kt) * C
                pe.wait_ge(sem("sampled"), kt + 1)
                if kt >= 2:
                    pe.wait_ge(sem("st"), 4 * (kt - 1))
                for j in range(J):
                    last = tr(bank(2 * (kt % 2) + j // 4, 0, rows, [1, P], off=(j % 4) * P),
                              bigv(SM + j * K * C + kt * P, [1, rows]), ident[:, :])
                last.then_inc(sem("st_ps"), 1)
                pe.wait_ge(sem("st"), 4 * (kt + 1))
                for n in range(2):
                    for kx in range(3):
                        for ky, m in ((1, 2 * C), (0, C)):
                            last = mm(bank(4 + n, 0, m, [1, 512]),
                                      V(w_cv, 0, ((kt * 3 + kx) * 3 + ky) * C, [[1, rows], [1, m]]),
                                      V(big, 0, ST + kt * STN + 2 * n * NP0 + ky * (W + 2) + kx,
                                        [[1, rows], [NP0, 2], [W + 2, H], [1, W]]),
                                      start=(kt == 0 and kx == 0 and ky == 1),
                                      stop=(kt == 4 and kx == 2), skip_group_check=True)
            last.then_inc(sem("conv_ps"), 1)
            pe.wait_ge(sem("convT"), 1)
            pe.wait_ge(sem("convT_up"), B + 1)
            pe.wait_ge(sem("two"), 1)
            for j in range(J):
                last = mm(bank(2, 0, P, [1, C], off=j * C), V(convT_of, 0, j, [[1, P], [J, P]]), two[:, :],
                          start=True, stop=True)
            last.then_inc(sem("x3_ps"), 1)

            xn_transposes(4)
            pe.wait_ge(sem("xT"), 5)
            pe.wait_ge(sem("w_ffn1"), 64)
            project(w_g1[:, :], 4, E, "gate_ps", slot=E)
            pe.wait_ge(sem("tri"), 1)
            pe.wait_ge(sem("tot"), 1)
            mm(bank(5, 0, P, [1, E]), tri[:, :], cum[:, J - 1, :], start=True, stop=True).then_inc(sem("before"), 1)
            pe.wait_ge(sem("cw"), 2)
            for j in range(J):
                last = tr(bank(6 + j // 4, 0, E, [1, P], off=(j % 4) * P), cw[:, j, :], ident[:, :])
            last.then_inc(sem("cwT_ps"), 1)
            pe.wait_ge(sem("cwT"), 2)
            for j in range(J):
                last = mm(bank(7, 0, P, [1, C], off=C * j), cwT[:, j, :], b_21[:, :], start=True, stop=True)
            last.then_inc(sem("yb_ps"), 1)
            pe.wait_ge(sem("slots_loaded"), 16)
            for i in range(ST_N):
                last = tr(bank(i // 4, 0, C, [1, P], off=(i % 4) * P), bigv(XS + i * C, [1, C]), ident[:, :])
            last.then_inc(sem("xs_ps"), 1)
            pe.wait_ge(sem("xsT"), 2)
            pe.wait_ge(sem("xsT2"), 1)
            for f in range(2 * E):
                n = f // 3
                last = mm(bank(n, 0, P, [1, CAP], off=(f % 3) * CAP), w_11[:, P * f:P * f + P],
                          bigv(XST + (f // 2) * QE, [P, ST_N], [1, QE], p=C + 1), start=True, stop=True)
                if f % 3 == 2 or f == 2 * E - 1:
                    last.then_inc(sem("h1_ps"), 1)
            for e in range(E):
                n = (2 * e + 1) // 3
                pe.wait_ge(sem("h1_act"), n // 2 + 1)
                if n:
                    pe.wait_ge(sem("h1_dve"), (n + 1) // 2)
                for f in range(2):
                    last = mm(bank((6, 0, 1)[e // 3], 0, C, [1, CAP], off=(e % 3) * CAP), w_21[:, 2 * e + f, :],
                              bigv(HS + (2 * e + f) * CAP, [1, CAP]), start=(f == 0), stop=(f == 1),
                              skip_group_check=True)
                if e in (2, 5, 7):
                    last.then_inc(sem("yT_ps"), 1)
            pe.wait_ge(sem("yT"), 3)
            for i in range(ST_N):
                last = tr(bank(3 + i // 8, 0, P, [1, C], off=(i % 8) * C), bigv(YT + i * P, [1, P], p=C),
                          ident[0:C, 0:C])
            last.then_inc(sem("ys_ps"), 1)

        @block.vector
        def _(dve):
            v = nc.vector
            n = [0]

            def step(ins):
                n[0] += 1
                ins.then_inc(sem("dve_step"), 1)
                dve.wait_ge(sem("dve_step"), n[0])

            def layernorm(k, src, eps, dup):
                for j in range(J):
                    last = v.bn_stats(stats[:, j, :], src[:, j, :])
                step(last)
                for j in range(J):
                    last = v.bn_aggr(aggr[:, j, :], stats[:, j, :])
                step(last)
                v.tensor_scalar(veps[:, :], aggr[:, :, 1], eps, None, ALU.add).then_inc(sem("var"), 1)
                dve.wait_ge(sem("rstd"), k)
                for j in range(J):
                    last = v.tensor_scalar(xn[:, j, 0:dup, :], V(src, 0, j * C, [[1, P], [0, dup], [1, C]]),
                                           aggr[:, j, 0:1], rstd[:, j:j + 1], ALU.subtract, ALU.mult)
                last.then_inc(sem("xn"), 1)

            def off_flag(tag, src, width, limit, op):
                step(v.tensor_reduce(flagf[:, tag:tag + 1], src, AX.X, ALU.max, apply_absolute_value=True))
                v.tensor_copy(flagf[:, 2:3], flagf[:, tag:tag + 1]).then_inc(sem("off_max"), 1)
                return limit, op

            def flag_finish(tag, src_bank, limit, op):
                dve.wait_ge(sem("off_maxT"), tag + 1)
                step(v.tensor_reduce(flagf[0:1, 2:3], bank(src_bank, 0, 1, [1, P]), AX.X, ALU.max))
                v.tensor_scalar(flagi[0:1, tag:tag + 1], flagf[0:1, 2:3], limit, None, op).then_inc(sem(f"flag{tag}"), 1)
                dve.wait_ge(sem(f"flag{tag}"), 1)

            v.memset(xT[C:C + 1, :, :], 1.0).then_inc(sem("ones_row"), 1)
            dve.wait_ge(sem("x_in"), 16)
            layernorm(1, x0, 1e-6, 2)
            dve.wait_ge(sem("w_conv0"), 32)
            v.tensor_scalar(bn[:, 0:1], w_dc[:, K + 3:K + 4], 1e-5, None, ALU.add).then_inc(sem("bnv"), 1)
            dve.wait_ge(sem("xT_ps"), 1)
            dve.wait_ge(sem("cpad_zero"), 1)
            dve.wait_ge(sem("xT"), 1)
            for hf in range(2):
                for b in range(2):
                    last = v.tensor_copy(V(cpad, C * hf, b * NP0 + W + 2 + 1, [[1, C], [1, J], [W + 2, H], [HC, 2]]),
                                         bank(0, C * hf, C * hf + C, [P, J], [2, H], [1, 2],
                                              off=32 * (2 * hf + b)))
            step(last)
            n_dw = 15 * (W + 2) + W
            for tap in range(K):
                ky, kx = divmod(tap, 3)
                src = V(cpad, 0, ky * (W + 2) + kx, [[1, P], [NP0, 2], [1, n_dw]])
                dst = V(dwc, 0, 0, [[1, P], [H * (W + 2), 2], [1, n_dw]])
                if tap == 0:
                    step(v.tensor_scalar(dst, src, w_dc[:, 0:1], None, ALU.mult))
                elif tap < K - 1:
                    step(v.scalar_tensor_tensor(dst, src, w_dc[:, tap:tap + 1], dst, ALU.mult, ALU.add))
                else:
                    v.scalar_tensor_tensor(dst, src, w_dc[:, tap:tap + 1], dst, ALU.mult, ALU.add).then_inc(sem("dwc"), 1)
            dve.wait_ge(sem("bnr"), 1)
            step(v.tensor_tensor(bn[:, 2:3], w_dc[:, K:K + 1], bn[:, 1:2], ALU.mult))
            step(v.tensor_tensor(bn[:, 4:5], w_dc[:, K + 2:K + 3], bn[:, 2:3], ALU.mult))
            v.tensor_tensor(bn[:, 3:4], w_dc[:, K + 1:K + 2], bn[:, 4:5], ALU.subtract).then_inc(sem("bn"), 1)
            dve.wait_ge(sem("om_ps"), 1)
            dve.wait_ge(sem("w_offm"), 48)
            for i, (dst, signal) in enumerate(((ox, "offx"), (ml, "ml"), (oy, "offy"))):
                c0 = {0: 0, 1: 2, 2: 1}[i] * GP0
                v.tensor_tensor(V(dst, 0, 0, [[1, P], [GP0, J], [1, GP0]]),
                                bank(4, 0, P, [256, J], [1, GP0], off=c0),
                                V(b_om, 0, c0, [[1, P], [0, J], [1, GP0]]), ALU.add).then_inc(sem(signal), 1)
            dve.wait_ge(sem("ml"), 1)
            step(v.tensor_reduce(m64[:, :], V(ml, 0, 0, [[1, P], [K, J * G0], [1, K]]), AX.X, ALU.max))
            v.tensor_tensor(V(ml, 0, 0, [[1, P], [K, J * G0], [1, K]]), V(ml, 0, 0, [[1, P], [K, J * G0], [1, K]]),
                            V(m64, 0, 0, [[1, P], [1, J * G0], [0, K]]), ALU.subtract).then_inc(sem("mask_in"), 1)
            dve.wait_ge(sem("offy"), 1)
            step(v.tensor_tensor(fy[:, 0:GP0 * J], ox[:, :], ox[:, :], ALU.mult))
            step(v.tensor_tensor(fx[:, 0:GP0 * J], oy[:, :], oy[:, :], ALU.mult))
            step(v.tensor_tensor(fy[:, 0:GP0 * J], fy[:, 0:GP0 * J], fx[:, 0:GP0 * J], ALU.max))
            v.tensor_reduce(flagf[:, 0:1], fy[:, 0:GP0 * J], AX.X, ALU.max).then_inc(sem("off_max"), 1)
            dve.wait_ge(sem("mask_e"), 1)
            step(v.tensor_reduce(m64[:, :], V(ml, 0, 0, [[1, P], [K, J * G0], [1, K]]), AX.X, ALU.add))
            step(v.reciprocal(r64[:, :], m64[:, :]))
            for k in range(D0):
                d = float(k - WIN0)
                step(v.tensor_scalar(aby[:, :], oy[:, :], -1.0, 1.0 + d, ALU.mult, ALU.add))
                step(v.scalar_tensor_tensor(aby[:, :], oy[:, :], 1.0 - d, aby[:, :], ALU.add, ALU.min))
                v.scalar_tensor_tensor(bigv(TY + k * J * GP0, [1, J * GP0]), aby[:, :], 0.0, ml[:, :],
                                       ALU.max, ALU.mult).then_inc(sem("tenty"), 1)
                dve.wait_ge(sem("tenty"), k + 1)
            dve.wait_ge(sem("A_zero"), 1)
            dve.wait_ge(sem("tenty"), D0)
            for c in range(D0 * D0):
                dy, dx = divmod(c, D0)
                if c % 2:
                    dve.wait_ge(sem("poolw"), c // 2 + 1)
                    src = V(ring, 0, 576 * ((c // 2) % 2), [[1, P], [K, J * G0], [3, 3], [1, 3]])
                else:
                    dve.wait_ge(sem("tentx"), dx + 1)
                    step(v.tensor_tensor(ring[:, 1152:1728], bigv(TY + dy * J * GP0, [1, J * GP0]),
                                         bigv(TX + dx * J * GP0, [1, J * GP0]), ALU.mult))
                    src = V(ring, 0, 1152, [[1, P], [K, J * G0], [3, 3], [1, 3]])
                dst = bigv(AW + dx * N0 + dy, [N0 * N0, J * G0], [N0, 3], [1, 3])
                add = v.tensor_tensor(dst, dst, src, ALU.add)
                if c % 2:
                    add.then_inc(sem("poolw_used"), 1)
                    dve.wait_ge(sem("poolw_used"), c // 2 + 1)
                elif c < D0 * D0 - 1:
                    step(add)
                else:
                    add.then_inc(sem("A_done"), 1)
            dve.wait_ge(sem("A_done"), 1)
            dve.wait_ge(sem("slab0"), 128)
            order = [w for w in range(N0 * N0) if OWNER(w) == "dve"]
            own = [w for w in range(N0 * N0) if OWNER(w) == "sum"]
            acc = V(ring, 0, 3328, [[1, P], [1, 512]])

            def product(w, dst_off):
                wy, wx = divmod(w, N0)
                return v.tensor_tensor(V(ring, 0, dst_off, [[1, P], [C0, J * G0], [1, C0]]),
                                       bigv(wy * SLAB0 + wx * C, [C0, J * G0], [1, C0]),
                                       bigv(AW + wx * N0 + wy, [N0 * N0, J * G0], [0, C0]), ALU.mult)
            todo = list(order)
            k = 0
            for i, w in enumerate(own):
                if i == 0:
                    step(product(w, 3328))
                else:
                    step(product(w, 3840))
                    step(v.tensor_tensor(acc, acc, V(ring, 0, 3840, [[1, P], [1, 512]]), ALU.add))
                while todo and k * len(own) <= i * len(order):
                    if k >= 3:
                        dve.wait_ge(sem("acc0"), PE_COUNT(order[k - 3]))
                    product(todo.pop(0), 512 * (k % 3)).then_inc(sem("dve_pr0"), 1)
                    k += 1
            while todo:
                dve.wait_ge(sem("acc0"), PE_COUNT(order[k - 3]))
                product(todo.pop(0), 512 * (k % 3)).then_inc(sem("dve_pr0"), 1)
                k += 1
            flag_finish(0, 2, float(WIN0 * WIN0), ALU.is_ge)
            dve.wait_ge(sem("acc0"), len(PE_ORDER))
            step(v.tensor_tensor(acc, acc, bank(3, 0, P, [1, 512]), ALU.add))

            def tent_loop(tag, width, xs, ys, prepare, consume):
                prepare()
                m = [0]

                def fstep(ins):
                    m[0] += 1
                    ins.then_inc(sem("general_step"), 1)
                    dve.wait_ge(sem("general_step"), m[0])

                def tent(dst, src, count):
                    fstep(v.tensor_scalar(dst, src, count, None, ALU.subtract))
                    fstep(v.scalar_tensor_tensor(dst, dst, -1.0, dst, ALU.mult, ALU.min))
                    fstep(v.tensor_scalar(dst, dst, 1.0, 0.0, ALU.add, ALU.max))

                v.memset(fcnt[:, 0:1], float(-RB)).then_inc(sem(f"general_start{tag}"), 1)
                dve.wait_ge(sem(f"general_start{tag}"), 1)
                dve.sem_inc(sem(f"fslab_used{tag}"), 1)
                with dve.Fori(1, NB + 1) as i:
                    dve.sem_clear(sem("general_step"))
                    m[0] = 0
                    dve.wait_ge(sem(f"fslab_in{tag}"), i * 128)
                    tent(fy[:, 0:width], ys, fcnt[:, 0:1])
                    fstep(v.memset(fcnt[:, 1:2], float(-RB)))
                    with dve.Fori(0, NB) as k:
                        dve.sem_clear(sem("general_step"))
                        m[0] = 0
                        tent(fx[:, 0:width], xs, fcnt[:, 1:2])
                        fstep(v.tensor_tensor(fx[:, 0:width], fx[:, 0:width], fy[:, 0:width], ALU.mult))
                        consume(fstep, fslab[:, bass.ds(k * C, HC * C)])
                        fstep(v.tensor_scalar(fcnt[:, 1:2], fcnt[:, 1:2], 1.0, None, ALU.add))
                    dve.sem_clear(sem("general_step"))
                    m[0] = 0
                    fstep(v.tensor_scalar(fcnt[:, 0:1], fcnt[:, 0:1], 1.0, None, ALU.add))
                    dve.sem_inc(sem(f"fslab_used{tag}"), 1)

            flag = dve.value_load(flagi[0:1, 0:1], min_val=0, max_val=1)
            with dve.If(flag > 0):
                def prepare0():
                    for ap_, px in ((ox, True), (oy, False)):
                        for t in range(3):
                            o = (3 * t if px else t)
                            vw = V(ap_, 0, o, [[1, P], [K, J * G0], [1 if px else 3, 3]])
                            v.tensor_scalar(vw, vw, float(t - 1), None, ALU.add).then_inc(sem("general_prep0"), 1)
                    v.memset(acc, 0.0).then_inc(sem("general_prep0"), 1)
                    dve.wait_ge(sem("general_prep0"), 7)

                def consume0(istep, slab):
                    istep(v.tensor_tensor(fx[:, :], fx[:, :], ml[:, :], ALU.mult))
                    istep(v.tensor_reduce(m64[:, :], V(fx, 0, 0, [[1, P], [K, J * G0], [1, K]]), AX.X, ALU.add))
                    istep(v.tensor_tensor(V(ring, 0, 3840, [[1, P], [C0, J * G0], [1, C0]]),
                                          slab.rearrange("p (g c) -> p g c", c=C0),
                                          V(m64, 0, 0, [[1, P], [1, J * G0], [0, C0]]), ALU.mult))
                    istep(v.tensor_tensor(acc, acc, V(ring, 0, 3840, [[1, P], [1, 512]]), ALU.add))
                tent_loop(0, J * GP0, ox[:, :], oy[:, :], prepare0, consume0)
            with dve.Else():
                dve.nop()
            v.tensor_tensor(o_tok[:, :, :].rearrange("p j (g c) -> p (j g) c", c=C0),
                            V(ring, 0, 3328, [[1, P], [C0, J * G0], [1, C0]]),
                            V(r64, 0, 0, [[1, P], [1, J * G0], [0, C0]]), ALU.mult).then_inc(sem("o_tok"), 1)
            dve.wait_ge(sem("x1_ps"), 1)
            step(v.tensor_tensor(x1[:, :, :], x0[:, :, :], bank(2, 0, P, [1, 512]), ALU.add))

            JE3 = [[8, J], [1, 8]]

            def je(t):
                return t[:, :, :]

            def bc(t):
                return V(t, 0, 0, [[1, P], [1, J], [0, E]])

            def first_of_max(src, m, dst):
                step(v.tensor_reduce(m[:, :], je(src), AX.X, ALU.max))
                step(v.tensor_tensor(je(t1), je(src), bc(m), ALU.is_equal))
                step(v.tensor_tensor(je(t1), je(t1), je(jneg), ALU.mult))
                step(v.tensor_reduce(den[:, :], je(t1), AX.X, ALU.max))
                step(v.tensor_tensor(je(dst), je(t1), bc(den), ALU.is_equal))

            def weighted_sum(tag):
                for i in range(J):
                    dve.wait_ge(sem(f"y{tag}_ps"), i + 1)
                    v.tensor_tensor(V(ring, 0, (i % 2) * E * C, [[1, P], [C, E], [1, C]]), bank(2 + i % 2, 0, P, [C, E], [1, C]),
                                    V(cw, 0, i * E, [[1, P], [1, E], [0, C]]), ALU.mult
                                    ).then_inc(sem(f"y{tag}_used"), 1)
                    dve.wait_ge(sem(f"y{tag}_used"), i + 1)
                    step(v.tensor_reduce(ysum[:, i, :], V(ring, 0, (i % 2) * E * C, [[1, P], [1, C], [C, E]]),
                                         AX.X, ALU.add))

            for e in range(E):
                last = v.memset(jneg[:, :, e:e + 1], float(E - e))
            step(last)
            layernorm(2, x1, 1e-5, 1)
            dve.wait_ge(sem("gate_ps"), 1)
            step(v.tensor_copy(je(lg), bank(4, 0, P, [E, J], [1, E])))
            first_of_max(lg, m1, oh1)
            v.tensor_tensor(je(lgw), je(lg), bc(m1), ALU.subtract).then_inc(sem("gate_in"), 1)
            step(v.tensor_scalar(je(t2), je(oh1), -BIGV, None, ALU.mult))
            step(v.tensor_tensor(je(t2), je(lg), je(t2), ALU.add))
            first_of_max(t2, m2, oh2)
            step(v.tensor_tensor(je(oh1), je(oh1), je(oh2), ALU.add))
            dve.wait_ge(sem("gate_ex"), 1)
            step(v.tensor_reduce(den[:, :], je(ex), AX.X, ALU.add))
            step(v.reciprocal(m2[:, :], den[:, :]))
            step(v.tensor_tensor(je(t1), je(oh1), je(ex), ALU.mult))
            v.tensor_tensor(je(cw), je(t1), bc(m2), ALU.mult).then_inc(sem("cw"), 1)
            dve.wait_ge(sem("cw"), 1)
            dve.wait_ge(sem("pidx"), 3)
            step(v.tensor_scalar(pidx[:, 1:2], pidx[:, 0:1], 1, 1, ALU.bitwise_and, ALU.bitwise_and))
            step(v.tensor_scalar(pidx[:, 2:3], pidx[:, 0:1], 1, 15, ALU.logical_shift_right, ALU.bitwise_and))
            step(v.tensor_scalar(pidx[:, 3:4], pidx[:, 0:1], 4, 3, ALU.logical_shift_right, ALU.bitwise_and))
            step(v.tensor_copy(pf[:, :], pidx[:, :]))
            step(v.tensor_scalar(pf[:, 1:2], pf[:, 1:2], float(HC), None, ALU.mult))
            v.tensor_scalar(gsel[:, :], e4[:, :], pf[:, 3:4], None, ALU.is_equal).then_inc(sem("gsel"), 1)
            for c0, col in ((0, 1), (GP1, 2)):
                vw = V(base1, 0, c0, [[1, P], [2 * GP1, J], [1, GP1]])
                step(v.tensor_scalar(vw, vw, pf[:, col:col + 1], None, ALU.add))
            weighted_sum(0)
            dve.wait_ge(sem("yb_ps"), 1)
            step(v.tensor_tensor(ysum[:, :, :], ysum[:, :, :], bank(5, 0, P, [C, J], [1, C]), ALU.add))
            step(v.tensor_tensor(x2[:, :, :], x1[:, :, :], ysum[:, :, :], ALU.add))

            layernorm(3, x2, 1e-6, 1)
            dve.wait_ge(sem("imgT_ps"), 1)
            dve.wait_ge(sem("cpad1_zero"), 1)
            for hf in range(2):
                for b in range(B):
                    last = v.tensor_copy(
                        V(cpad1, C * hf, b * NP0 + (W + 2) * (1 - hf) + 1, [[1, C], [1, J], [W + 2, H], [HC, 2]]),
                        bank(4, C * hf, C * hf + C, [P, J], [2, H], [1, 2], off=32 * b))
            last.then_inc(sem("cpad1"), 1)
            dve.wait_ge(sem("off1_ps"), 1)
            FU = [[1, P], [1, J * 2 * GP1]]
            step(v.tensor_tensor(V(loc1, 0, 0, [[1, P], [2 * GP1, J], [1, 2 * GP1]]),
                                 bank(2, 0, P, [P, J], [1, 2 * GP1]),
                                 V(base1, 0, 0, [[1, P], [2 * GP1, J], [1, 2 * GP1]]), ALU.add))
            step(v.tensor_scalar(val1[:, :], loc1[:, :], W - 1.0, None, ALU.is_lt))
            step(v.tensor_scalar(loc1[:, :], loc1[:, :], 0.0, W - 1.0, ALU.max, ALU.min))
            v.tensor_tensor(u1[:, :], loc1[:, :], base1[:, :], ALU.subtract).then_inc(sem("off1"), 1)
            dve.wait_ge(sem("off1"), 1)
            step(v.tensor_reduce(flagf[:, 1:2], u1[:, :], AX.X, ALU.max, apply_absolute_value=True))
            v.tensor_copy(flagf[:, 3:4], flagf[:, 1:2]).then_inc(sem("off_max"), 1)
            NT = J * 2 * GP1
            step(v.tensor_scalar(loc1[:, :], u1[:, :], -1.0, 0.0, ALU.mult, ALU.max))
            v.scalar_tensor_tensor(bigv(T1 + 2 * NT, [1, NT]), u1[:, :], 0.0, val1[:, :], ALU.max, ALU.mult)
            step(v.tensor_tensor(bigv(T1, [1, NT]), loc1[:, :], val1[:, :], ALU.mult))
            step(v.tensor_scalar(loc1[:, :], u1[:, :], -1.0, 1.0, ALU.mult, ALU.add))
            step(v.scalar_tensor_tensor(loc1[:, :], u1[:, :], 1.0, loc1[:, :], ALU.add, ALU.min))
            step(v.tensor_tensor(bigv(T1 + NT, [1, NT]), loc1[:, :], val1[:, :], ALU.mult))
            for d in range(9):
                dy, dx = divmod(d, 3)
                v.tensor_tensor(bigv(AD + d * J * GP1, [GP1, J], [1, GP1]),
                                bigv(T1 + dy * NT + GP1, [2 * GP1, J], [1, GP1]),
                                bigv(T1 + dx * NT, [2 * GP1, J], [1, GP1]), ALU.mult).then_inc(sem("pairs"), 1)
            dve.wait_ge(sem("pairs"), 9)
            flag_finish(1, 6, 1.0, ALU.is_gt)
            flag = dve.value_load(flagi[0:1, 1:2], min_val=0, max_val=1)
            with dve.If(flag > 0):
                U = V(u1, 0, 0, [[1, P], [2 * GP1, J], [1, GP1]])

                dve.sem_inc(sem("pool_pr1_used"), 5 * len(POOL_D))

                def prepare1():
                    for c0 in (0, GP1):
                        for t in range(3):
                            for g in range(G1):
                                o = c0 + g * K + (t if c0 == 0 else 3 * t)
                                vw = V(u1, 0, o, [[1, P], [2 * GP1, J], [3 if c0 == 0 else 1, 3]])
                                v.tensor_scalar(vw, vw, float(t - 1), None, ALU.add).then_inc(sem("general_prep1"), 1)
                    dve.wait_ge(sem("general_prep1"), 24)
                    for c0, dst in ((0, ox), (GP1, oy)):
                        v.tensor_copy(V(dst, 0, 0, [[1, P], [GP1, J], [1, GP1]]),
                                      V(u1, 0, c0, [[1, P], [2 * GP1, J], [1, GP1]])).then_inc(sem("general_prep1"), 1)
                    v.tensor_tensor(V(ml, 0, 0, [[1, P], [GP1, J], [1, GP1]]),
                                    V(val1, 0, 0, [[1, P], [2 * GP1, J], [1, GP1]]),
                                    V(val1, 0, GP1, [[1, P], [2 * GP1, J], [1, GP1]]), ALU.mult
                                    ).then_inc(sem("general_prep1"), 1)
                    v.memset(bigv(SM, [1, J * K * C]), 0.0).then_inc(sem("general_prep1"), 1)
                    dve.wait_ge(sem("general_prep1"), 28)

                def consume1(istep, slab):
                    istep(v.tensor_tensor(fx[:, 0:J * GP1], fx[:, 0:J * GP1], ml[:, 0:J * GP1], ALU.mult))
                    for p in range(K):
                        istep(v.tensor_tensor(V(ring, 0, 3072, [[1, P], [C1, J * G1], [1, C1]]),
                                              slab.rearrange("p (g c) -> p g c", c=C1),
                                              V(fx, 0, p, [[1, P], [K, J * G1], [0, C1]]), ALU.mult))
                        smp = bigv(SM + p * C, [K * C, J], [1, C])
                        istep(v.tensor_tensor(smp, smp, V(ring, 0, 3072, [[1, P], [C, J], [1, C]]), ALU.add))
                tent_loop(1, J * GP1, ox[:, 0:J * GP1], oy[:, 0:J * GP1], prepare1, consume1)
                dve.wait_ge(sem("pool_pr1"), 5 * len(POOL_D))
                dve.sem_inc(sem("sampled"), 5)
            with dve.Else():
                dve.wait_ge(sem("slab1"), 128)
                m = [0]

                def sstep(ins):
                    m[0] += 1
                    ins.then_inc(sem("sample_step"), 1)
                    dve.wait_ge(sem("sample_step"), m[0])

                def rv(slot, kt):
                    return V(ring, 0, slot * 1024, [[1, P], [512, TAPS(kt)], [C, J], [1, C]])

                for kt in range(5):
                    smp = bigv(SM + kt * P, [C, TAPS(kt)], [K * C, J], [1, C])
                    sample_product(v, 3, kt, DVE_D[0]).then_inc(sem("sample_first"), 1)
                    sstep(sample_product(v, 4, kt, DVE_D[1]))
                    dve.wait_ge(sem("sample_first"), kt + 1)
                    sstep(v.tensor_tensor(smp, rv(3, kt), rv(4, kt), ALU.add))
                    for i, (who, d) in enumerate(REST):
                        if who == "dve":
                            sstep(sample_product(v, 3, kt, d))
                            add = v.tensor_tensor(smp, smp, rv(3, kt), ALU.add)
                        else:
                            k = kt * len(POOL_D) + POOL_D.index(d)
                            dve.wait_ge(sem("pool_pr1"), k + 1)
                            add = v.tensor_tensor(smp, smp, rv(k % 3, kt), ALU.add)
                        if who == "pool":
                            add.then_inc(sem("pool_pr1_used"), 1)
                            dve.wait_ge(sem("pool_pr1_used"), k + 1)
                        else:
                            sstep(add)
                    dve.sem_inc(sem("sampled"), 1)
            dve.wait_ge(sem("b_cv_ps"), 1)
            v.tensor_tensor(b_cv[:, :], b_pw[:, :], bank(7, 0, C, [1, 1]), ALU.add).then_inc(sem("b_cv"), 1)
            dve.wait_ge(sem("conv_ps"), 1)
            for b in range(B):
                v.tensor_copy(V(convT_of, C, b * H * W, [[1, C], [1, (H - 1) * W]]),
                                     bank(4, C, P, [1, (H - 1) * W], off=b * H * W + W)).then_inc(sem("convT_up"), 1)
            v.memset(V(convT_of, C, (H - 1) * W, [[1, C], [H * W, B], [1, W]]), 0.0).then_inc(sem("convT_up"), 1)
            dve.wait_ge(sem("x3_ps"), 1)
            step(v.tensor_tensor(x3[:, :, :], x2[:, :, :], bank(2, 0, P, [1, 512]), ALU.add))

            layernorm(4, x3, 1e-5, 1)
            dve.wait_ge(sem("gate_ps"), 2)
            step(v.tensor_copy(je(lg), bank(4, 0, P, [E, J], [1, E])))
            first_of_max(lg, m1, oh1)
            v.tensor_tensor(je(lgw), je(lg), bc(m1), ALU.subtract).then_inc(sem("gate_in"), 1)
            step(v.tensor_copy(cum[:, 0, :], oh1[:, 0, :]))
            for j in range(1, J - 1):
                step(v.tensor_tensor(cum[:, j, :], cum[:, j - 1, :], oh1[:, j, :], ALU.add))
            v.tensor_tensor(cum[:, J - 1, :], cum[:, J - 2, :], oh1[:, J - 1, :], ALU.add).then_inc(sem("tot"), 1)
            dve.wait_ge(sem("before"), 1)
            step(v.tensor_tensor(je(t2), je(cum), bank(5, 0, P, [0, J], [1, E]), ALU.add))
            step(v.tensor_tensor(je(t2), je(t2), je(oh1), ALU.mult))
            step(v.tensor_reduce(posf[:, :], je(t2), AX.X, ALU.add))
            step(v.tensor_scalar(slot[:, :], den[:, :], -float(CAP), float(E * CAP - 1), ALU.mult, ALU.add))
            step(v.scalar_tensor_tensor(slot[:, :], posf[:, :], float(CAP), slot[:, :], ALU.min, ALU.add))
            step(v.tensor_scalar(lost[:, :], posf[:, :], float(CAP), None, ALU.is_gt))
            v.tensor_copy(idx_out[:, :], slot[:, :]).then_inc(sem("idx"), 1)
            step(v.tensor_tensor(posf[:, :], trash[:, :], slot[:, :], ALU.subtract))
            step(v.tensor_tensor(posf[:, :], posf[:, :], lost[:, :], ALU.mult))
            step(v.tensor_tensor(posf[:, :], posf[:, :], slot[:, :], ALU.add))
            v.tensor_copy(idx_in[:, :], posf[:, :]).then_inc(sem("idx"), 1)
            step(v.tensor_scalar(lost[:, :], lost[:, :], -1.0, 1.0, ALU.mult, ALU.add))
            dve.wait_ge(sem("gate_ex"), 2)
            step(v.tensor_reduce(den[:, :], je(ex), AX.X, ALU.add))
            step(v.reciprocal(m2[:, :], den[:, :]))
            step(v.tensor_tensor(wtok[:, :], lost[:, :], m2[:, :], ALU.mult))
            v.tensor_tensor(je(cw), je(oh1), bc(wtok), ALU.mult).then_inc(sem("cw"), 1)
            v.memset(V(big, C, XST, [[1, 1], [1, SLOTS]]), 1.0).then_inc(sem("xsT"), 1)
            dve.wait_ge(sem("xs_ps"), 1)
            v.tensor_copy(bigv(XST + 1024, [1, SLOTS - 1024], p=C), bank(2, 0, C, [1, SLOTS - 1024])
                          ).then_inc(sem("xsT2"), 1)
            for nb in range(HB):
                if nb % 2:
                    dve.wait_ge(sem("h1_ps"), nb + 1)
                    w = min(3, 2 * E - 3 * nb) * CAP
                    v.tensor_scalar(bigv(HS + nb * 3 * CAP, [1, w]), bank(nb, 0, P, [1, w]), 0.0, None, ALU.max
                                    ).then_inc(sem("h1_dve"), 1)
            for g, (b, e0, ne) in enumerate(((6, 0, 3), (0, 3, 3), (1, 6, 2))):
                dve.wait_ge(sem("yT_ps"), g + 1)
                for e in range(ne):
                    last = v.tensor_copy(bigv(YT + (e0 + e) * QE, [P, ST_N], [1, QE], p=C),
                                         bank(b, 0, C, [QE, ST_N], [1, QE], off=e * CAP))
                last.then_inc(sem("yT"), 1)
            dve.wait_ge(sem("ys_ps"), 1)
            v.tensor_copy(bigv(YS, [1, ST_N * C]), bank(3, 0, P, [1, ST_N * C])).then_inc(sem("ys"), 1)
            dve.wait_ge(sem("gathered"), 16 * J)
            step(v.tensor_tensor(ysum[:, :, :], bigv(YG, [C, J], [1, C]), V(wtok, 0, 0, [[1, P], [1, J], [0, C]]),
                                 ALU.mult))
            dve.wait_ge(sem("yb_ps"), 2)
            step(v.tensor_tensor(ysum[:, :, :], ysum[:, :, :], bank(7, 0, P, [C, J], [1, C]), ALU.add))
            dve.wait_ge(sem("limits"), 1)
            ys = V(ysum, 0, 0, [[1, P], [1, J * C]])
            for op, limit, col in ((ALU.is_gt, BIGV, 0), (ALU.is_lt, -BIGV, 1), (None, None, 2)):
                if op is None:
                    step(v.tensor_tensor(nmask[:, :], ys, ys, ALU.not_equal))
                else:
                    step(v.tensor_scalar(nmask[:, :], ys, limit, None, op))
                step(v.copy_predicated(ys, nmask[:, :], V(big1e4, 0, col, [[1, P], [0, J * C]])))
            v.tensor_tensor(x0[:, :, :], x3[:, :, :], ysum[:, :, :], ALU.add).then_inc(sem("x4"), 1)


def V2(t, dims, off=0):
    if isinstance(t, bass.AP):
        return bass.AP(tensor=t.tensor, offset=t.offset + off, ap=[list(d) for d in dims])
    return bass.AP(tensor=t, offset=off, ap=[list(d) for d in dims])


def OWNER(w):
    return ("pool", "sum", "dve", "pool", "sum", "pool", "sum")[w % 7]


PE_ORDER = [w for w in range(N0 * N0) if OWNER(w) != "sum"]


def PE_COUNT(w):
    return PE_ORDER.index(w) + 1


def TAPS(kt):
    return 2 if kt < 4 else 1


POOL_D = (1, 2, 4, 5, 7, 8)
DVE_D = (0, 3, 6)
REST = (("pool", 1), ("pool", 2), ("dve", 6), ("pool", 4), ("pool", 5), ("pool", 7), ("pool", 8))

_ORDER = [w for w in range(N0 * N0) if OWNER(w) != "sum"]


def PE_COUNT(w):
    return PE_ORDER.index(w) + 1


def POOL1(c):
    return c % 9 in (2, 5, 8)



_ORDER = ["x", "dc", "w_in", "om", "omb", "w_out", "w_g0", "w_10", "w_20", "b_20", "w_i1", "w_of_a", "w_of_b",
          "b_of", "w_dp_a", "w_dp_b", "b_pw", "w_g1", "w_11", "w_21", "b_21"]


def kernel(**inputs):
    import numpy as np
    import concourse.bacc as _bacc
    from concourse.bass_utils import run_bass_kernel_spmd as _run

    i = {k: np.asarray(v) for k, v in inputs.items()}

    def rows(*parts):
        return np.concatenate(parts, axis=0)

    om = i["L0_conv_off_w"].reshape(C, GP0, 2).transpose(0, 2, 1).reshape(C, 2 * GP0)
    omb = i["L0_conv_off_b"].reshape(GP0, 2).transpose(1, 0).reshape(2 * GP0)
    w_of = i["L1_conv_w_off"].reshape(G1, 3, 3, C1, K, 2).transpose(1, 0, 3, 2, 5, 4).reshape(3 * C, 54)
    b_of = i["L1_conv_b_off"].reshape(G1, K, 2).transpose(2, 0, 1).reshape(72, 1)
    w_dw = i["L1_conv_w_dw"].reshape(G1, K, K, C1).transpose(2, 0, 3, 1).reshape(K * C, K)
    w_pw = i["L1_conv_w_pw"].reshape(G1, K, C1, C1).transpose(1, 0, 2, 3).reshape(K * C, C1)
    b_dw = i["L1_conv_b_dw"].reshape(G1, K, C1).transpose(1, 0, 2).reshape(K * C, 1)
    w_dp = np.concatenate([w_dw, w_pw, b_dw], axis=1)
    data = {
        "x": i["x"],
        "dc": np.concatenate([i["L0_conv_dw_k"].reshape(C, K)] +
                             [i["L0_conv_bn_" + s].reshape(C, 1) for s in "gbmv"], axis=1),
        "w_in": rows(i["L0_conv_in_w"], i["L0_conv_in_b"][None]),
        "om": np.concatenate([om, i["L0_conv_mask_w"]], axis=1),
        "omb": np.concatenate([omb, i["L0_conv_mask_b"]]),
        "w_out": rows(i["L0_conv_out_w"], i["L0_conv_out_b"][None]),
        "w_g0": rows(i["L0_ffn_gate_w"], i["L0_ffn_gate_b"][None]),
        "w_10": rows(i["L0_ffn_W1"].transpose(1, 0, 2).reshape(C, E * F0), i["L0_ffn_b1"].reshape(1, E * F0)),
        "w_20": i["L0_ffn_W2"].transpose(1, 0, 2).reshape(F0, E * C),
        "b_20": i["L0_ffn_b2"],
        "w_i1": rows(i["L1_conv_w_init"].reshape(C, C), i["L1_conv_b_init"][None]),
        "w_of_a": w_of[:P], "w_of_b": w_of[P:],
        "b_of": b_of,
        "w_dp_a": w_dp[:4 * P], "w_dp_b": w_dp[4 * P:],
        "b_pw": i["L1_conv_b_pw"].reshape(C, 1),
        "w_g1": rows(i["L1_ffn_gate_w"], i["L1_ffn_gate_b"][None]),
        "w_11": rows(i["L1_ffn_w1"].transpose(1, 0, 2).reshape(C, E * F1), i["L1_ffn_b1"].reshape(1, E * F1)),
        "w_21": i["L1_ffn_w2"].reshape(E * F1, C),
        "b_21": i["L1_ffn_b2"],
    }
    nc = _bacc.Bacc("TRN2", target_bir_lowering=False, num_devices=1)
    arrays, aps = {}, {}
    for name in _ORDER:
        v = np.ascontiguousarray(data[name])
        arrays[f"in_{name}_dram"] = v
        aps[name] = nc.dram_tensor(f"in_{name}_dram", v.shape, F32, kind="ExternalInput").ap()
    out = nc.dram_tensor("out_0_dram", (B, H, W, C), F32, kind="ExternalOutput").ap()
    program(nc, aps, out)
    r = _run(nc, [arrays], core_ids=[0])
    return r.results[0]["out_0_dram"]
```

```python
from contextlib import ExitStack

import concourse.bass as bass
from concourse import mybir

F32 = mybir.dt.float32
I32 = mybir.dt.int32
BF16 = mybir.dt.bfloat16
U32 = mybir.dt.uint32
ALU = mybir.AluOpType
ACT = mybir.ActivationFunctionType
AX = mybir.AxisListType

B, H, W, C = 4, 16, 16, 64
P = 128
J = B * H * W // P
HC = J
HJ = J // 2
K = 9
G0, C0 = 8, 8
G1, C1 = 4, 16
GP0, GP1 = G0 * K, G1 * K
K1 = K + 1
E, F0, F1 = 8, 128, 256
T = B * H * W
CAP = -(-5 * B * H * W // (4 * E))
SLOTS = E * CAP
ST_N = SLOTS // P
QE = CAP // ST_N
WIN0 = 2
R0 = 1 + WIN0
R1 = 2
D0, D1 = 2 * WIN0 + 1, 3
N0, N1 = 2 * R0 + 1, 2 * R1 + 1
HB = -(-2 * E // 3)
RB = 15
NB = 2 * RB + 1
NPART = 3
BIGV = 3.4028234663852886e38


def V(t, p0, off, dims):
    if isinstance(t, tuple):
        t, off = t[0], t[1] + off
    pitch = 1
    for s in t.shape[1:]:
        pitch *= s
    return bass.AP(tensor=t, offset=p0 * pitch + off,
                   ap=[[dims[0][0] * pitch, dims[0][1]]] + [list(d) for d in dims[1:]])


def program(nc, a, out):
    ctx = ExitStack()
    with ctx:
        def sb(name, *shape, dt=F32):
            return ctx.enter_context(nc.sbuf_tensor(name, list(shape), dt))

        sems = {}

        def sem(name):
            if name not in sems:
                sems[name] = ctx.enter_context(nc.semaphore(name))
            return sems[name]

        def scratch(name, reach):
            return nc.dram_tensor(name, [B, H + 2 * reach, W + 2 * reach, C], F32)
        pad0, pad1 = scratch("pad0", R0), scratch("pad1", R1)
        wide = scratch("wide", RB)
        slots_in = nc.dram_tensor("slots_in", [SLOTS + T, C], F32)
        slots_out = nc.dram_tensor("slots_out", [SLOTS, C], F32)

        ps = ctx.enter_context(nc.psum_tensor("ps", [P, 8, 512], F32))

        def bank(i, p0, p1, *dims, off=0):
            return V(ps, p0, 512 * i + off, [[1, p1 - p0], *dims])

        def cwT_bank(j0=0, nj=J):
            return ps[:, 7, :].bitcast(BF16)[:, j0 * P:(j0 + nj) * P]

        x0 = sb("x0", P, J, C)
        x1 = sb("x1", P, J, C)
        x2 = sb("x2", P, J, C)
        x3 = x1
        xn = sb("xn", P, J, 2, C)
        xT = sb("xT", P, J, P)
        stats = sb("stats", P, J, 6)
        aggr = sb("aggr", P, J, 2)
        veps = sb("veps", P, J)
        rstd = sb("rstd", P, J)
        mhalf = sb("mhalf", P, J)
        ident = sb("ident", P, P)
        tri = sb("tri", P, P)
        img = sb("img", P, J, C)
        zero = sb("zero", P, 1058)
        o_tok = sb("o_tok", P, J, C)
        pidx = sb("pidx", P, 4, dt=I32)
        pf = sb("pf", P, 4)
        gsel = sb("gsel", P, G1)
        e4 = sb("e4", P, G1)
        jneg = sb("jneg", P, J, E)
        cval = sb("cval", P, 8)
        flagf = sb("flagf", P, 4)
        flagi = sb("flagi", 1, 4, dt=I32)
        w_in = sb("w_in", C + 1, C)
        w_out = sb("w_out", C + 1, C)
        w_om = sb("w_om", P, 3 * GP0)
        b_om = sb("b_om", P, 3 * GP0)
        w_dc = sb("w_dc", P, K + 4)
        bn = sb("bn", P, 8)
        w_g0 = sb("w_g0", C + 1, E)
        w_10 = sb("w_10", P, E * F0)
        w_20 = sb("w_20", F0, E * C)
        b_20 = sb("b_20", NPART * E, C)
        b_rest = sb("b_rest", NPART * E, C)
        b_parts = sb("b_parts", NPART * E, NPART, C, dt=BF16)
        w_i1 = sb("w_i1", P, 2, C)
        w_of = sb("w_of", P, 2, 54)
        w_ob = sb("w_ob", P, 2, 3, 72)
        b_of = sb("b_of", 72, 1)
        w_dp = sb("w_dp", P, 5, K + C1 + 1)
        w_pb = sb("w_pb", P, 5, C)
        w_cv = sb("w_cv", P, 5, 3, 3, C)
        two = sb("two", P, C)
        b_pw = sb("b_pw", C, 1)
        b_cv = sb("b_cv", C, 1)
        w_g1 = sb("w_g1", C + 1, E)
        w_11 = sb("w_11", P, E * F1)
        w_21 = sb("w_21", P, 2 * E, C)
        b_21 = sb("b_21", C, E)
        lg = sb("lg", P, J, E)
        lgw = sb("lgw", P, J, E)
        t1 = sb("t1", P, J, E)
        t2 = sb("t2", P, J, E)
        oh1 = sb("oh1", P, J, E)
        oh2 = sb("oh2", P, J, E)
        ex = sb("ex", P, J, E)
        cw = sb("cw", P, J, E)
        m1 = sb("m1", P, J)
        m2 = sb("m2", P, J)
        den = sb("den", P, J)
        cum = sb("cum", P, J, E)
        total1 = sb("total1", P, E)
        cw_parts = sb("cw_parts", P, J, P, dt=BF16)
        cw_rest = sb("cw_rest", P, J, E)
        cwT = sb("cwT", P, J, P, dt=BF16)
        ident_bf = sb("ident_bf", P, P, dt=BF16)
        pick = sb("pick", P, E, P, dt=BF16)
        pick8 = sb("pick8", P, E)
        ysum = o_tok
        trash = sb("trash", P, J)
        slot = sb("slot", P, J)
        posf = sb("posf", P, J)
        lost = sb("lost", P, J)
        wtok = sb("wtok", P, J)
        idx_in = sb("idx_in", P, J, dt=U32)
        idx_out = sb("idx_out", P, J, dt=U32)
        big1e4 = sb("big1e4", P, 3, 1)
        NP0 = (H + 2) * (W + 2)
        cm = sb("cm", P, B * NP0)
        cpad, dwc, x1T, cpad1 = (cm, 0), (cm, 2 * NP0), (o_tok, 0), (cm, 0)
        ox = sb("ox", P, J * GP0)
        oy = sb("oy", P, J * GP0)
        ml = sb("ml", P, J * GP0)
        m64 = sb("m64", P, J * G0)
        r64 = sb("r64", P, J * G0)
        abx = sb("abx", P, J * GP0)
        aby = sb("aby", P, J * GP0)
        BIG = 19760
        big = sb("big", P, BIG)
        ring = sb("ring", P, 6144)
        nmask = ring[:, :].bitcast(I32)
        base1 = sb("base1", P, J * 2 * GP1)
        loc1, u1 = abx, aby
        val1 = sb("val1", P, J * 2 * GP1)
        fslab = sb("fslab", P, (HC + 2 * RB) * C)
        offT = fslab[0:72, 0:B * H * W]
        convT_of = (ring, 0)
        convT = ring[:, 0:B * H * W]
        fy = sb("fy", P, J * GP0)
        fx = sb("fx", P, J * GP0)
        fcnt = sb("fcnt", P, 2)

        def bigv(off, *dims, p=P):
            return V(big, 0, off, [[1, p], *dims])
        SLAB0 = (HC + 2 * R0) * C
        SLAB1 = (HC + 2 * R1) * C
        TX, TY = N0 * SLAB0, N0 * SLAB0 + D0 * J * GP0
        AW = TY + D0 * J * GP0
        A_PITCH = N0 * J * G0
        NA = N0 * A_PITCH
        assert AW + NA <= BIG
        AD = N1 * SLAB1
        T1 = AD + 9 * J * GP1
        SM = T1 + 3 * J * 2 * GP1
        ST = SM + J * K1 * C
        STN = B * NP0
        XS, XST = 0, ST_N * C
        HS = XST + SLOTS
        YT = HS + 2 * E * CAP
        YS = YT + SLOTS
        YG = YS + ST_N * C
        Y0 = E * 512
        assert ST + 5 * STN <= BIG, ST + 5 * STN

        block = ctx.enter_context(nc.Block())

        def pad_image(copy, n):
            for hf in range(2):
                for b in range(B):
                    last = copy(V(cpad1, C * hf, b * NP0 + (W + 2) * (1 - hf) + 1 + HJ * n,
                                  [[1, C], [1, HJ], [W + 2, H], [HC, 2]]),
                                bank(4 + n, C * hf, C * hf + C, [P, HJ], [2, H], [1, 2], off=32 * b))
            return last

        def product_slot(slot):
            return (fslab, 0) if slot == EXTRA_SLOT else (ring, slot * 1024)

        def sample_product(eng, slot, kt, d):
            py, px = divmod(2 * kt, 3)
            dy, dx = divmod(d, 3)
            step = C if px < 2 else SLAB1 - 2 * C
            n = TAPS(kt)
            return eng.tensor_tensor(
                V(product_slot(slot), 0, 0, [[1, P], [512, n], [C1, J * G1], [1, C1]]),
                bigv((py + dy) * SLAB1 + (px + dx) * C, [step, n], [C1, J * G1], [1, C1]),
                bigv(AD + d * J * GP1 + 2 * kt, [1, n], [K, J * G1], [0, C1]), ALU.mult)

        def pair_weights(eng, d):
            dy, dx = divmod(d, 3)
            width = J * 2 * GP1
            eng.tensor_tensor(bigv(AD + d * J * GP1, [GP1, J], [1, GP1]),
                              bigv(T1 + dy * width + GP1, [2 * GP1, J], [1, GP1]),
                              bigv(T1 + dx * width, [2 * GP1, J], [1, GP1]), ALU.mult).then_inc(sem("pairs"), 1)

        def tent_product(eng, dx, dy, slot):
            return eng.tensor_tensor(ring[:, slot:slot + J * GP0],
                                     bigv(TY + dy * J * GP0, [1, J * GP0]), bigv(TX + dx * J * GP0, [1, J * GP0]),
                                     ALU.mult)

        def slab_product(eng, w, slot):
            wx, wy = divmod(w, N0)
            return eng.tensor_tensor(V(ring, 0, slot, [[1, P], [C0, J * G0], [1, C0]]),
                                     bigv(wy * SLAB0 + wx * C, [C0, J * G0], [1, C0]),
                                     bigv(AW + wx * A_PITCH + wy * J * G0, [1, J * G0], [0, C0]), ALU.mult)

        @block.sync
        def _(sp):
            def load(dst, name, s="wts"):
                sp.dma_start(dst, a[name]).then_inc(sem(s), 16)

            sp.dma_start(x0[:, :, :], a["x"].rearrange("b (r q) w c -> (b r q w) c", r=H)
                         .rearrange("(p j) c -> p j c", j=J)).then_inc(sem("x_in"), 16)
            for hf in range(2):
                sp.dma_start(w_dc[C * hf:C * hf + C, :], a["dc"]).then_inc(sem("w_conv0"), 16)
            load(w_in[:, :], "w_in", "w_proj0")
            for hf in range(2):
                sp.dma_start(w_om[C * hf:C * hf + C, :], a["om"]).then_inc(sem("w_offm"), 16)
            sp.dma_start(b_om[:, :], V2(a["omb"], [[0, P], [1, 3 * GP0]])).then_inc(sem("w_offm"), 16)

            sp.wait_ge(sem("zero_set"), 1)
            for pad, reach in ((pad0, R0), (pad1, R1)):
                n = B * (H + 2 * reach) * (W + 2 * reach) * C // P
                sp.dma_start(V2(pad, [[n, P], [1, n]]), zero[:, 0:n]).then_inc(sem("pad_zeroed"), 16)
            sp.dma_start(V2(slots_in, [[ST_N * C, P], [1, ST_N * C]]), zero[:, 0:ST_N * C]
                         ).then_inc(sem("slots_zeroed"), 16)
            load(w_out[:, :], "w_out", "w_o0")
            load(w_g0[:, :], "w_g0", "w_ffn0")
            sp.wait_ge(sem("pads_zero"), 1)
            load(w_10[0:C + 1, :], "w_10", "w_ffn0")
            load(w_20[:, :], "w_20", "w_ffn0")
            load(b_20[:, :], "b_20", "w_ffn0")
            for i in range(2):
                load(w_i1[0:C + 1, i, :], "w_i1", "w_i1")
            load(w_of[:, 0, :], "w_of_a", "w_of")
            load(w_of[0:C, 1, :], "w_of_b", "w_of")
            load(b_of[:, :], "b_of", "w_of")
            sp.dma_start(w_dp[:, 0:4, :], a["w_dp_a"].rearrange("(t q) n -> q t n", t=4)).then_inc(sem("w_dp"), 16)
            for hf in range(2):
                load(w_dp[C * hf:C * hf + C, 4, :], "w_dp_b", "w_dp")
            load(b_pw[:, :], "b_pw", "w_dp")
            load(w_g1[:, :], "w_g1", "w_ffn1")
            load(w_11[0:C + 1, :], "w_11", "w_ffn1")
            sp.dma_start(w_21[:, :, :], a["w_21"].rearrange("(t q) n -> q t n", q=P)).then_inc(sem("w_ffn1"), 16)
            load(b_21[:, :], "b_21", "w_ffn1")

            def image_out(pad, reach, ready, stored):
                wd = W + 2 * reach
                sp.wait_ge(sem(ready), 1)
                for b in range(B):
                    dst = V2(pad, [[wd * C, H], [HC * C, 2], [1, HC * C]],
                             off=((b * (H + 2 * reach) + reach) * wd + reach) * C)
                    sp.dma_start(dst, img[32 * b:32 * b + 32, :, :]).then_inc(sem(stored), 16)

            def slabs_in(pad, reach, stored, arrived):
                wd = W + 2 * reach
                n = 2 * reach + 1
                size = (HC + 2 * reach) * C
                sp.wait_ge(sem(stored), 16 * B)
                for b in range(B):
                    for h in range(2):
                        src = V2(pad, [[wd * C, H], [wd * C, n], [1, size]],
                                 off=(b * (H + 2 * reach) * wd + HC * h) * C)
                        dst = V(big, 32 * b + h, 0, [[2, H], [size, n], [1, size]])
                        sp.dma_start(dst, src).then_inc(sem(arrived), 16)

            def general_loads(tag):
                wd = W + 2 * RB
                flag = sp.value_load(flagi[0:1, tag:tag + 1], min_val=0, max_val=1)
                with sp.If(flag > 0):
                    n = B * (H + 2 * RB) * wd * C // P
                    sp.dma_start(V2(wide, [[n, P], [n // 4, 4], [1, n // 4]]),
                                 V(zero, 0, 0, [[1, P], [0, 4], [1, n // 4]])).then_inc(sem(f"wide_zero{tag}"), 16)
                    sp.wait_ge(sem(f"wide_zero{tag}"), 16)
                    for b in range(B):
                        dst = V2(wide, [[wd * C, H], [HC * C, 2], [1, HC * C]],
                                 off=((b * (H + 2 * RB) + RB) * wd + RB) * C)
                        sp.dma_start(dst, img[32 * b:32 * b + 32, :, :]).then_inc(sem(f"wide_img{tag}"), 16)
                    sp.wait_ge(sem(f"wide_img{tag}"), 16 * B)
                    with sp.Fori(1, NB + 1) as i:
                        sp.wait_ge(sem(f"fslab_used{tag}"), i)
                        for b in range(B):
                            rows = wide.ap()[b, bass.ds(i - 1, H), :, :].rearrange("r w c -> r (w c)")
                            for h in range(2):
                                sp.dma_start(V(fslab, 32 * b + h, 0, [[2, H], [1, (HC + 2 * RB) * C]]),
                                             rows[:, HC * h * C:(HC * h + HC + 2 * RB) * C]
                                             ).then_inc(sem(f"fslab_in{tag}"), 16)
                with sp.Else():
                    sp.nop()

            sp.wait_ge(sem("pad_zeroed"), 32)
            image_out(pad0, R0, "img0", "pad0_stored")
            slabs_in(pad0, R0, "pad0_stored", "slab0")
            sp.wait_ge(sem("flag0"), 1)
            general_loads(0)
            sp.wait_ge(sem("img1"), 1)
            image_out(pad1, R1, "img1", "pad1_stored")
            slabs_in(pad1, R1, "pad1_stored", "slab1")
            sp.wait_ge(sem("flag1"), 1)
            general_loads(1)
            sp.wait_ge(sem("scattered"), 16 * J)
            sp.dma_start(bigv(XS, [1, ST_N * C]), V2(slots_in, [[ST_N * C, P], [1, ST_N * C]])
                         ).then_inc(sem("slots_loaded"), 16)
            sp.wait_ge(sem("ys"), 2)
            sp.dma_start(V2(slots_out, [[ST_N * C, P], [1, ST_N * C]]), bigv(YS, [1, ST_N * C])
                         ).then_inc(sem("slots_stored"), 16)
            for h, cols in enumerate(LAST):
                sp.wait_ge(sem("x4"), h + 1)
                sp.dma_start(out.rearrange("b r w c -> (b r w) c").rearrange("(p j) c -> p j c", j=J)[:, cols, :],
                             x0[:, cols, :]).then_inc(sem("stored"), 16)
            sp.wait_ge(sem("stored"), 16 * len(LAST))

        @block.gpsimd
        def _(pool):
            gp = nc.gpsimd
            n = [0]

            def step(ins):
                n[0] += 1
                ins.then_inc(sem("pool_step"), 1)
                pool.wait_ge(sem("pool_step"), n[0])

            gp.memset(mhalf[:, :], -0.5).then_inc(sem("mhalf"), 1)
            gp.memset(V(cpad, 0, 0, [[1, P], [1, 2 * NP0]]), 0.0).then_inc(sem("cpad_zero"), 1)
            step(gp.memset(ident[:, :], 0.0))
            gp.affine_select(out=ident[:, :], in_=ident[:, :], compare_op=ALU.not_equal, fill=1.0, base=0,
                             pattern=[[-1, P]], channel_multiplier=1).then_inc(sem("ident"), 1)
            gp.memset(zero[:, :], 0.0).then_inc(sem("zero_set"), 1)

            def inv_std(k):
                columns = slice(HJ, J) if k % 2 == 0 else slice(0, HJ)
                pool.wait_ge(sem("mhalf"), 1)
                pool.wait_ge(sem("var"), k)
                gp.tensor_tensor(rstd[:, columns], veps[:, columns], mhalf[:, columns], ALU.pow
                                 ).then_inc(sem("rstd"), 1)
            inv_std(1)
            inv_std(2)
            pool.wait_ge(sem("bnv"), 1)
            gp.tensor_tensor(bn[:, 1:2], bn[:, 0:1], mhalf[:, 0:1], ALU.pow).then_inc(sem("bnr"), 1)
            for weights in (w_cv[:, 4, :, :, :], w_10[:, :], w_i1[:, :, :], w_11[:, :], cw_parts[:, :, :], w_ob[:, 1, :, :]):
                last = gp.memset(weights, 0.0)
            last.then_inc(sem("pads_zero"), 1)
            for k in range(D0):
                last = gp.memset(cval[:, k:k + 1], float(WIN0 - k))
            last.then_inc(sem("cval"), 1)
            gp.memset(bigv(AW, [1, NA]), 0.0).then_inc(sem("A_zero"), 1)

            i = 0
            for dx in range(D0):
                for dy in range(D0):
                    if A_OWNER(dx, dy) == "pool":
                        pool.wait_ge(sem("tenty"), dy + 1)
                        pool.wait_ge(sem("tentx"), dx + 1)
                        if i >= 3:
                            pool.wait_ge(sem("a_ps"), A_COUNT("pool", i - 3))
                        tent_product(gp, dx, dy, POOL0 + J * GP0 * (i % 3)).then_inc(sem("a_pool"), 1)
                        i += 1
            pool.wait_ge(sem("slab0"), 128)
            pool.wait_ge(sem("a_ps"), A_TOTAL)
            order = [w for w in DISPLACED if OWNER(w) == "pool"]
            for i, w in enumerate(order):
                pool.wait_ge(sem("A_done"), w // N0 + 1)
                if i >= 4:
                    pool.wait_ge(sem("acc0"), PE_COUNT(order[i - 4]))
                slab_product(gp, w, POOL0 + 512 * (i % 4)).then_inc(sem("pool_pr0"), 1)
            gp.tensor_copy(ident_bf[:, :], ident[:, :]).then_inc(sem("ident_bf"), 1)
            step(gp.tensor_tensor(pick8[:, :], ident[:, 0:E], ident[:, E:2 * E], ALU.add))
            step(gp.tensor_tensor(pick8[:, :], pick8[:, :], ident[:, 2 * E:3 * E], ALU.add))
            gp.tensor_copy(pick[:, :, :], V(pick8, 0, 0, [[1, P], [1, E], [0, P]])).then_inc(sem("pick"), 1)
            pool.wait_ge(sem("w_ffn0"), 64)
            step(gp.tensor_copy(b_parts[:, 0, :], b_20[:, :]))
            step(gp.tensor_tensor(b_rest[:, :], b_20[:, :], b_parts[:, 0, :], ALU.subtract))
            step(gp.tensor_copy(b_parts[:, 1, :], b_rest[:, :]))
            step(gp.tensor_tensor(b_rest[:, :], b_rest[:, :], b_parts[:, 1, :], ALU.subtract))
            gp.tensor_copy(b_parts[:, 2, :], b_rest[:, :]).then_inc(sem("b_parts"), 1)
            inv_std(3)
            inv_std(4)
            gp.memset(V(cpad1, 0, 0, [[1, P], [1, B * NP0]]), 0.0).then_inc(sem("cpad1_zero"), 1)
            gp.iota(pidx[:, 0:1], [[0, 1]], base=0, channel_multiplier=1).then_inc(sem("pidx"), 1)
            gp.iota(e4[:, :], [[1, G1]], base=0, channel_multiplier=0,
                    allow_small_or_imprecise_dtypes=True).then_inc(sem("pidx"), 1)
            pool.wait_ge(sem("table"), 1)
            gp.iota(trash[:, :], [[1, J]], base=SLOTS, channel_multiplier=J,
                    allow_small_or_imprecise_dtypes=True)
            for g in range(G1):
                gp.iota(V(base1, 0, g * K, [[1, P], [2 * GP1, J], [3, 3], [1, 3]]),
                        [[1, J], [0, 3], [1, 3]], base=-1, channel_multiplier=0,
                        allow_small_or_imprecise_dtypes=True)
                last = gp.iota(V(base1, 0, GP1 + g * K, [[1, P], [2 * GP1, J], [3, 3], [1, 3]]),
                               [[0, J], [1, 3], [0, 3]], base=-1, channel_multiplier=0,
                               allow_small_or_imprecise_dtypes=True)
            last.then_inc(sem("pidx"), 1)
            step(gp.memset(tri[:, :], 1.0))
            gp.affine_select(out=tri[:, :], in_=tri[:, :], compare_op=ALU.is_gt, fill=0.0, base=0,
                             pattern=[[1, P]], channel_multiplier=-1).then_inc(sem("tri"), 1)
            gp.tensor_tensor(two[:, :], ident[:, 0:C], ident[:, C:P], ALU.add).then_inc(sem("two"), 1)
            gp.memset(big1e4[:, 0, :], 1.0e4)
            gp.memset(big1e4[:, 1, :], -1.0e4)
            gp.memset(big1e4[:, 2, :], 0.0).then_inc(sem("limits"), 1)
            inv_std(5)
            inv_std(6)
            pool.wait_ge(sem("w_of"), 48)
            pool.wait_ge(sem("w_dp"), 64)
            pool.wait_ge(sem("gsel"), 1)
            for kt, rows in ((0, P), (1, C)):
                gp.tensor_tensor(V(w_ob, 0, kt * 216, [[1, rows], [36, 6], [9, G1], [1, 9]]),
                                 V(w_of, 0, kt * 54, [[1, rows], [9, 6], [0, G1], [1, 9]]),
                                 V(gsel, 0, 0, [[1, rows], [0, 6], [1, G1], [0, 9]]), ALU.mult
                                 ).then_inc(sem("w_ob"), 1)
            for kt in range(5):
                gp.tensor_tensor(V(w_pb, 0, kt * C, [[1, P], [C1, G1], [1, C1]]),
                                 V(w_dp, 0, kt * 26 + K, [[1, P], [0, G1], [1, C1]]),
                                 V(gsel, 0, 0, [[1, P], [1, G1], [0, C1]]), ALU.mult).then_inc(sem("w_pb"), 1)
            pool.wait_ge(sem("w_pb"), 5)
            for n, (p0, p1, kt, ky, n_ky) in enumerate(
                    [(0, P, kt, 0, 3) for kt in range(4)] + [(0, C, 4, 0, 1), (C, P, 4, 1, 2)]):
                if n >= 4:
                    pool.wait_ge(sem("w_cv"), n)
                gp.tensor_tensor(V(w_cv, p0, kt * K * C, [[1, p1 - p0], [3 * C, 3], [C, n_ky], [1, C]]),
                                 V(w_dp, p0, kt * 26 + 3 * ky, [[1, p1 - p0], [1, 3], [3, n_ky], [0, C]]),
                                 V(w_pb, p0, kt * C, [[1, p1 - p0], [0, 3], [0, n_ky], [1, C]]), ALU.mult
                                 ).then_inc(sem("w_cv"), 1)
            pool.wait_ge(sem("w_cv"), 6)
            gp.memset(bigv(ST, [1, 5 * STN]), 0.0).then_inc(sem("st_zero"), 1)
            pool.wait_ge(sem("val1"), 1)
            gp.tensor_scalar(ml[:, :], val1[:, :], -1.0, None, ALU.mult).then_inc(sem("neg_val1"), 1)
            pool.wait_ge(sem("tents1"), 1)
            for d in range(9 - POOL_PAIRS, 9):
                pair_weights(gp, d)
            pool.wait_ge(sem("slab1"), 128)
            pool.wait_ge(sem("pairs"), 9)
            k = 0
            for kt in range(5):
                for d in POOL_D(kt):
                    if k >= POOL_SLOTS:
                        chain, count = POOL_USED(k - POOL_SLOTS)
                        pool.wait_ge(sem(chain), count)
                    sample_product(gp, k % POOL_SLOTS, kt, d).then_inc(sem("pool_pr1"), 1)
                    k += 1
            inv_std(7)
            inv_std(8)
            pool.wait_ge(sem("slots_zeroed"), 16)
            pool.wait_ge(sem("idx"), 1)
            pool.wait_ge(sem("xn"), 8)
            for j in range(J):
                gp.indirect_dma_start(out=slots_in.ap(), out_offset=bass.IndirectOffsetOnAxis(
                    ap=idx_in[:, j:j + 1], axis=0), in_=xn[:, j, 0, :], in_offset=None
                ).then_inc(sem("scattered"), 16)
            pool.wait_ge(sem("slots_stored"), 16)
            pool.wait_ge(sem("idx"), 2)
            for j in range(J):
                gp.indirect_dma_start(out=bigv(YG + j * C, [1, C]), out_offset=None, in_=slots_out.ap(),
                                      in_offset=bass.IndirectOffsetOnAxis(ap=idx_out[:, j:j + 1], axis=0)
                                      ).then_inc(sem(f"gathered{sum(j >= part.stop for part in LAST)}"), 16)

        @block.scalar
        def _(act):
            sc = nc.scalar

            def copy_T(k, halves=range(2)):
                for h in halves:
                    act.wait_ge(sem("xT_ps"), 2 * k + h - 1)
                    sc.copy(xT[0:C, HJ * h:HJ * h + HJ, :], bank(h, 0, C, [1, 512])).then_inc(sem("xT"), 1)

            def gate_exp(k):
                act.wait_ge(sem("gate_in"), k)
                sc.activation(ex[:, :, :], lgw[:, :, :], ACT.Exp).then_inc(sem("gate_ex"), 1)

            copy_T(1)
            act.wait_ge(sem("img0_ps"), 2)
            sc.copy(V(img, 0, 0, [[1, P], [256, 2], [1, 256]]), bank(2, 0, P, [512, 2], [1, 256])).then_inc(sem("img0"), 1)
            act.wait_ge(sem("mhalf"), 1)
            sc.activation(trash[:, 0:1], mhalf[:, 0:1], ACT.Silu).then_inc(sem("table"), 1)
            act.wait_ge(sem("bn"), 1)
            act.wait_ge(sem("dwc"), 1)
            sc.activation(V(x1T, 0, 0, [[1, P], [256, 2], [16, 16], [1, 16]]),
                          V(dwc, 0, 0, [[1, P], [288, 2], [18, 16], [1, 16]]), ACT.Silu,
                          bias=bn[:, 3:4], scale=bn[:, 2:3]).then_inc(sem("x1T"), 1)
            act.wait_ge(sem("offx"), 1)
            act.wait_ge(sem("cval"), 1)
            made = {"tentx": 0, "tenty_raw": 0}
            for n, (name, src, base, k) in enumerate(
                    [("tentx", ox, TX, 0)] + [("tenty_raw", oy, TY, k) for k in range(DVE_TENTS, D0)] +
                    [("tentx", ox, TX, k) for k in range(1, D0)]):
                if n == 1:
                    act.wait_ge(sem("mask_in"), 1)
                    sc.activation(ml[:, :], ml[:, :], ACT.Exp).then_inc(sem("mask_e"), 1)
                    act.wait_ge(sem("offy"), 1)
                if n:
                    act.wait_ge(sem(before), made[before])
                sc.activation(abx[:, :], src[:, :], ACT.Abs, bias=cval[:, k:k + 1]).then_inc(sem("abx"), 1)
                act.wait_ge(sem("abx"), n + 1)
                sc.activation(bigv(base + k * J * GP0, [1, J * GP0]), abx[:, :], ACT.Relu, bias=1.0,
                              scale=-1.0).then_inc(sem(name), 1)
                made[name] += 1
                before = name
            act.wait_ge(sem(before), made[before])
            sc.activation(abx[:, :], ox[:, :], ACT.Abs).then_inc(sem("off_abs"), 1)
            act.wait_ge(sem("tenty"), DVE_TENTS)
            sc.activation(aby[:, :], oy[:, :], ACT.Abs).then_inc(sem("off_abs"), 1)
            copy_T(2)
            copy_T(3)
            gate_exp(1)
            for u in range(2 * E):
                act.wait_ge(sem("h0_ps"), u + 1)
                if u >= E:
                    act.wait_ge(sem("y0_ps"), u - E + 1)
                sc.activation(bigv((u % E) * 512, [1, 512]), bank(u % 2, 0, F0, [1, 512]), ACT.Gelu
                              ).then_inc(sem("h0"), 1)
                if u == AHEAD - 1:
                    act.wait_ge(sem("cwT_ps"), 1)
                    sc.copy(cwT[:, :, :], cwT_bank()).then_inc(sem("cwT"), 1)
            for hf in range(2):
                act.wait_ge(sem("y0_ps"), E * (hf + 1))
                sc.copy(bigv(Y0 + 512 * hf, [1, 512], p=C), bank(4 + hf, 0, C, [1, 512])).then_inc(sem("yT0"), 1)
                if hf == 0:
                    copy_T(4, [0])
            act.wait_ge(sem("cpad1_zero"), 1)
            act.wait_ge(sem("imgT_ps"), 1)
            pad_image(sc.copy, 0).then_inc(sem("cpad1"), 1)
            copy_T(4, [1])
            act.wait_ge(sem("img1_ps"), 2)
            sc.copy(V(img, 0, 0, [[1, P], [256, 2], [1, 256]]), bank(2, 0, P, [512, 2], [1, 256])).then_inc(sem("img1"), 1)
            act.wait_ge(sem("w_of"), 48)
            act.wait_ge(sem("offT_ps"), 1)
            sc.activation(offT, bank(0, 0, 72, [1, 1024]), ACT.Identity, bias=b_of[:, 0:1]
                          ).then_inc(sem("offT"), 1)
            act.wait_ge(sem("off1"), 1)
            sc.activation(loc1[:, :], u1[:, :], ACT.Abs).then_inc(sem("tent1"), 1)
            act.wait_ge(sem("tent1"), 1)
            sc.activation(loc1[:, :], loc1[:, :], ACT.Relu, bias=1.0, scale=-1.0).then_inc(sem("tent1"), 1)
            act.wait_ge(sem("st_zero"), 1)
            for kt in range(5):
                act.wait_ge(sem("st_ps"), kt + 1)
                for p0, p1, up in (((0, P, 0),) if kt < 4 else ((0, C, 0), (C, P, 1))):
                    for b in range(B):
                        last = sc.copy(V(big, p0, ST + kt * STN + b * NP0 + (W + 2) * (1 - up) + 1,
                                         [[1, p1 - p0], [1, J], [W + 2, H], [HC, 2]]),
                                       bank(2 * (kt % 2), p0, p1, [P, J], [2, H], [1, 2], off=32 * b))
                last.then_inc(sem("st"), 1)
            act.wait_ge(sem("b_cv"), 1)
            act.wait_ge(sem("conv_ps"), 1)
            sc.activation(convT[0:C, :], bank(4, 0, C, [1, 1024]), ACT.Identity, bias=b_cv[:, 0:1]
                          ).then_inc(sem("convT"), 1)
            copy_T(5)
            gate_exp(2)
            act.wait_ge(sem("xs_ps"), 1)
            sc.copy(bigv(XST, [1, 1024], p=C), bank(0, 0, C, [1, 1024])).then_inc(sem("xsT"), 1)
            for n in range(HB):
                if n % 2 == 0:
                    act.wait_ge(sem("h1_ps"), n + 1)
                    w = min(3, 2 * E - 3 * n) * CAP
                    sc.activation(bigv(HS + n * 3 * CAP, [1, w]), bank(n, 0, P, [1, w]), ACT.Relu
                                  ).then_inc(sem("h1_act"), 1)
            act.wait_ge(sem("w_ffn1"), 64)
            act.wait_ge(sem("yT_ps"), 2)
            b, e0, ne = Y_GROUPS[1]
            for e in range(e0, e0 + ne):
                last = sc.activation(bigv(YT + e * QE, [P, ST_N], [1, QE], p=C),
                                     bank(b, 0, C, [QE, ST_N], [1, QE], off=(e - e0) * CAP), ACT.Identity,
                                     bias=b_21[:, e:e + 1])
            last.then_inc(sem("yT"), 1)
            act.wait_ge(sem("ys_ps"), 2)
            sc.copy(bigv(YS + 8 * C, [1, (ST_N - 8) * C]), bank(4, 0, P, [1, (ST_N - 8) * C])).then_inc(sem("ys"), 1)

        @block.tensor
        def _(pe):
            mm, tr = nc.tensor.matmul, nc.tensor.transpose

            def keep_clock(n, free_bank):
                for _ in range(n):
                    mm(bank(free_bank, 0, P, [1, 512]), ident[:, :], zero[:, 0:512], start=True, stop=True)

            def transposes(k, src, ready, done_before, halves=range(2), m=C):
                pe.wait_ge(sem("ident"), 1)
                for h in halves:
                    pe.wait_ge(sem(ready), 2 * done_before + h + 1)
                    for j in range(HJ * h, HJ * h + HJ):
                        last = tr(bank(h, 0, m, [1, P], off=(j % HJ) * P), src(j), ident[:, :])
                    last.then_inc(sem("xT_ps"), 1)

            def normalised(j):
                return xn[:, j, 0, :]

            def project(w, first_bank, width, done, k, slot=C):
                for j in range(J):
                    if j % HJ == 0:
                        pe.wait_ge(sem("xT"), 2 * k - 1 + j // HJ)
                    last = mm(bank(first_bank + j // HJ, 0, P, [1, width], off=(j % HJ) * slot), xT[0:C + 1, j, :], w,
                              start=True, stop=True)
                    if j % HJ == HJ - 1:
                        last.then_inc(sem(done), 1)

            transposes(1, lambda j: xn[:, j, :, :], "xn", 0, m=P)
            pe.wait_ge(sem("w_proj0"), 16)
            pe.wait_ge(sem("ones_row"), 1)
            project(w_in[:, :], 2, C, "img0_ps", 1)
            pe.wait_ge(sem("zero_set"), 1)
            keep_clock(4, 4)
            pe.wait_ge(sem("x1T"), 1)
            pe.wait_ge(sem("w_offm"), 48)
            for j in range(J):
                for hf in range(2):
                    p0 = C * hf
                    last = mm(bank(4 + j // 2, p0, p0 + C, [1, 3 * GP0], off=256 * (j % 2)),
                              V(x1T, p0, j, [[1, C], [J, C]]), w_om[p0:p0 + C, :], start=True, stop=True)
                if j % 2:
                    last.then_inc(sem("om_ps"), 1)
            pe.wait_ge(sem("zero_set"), 1)
            pe.wait_ge(sem("img0"), 1)
            for wx in range(N0):
                if wx == 4:
                    pe.wait_ge(sem("offx"), 1)
                    pe.wait_ge(sem("ml"), 1)
                    pe.wait_ge(sem("offy"), 1)
                mm(bank(wx, 0, P, [1, A_PITCH]), ident[:, :], zero[:, 0:A_PITCH], start=True, stop=False,
                   skip_group_check=True)
            for n, (dx, dy) in enumerate(A_ORDER):
                who = A_OWNER(dx, dy)
                i = A_ORDER_OF(who).index((dx, dy))
                pe.wait_ge(sem("a_pool" if who == "pool" else "a_dve"), i + 1)
                slot = POOL0 + J * GP0 * (i % 3) if who == "pool" else J * GP0 * (i % 2)
                for px in range(3):
                    last = mm(bank(px + dx, 0, P, [1, 3 * J * G0], off=dy * J * G0), ident[:, :],
                              V(ring, 0, slot + 3 * px, [[1, P], [1, 3], [K, J * G0]]), start=False,
                              stop=(n == len(A_ORDER) - 1), skip_group_check=True)
                last.then_inc(sem("a_ps"), 1)
            seen = {"pool": 0, "dve": 0}
            first = True
            for w in PE_ORDER:
                who = OWNER(w)
                i = seen[who]
                seen[who] += 1
                pe.wait_ge(sem("pool_pr0" if who == "pool" else "dve_pr0"), i + 1)
                slot = (POOL0 if who == "pool" else 0) + 512 * (i % 4)
                mm(bank(7, 0, P, [1, 512]), ident[:, :], ring[:, slot:slot + 512], start=first,
                   stop=(w == PE_ORDER[-1])).then_inc(sem("acc0"), 1)
                first = False
                if w == PE_ORDER[FLAG_AT[1]]:
                    pe.wait_ge(sem("off_max"), 1)
                    tr(bank(2, 0, 1, [1, P]), flagf[:, 0:1], ident[:, :]).then_inc(sem("off_maxT"), 1)
            transposes(2, lambda j: o_tok[:, j, :], "o_tok", 0)
            pe.wait_ge(sem("w_o0"), 16)
            project(w_out[:, :], 2, C, "x1_ps", 2)

            keep_clock(3, 4)
            transposes(3, normalised, "xn", 1)
            pe.wait_ge(sem("w_ffn0"), 64)
            project(w_g0[:, :], 4, E, "gate_ps", 3, slot=E)

            def hidden(u):
                hf, e = divmod(u, E)
                if u >= 2:
                    pe.wait_ge(sem("h0"), u - 1)
                mm(bank(u % 2, 0, F0, [1, 512]), w_10[:, F0 * e:F0 * e + F0], xT[:, 4 * hf:4 * hf + 4, :],
                   start=True, stop=True).then_inc(sem("h0_ps"), 1)

            def gates(u):
                hf, e = divmod(u, E)
                if u >= 2:
                    pe.wait_ge(sem("hw"), u - 1)
                mm(bank(2 + u % 2, 0, F0, [1, 512]), pick[:, e, :], cwT[:, 4 * hf:4 * hf + 4, :],
                   start=True, stop=True).then_inc(sem("cwb_ps"), 1)

            def biases(hf):
                for part in range(NPART):
                    mm(bank(4 + hf, 0, C, [1, 512]), b_parts[:, part, :], cwT[0:NPART * E, 4 * hf:4 * hf + 4, :],
                       start=(part == 0), stop=False, skip_group_check=True)

            def outputs_by_token(hf):
                pe.wait_ge(sem("yT0"), hf + 1)
                for j in range(4 * hf, 4 * hf + 4):
                    last = tr(bank(6, 0, P, [1, C], off=j * C), bigv(Y0 + j * P, [1, P], p=C), ident[0:C, 0:C])
                last.then_inc(sem("y0_tok"), 1)

            for u in range(AHEAD):
                hidden(u)
            pe.wait_ge(sem("cw"), 1)
            pe.wait_ge(sem("ident_bf"), 1)
            for j in range(J):
                last = tr(cwT_bank(j, 1), cw_parts[:, j, :], ident_bf[:, :])
            last.then_inc(sem("cwT_ps"), 1)
            for u in range(AHEAD, E):
                hidden(u)
            pe.wait_ge(sem("cwT"), 1)
            pe.wait_ge(sem("pick"), 1)
            pe.wait_ge(sem("b_parts"), 1)
            gates(0)
            gates(1)
            biases(0)
            biases(1)
            for u in range(2 * E):
                hf, e = divmod(u, E)
                pe.wait_ge(sem("hw"), u + 1)
                mm(bank(4 + hf, 0, C, [1, 512]), w_20[:, C * e:C * e + C], bigv((u % E) * 512, [1, 512]),
                   start=False, stop=(e == E - 1), skip_group_check=True).then_inc(sem("y0_ps"), 1)
                if u + 2 < 2 * E:
                    gates(u + 2)
                if u + E < 2 * E:
                    hidden(u + E)
                if u == E + 1:
                    outputs_by_token(0)
                if u == E + 5:
                    transposes(4, normalised, "xn", 2, [0])

            def image_by_channel(n):
                pe.wait_ge(sem("xT"), 7 + n)
                mm(bank(4 + n, 0, P, [1, 512]), w_i1[:, :, :], xT[:, 4 * n:4 * n + 4, :], start=True, stop=True
                   ).then_inc(sem("imgT_ps"), 1)
            pe.wait_ge(sem("w_i1"), 32)
            image_by_channel(0)
            outputs_by_token(1)
            keep_clock(4, 7)
            transposes(4, normalised, "xn", 2, [1])
            image_by_channel(1)
            project(w_i1[0:C + 1, 0, :], 2, C, "img1_ps", 4)
            pe.wait_ge(sem("w_ob"), 2)
            pe.wait_ge(sem("cpad1"), 2)
            for n in range(2):
                k = 0
                for kt, rows, dy in ((0, P, 0), (1, P, 2)):
                    for kx in range(3):
                        last = mm(bank(n, 0, 72, [1, 512]), V(w_ob, 0, kt * 216 + kx * 72, [[1, rows], [1, 72]]),
                                  V(cpad1, 0, 2 * n * NP0 + dy * (W + 2) + kx,
                                    [[1, rows], [NP0, 2], [W + 2, H], [1, W]]),
                                  start=(k == 0), stop=(k == 5))
                        k += 1
            last.then_inc(sem("offT_ps"), 1)
            pe.wait_ge(sem("offT"), 1)
            for j in range(J):
                last = tr(bank(2 + j // 4, 0, P, [1, 72], off=(j % 4) * P), V(fslab, 0, j, [[1, 72], [J, P]]),
                          ident[0:72, 0:72])
            last.then_inc(sem("off1_ps"), 1)
            pe.wait_ge(sem("off_max"), 2)
            tr(bank(6, 0, 1, [1, P]), flagf[:, 1:2], ident[:, :]).then_inc(sem("off_maxT"), 1)
            pe.wait_ge(sem("w_pb"), 5)
            for kt in range(5):
                rows = P if kt < 4 else C
                last = mm(bank(7, 0, C, [1, 1]), w_pb[0:rows, kt, :], w_dp[0:rows, kt, K + C1:K + C1 + 1],
                          start=(kt == 0), stop=(kt == 4))
            last.then_inc(sem("b_cv_ps"), 1)
            pe.wait_ge(sem("w_cv"), 6)
            def samples_by_channel(kt):
                pe.wait_ge(sem("sampled"), kt + 1)
                if kt >= 2:
                    pe.wait_ge(sem("st"), kt - 1)
                for j in range(J):
                    last = tr(bank(2 * (kt % 2) + j // 4, 0, P, [1, P], off=(j % 4) * P),
                              bigv(SM + j * K1 * C + kt * P, [1, P]), ident[:, :])
                last.then_inc(sem("st_ps"), 1)

            pe.wait_ge(sem("even"), 4)
            keep_clock(3, 4)
            samples_by_channel(0)
            for kt in range(5):
                pe.wait_ge(sem("st"), kt + 1)
                for i in range(6):
                    n, kx = divmod(i, 3)
                    if kt < 4 and i == NEXT_TILE[kt]:
                        samples_by_channel(kt + 1)
                    for ky, m in (((1, 2 * C), (0, C)) if kt < 4 else ((0, 2 * C),)):
                        last = mm(bank(4 + n, 0, m, [1, 512]),
                                  V(w_cv, 0, ((kt * 3 + kx) * 3 + ky) * C, [[1, P], [1, m]]),
                                  V(big, 0, ST + kt * STN + 2 * n * NP0 + ky * (W + 2) + kx,
                                    [[1, P], [NP0, 2], [W + 2, H], [1, W]]),
                                  start=(kt == 0 and kx == 0 and ky == 1),
                                  stop=(kt == 4 and kx == 2), skip_group_check=True)
            last.then_inc(sem("conv_ps"), 1)
            pe.wait_ge(sem("convT"), 1)
            pe.wait_ge(sem("convT_up"), B + 1)
            pe.wait_ge(sem("two"), 1)
            for j in range(J):
                last = mm(bank(2 + j // HJ, 0, P, [1, C], off=(j % HJ) * C), V(convT_of, 0, j, [[1, P], [J, P]]), two[:, :],
                          start=True, stop=True)
                if j % HJ == HJ - 1:
                    last.then_inc(sem("x3_ps"), 1)

            keep_clock(3, 4)
            transposes(5, normalised, "xn", 3)
            pe.wait_ge(sem("w_ffn1"), 64)
            project(w_g1[:, :], 4, E, "gate_ps", 5, slot=E)
            pe.wait_ge(sem("tri"), 1)
            pe.wait_ge(sem("tot"), 1)
            mm(bank(5, 0, P, [1, E]), tri[:, :], total1[:, :], start=True, stop=True).then_inc(sem("before"), 1)
            pe.wait_ge(sem("scattered"), 16 * J)
            keep_clock(2, 6)
            pe.wait_ge(sem("slots_loaded"), 16)
            for i in range(ST_N):
                last = tr(bank(i // 4, 0, C, [1, P], off=(i % 4) * P), bigv(XS + i * C, [1, C]), ident[:, :])
            last.then_inc(sem("xs_ps"), 1)
            pe.wait_ge(sem("xsT"), 2)
            pe.wait_ge(sem("xsT2"), 1)
            for f in range(2 * E):
                n = f // 3
                last = mm(bank(n, 0, P, [1, CAP], off=(f % 3) * CAP), w_11[:, P * f:P * f + P],
                          bigv(XST + (f // 2) * QE, [P, ST_N], [1, QE]), start=True, stop=True)
                if f % 3 == 2 or f == 2 * E - 1:
                    last.then_inc(sem("h1_ps"), 1)
            for e in range(E):
                n = (2 * e + 1) // 3
                pe.wait_ge(sem("h1_act"), n // 2 + 1)
                if n:
                    pe.wait_ge(sem("h1_dve"), (n + 1) // 2)
                for f in range(2):
                    last = mm(bank(Y_GROUPS[e // 3][0], 0, C, [1, CAP], off=(e % 3) * CAP), w_21[:, 2 * e + f, :],
                              bigv(HS + (2 * e + f) * CAP, [1, CAP]), start=(f == 0), stop=(f == 1),
                              skip_group_check=True)
                if e in (2, 5, 7):
                    last.then_inc(sem("yT_ps"), 1)
            pe.wait_ge(sem("yT"), 3)
            for i in range(ST_N):
                last = tr(bank(3 + i // 8, 0, P, [1, C], off=(i % 8) * C), bigv(YT + i * P, [1, P], p=C),
                          ident[0:C, 0:C])
                if i in (7, ST_N - 1):
                    last.then_inc(sem("ys_ps"), 1)

        @block.vector
        def _(dve):
            v = nc.vector
            n = [0]

            def step(ins):
                n[0] += 1
                ins.then_inc(sem("dve_step"), 1)
                dve.wait_ge(sem("dve_step"), n[0])

            def moments(src, columns):
                for j in columns:
                    last = v.bn_stats(stats[:, j, :], src[:, j, :])
                step(last)
                for j in columns:
                    last = v.bn_aggr(aggr[:, j, :], stats[:, j, :])
                step(last)

            def inverse_std(columns, eps):
                v.tensor_scalar(veps[:, columns], aggr[:, columns, 1], eps, None, ALU.add).then_inc(sem("var"), 1)

            def normalise(src, dup, columns):
                for j in columns:
                    last = v.tensor_scalar(xn[:, j, 0:dup, :], V(src, 0, j * C, [[1, P], [0, dup], [1, C]]),
                                           aggr[:, j, 0:1], rstd[:, j:j + 1], ALU.subtract, ALU.mult)
                last.then_inc(sem("xn"), 1)

            def layernorm(k, src, eps, dup, before=None):
                for h in range(2):
                    if before is not None:
                        before(h)
                    moments(src, range(HJ * h, HJ * h + HJ))
                    inverse_std(slice(HJ * h, HJ * h + HJ), eps)
                for h in range(2):
                    dve.wait_ge(sem("rstd"), 2 * k - 1 + h)
                    normalise(src, dup, range(HJ * h, HJ * h + HJ))

            def flag_finish(tag, src_bank, limit, op):
                dve.wait_ge(sem("off_maxT"), tag + 1)
                step(v.tensor_reduce(flagf[0:1, 2:3], bank(src_bank, 0, 1, [1, P]), AX.X, ALU.max))
                v.tensor_scalar(flagi[0:1, tag:tag + 1], flagf[0:1, 2:3], limit, None, op).then_inc(sem(f"flag{tag}"), 1)
                dve.wait_ge(sem(f"flag{tag}"), 1)

            step(v.memset(xT[C:P, :, :], 0.0))
            v.memset(xT[C:C + 1, :, :], 1.0).then_inc(sem("ones_row"), 1)
            dve.wait_ge(sem("x_in"), 16)
            layernorm(1, x0, 1e-6, 2)
            dve.wait_ge(sem("w_conv0"), 32)
            v.tensor_scalar(bn[:, 0:1], w_dc[:, K + 3:K + 4], 1e-5, None, ALU.add).then_inc(sem("bnv"), 1)
            dve.wait_ge(sem("cpad_zero"), 1)
            dve.wait_ge(sem("xT"), 2)
            for hf in range(2):
                for b in range(2):
                    last = v.tensor_copy(V(cpad, C * hf, b * NP0 + W + 2 + 1, [[1, C], [1, J], [W + 2, H], [HC, 2]]),
                                         bank(0, C * hf, C * hf + C, [P, J], [2, H], [1, 2],
                                              off=32 * (2 * hf + b)))
            step(last)
            n_dw = 15 * (W + 2) + W
            for tap in range(K):
                ky, kx = divmod(tap, 3)
                src = V(cpad, 0, ky * (W + 2) + kx, [[1, P], [NP0, 2], [1, n_dw]])
                dst = V(dwc, 0, 0, [[1, P], [H * (W + 2), 2], [1, n_dw]])
                if tap == 0:
                    step(v.tensor_scalar(dst, src, w_dc[:, 0:1], None, ALU.mult))
                elif tap < K - 1:
                    step(v.scalar_tensor_tensor(dst, src, w_dc[:, tap:tap + 1], dst, ALU.mult, ALU.add))
                else:
                    v.scalar_tensor_tensor(dst, src, w_dc[:, tap:tap + 1], dst, ALU.mult, ALU.add).then_inc(sem("dwc"), 1)
            dve.wait_ge(sem("bnr"), 1)
            step(v.tensor_tensor(bn[:, 2:3], w_dc[:, K:K + 1], bn[:, 1:2], ALU.mult))
            step(v.tensor_tensor(bn[:, 4:5], w_dc[:, K + 2:K + 3], bn[:, 2:3], ALU.mult))
            v.tensor_tensor(bn[:, 3:4], w_dc[:, K + 1:K + 2], bn[:, 4:5], ALU.subtract).then_inc(sem("bn"), 1)
            dve.wait_ge(sem("w_offm"), 48)
            for q in range(J // 2):
                dve.wait_ge(sem("om_ps"), q + 1)
                for dst, c0, signal in ((ox, 0, "offx"), (ml, 2 * GP0, "ml"), (oy, GP0, "offy")):
                    last = v.tensor_tensor(V(dst, 0, 2 * q * GP0, [[1, P], [GP0, 2], [1, GP0]]),
                                           bank(4 + q, 0, P, [256, 2], [1, GP0], off=c0),
                                           V(b_om, 0, c0, [[1, P], [0, 2], [1, GP0]]), ALU.add)
                    if q == J // 2 - 1:
                        last.then_inc(sem(signal), 1)
            dve.wait_ge(sem("ml"), 1)
            step(v.tensor_reduce(m64[:, :], V(ml, 0, 0, [[1, P], [K, J * G0], [1, K]]), AX.X, ALU.max))
            v.tensor_tensor(V(ml, 0, 0, [[1, P], [K, J * G0], [1, K]]), V(ml, 0, 0, [[1, P], [K, J * G0], [1, K]]),
                            V(m64, 0, 0, [[1, P], [1, J * G0], [0, K]]), ALU.subtract).then_inc(sem("mask_in"), 1)
            dve.wait_ge(sem("offy"), 1)
            for k in range(DVE_TENTS):
                d = float(k - WIN0)
                step(v.tensor_scalar(aby[:, :], oy[:, :], -1.0, 1.0 + d, ALU.mult, ALU.add))
                step(v.scalar_tensor_tensor(aby[:, :], oy[:, :], 1.0 - d, aby[:, :], ALU.add, ALU.min))
                dve.wait_ge(sem("mask_e"), 1)
                v.scalar_tensor_tensor(bigv(TY + k * J * GP0, [1, J * GP0]), aby[:, :], 0.0, ml[:, :],
                                       ALU.max, ALU.mult).then_inc(sem("tenty"), 1)
                dve.wait_ge(sem("tenty"), k + 1)
            for k in range(DVE_TENTS, D0):
                dve.wait_ge(sem("tenty_raw"), k - DVE_TENTS + 1)
                tent = bigv(TY + k * J * GP0, [1, J * GP0])
                v.tensor_tensor(tent, tent, ml[:, :], ALU.mult).then_inc(sem("tenty"), 1)
            dve.wait_ge(sem("A_zero"), 1)
            dve.wait_ge(sem("tenty"), D0)
            made, added, to_pe = 0, 0, 0

            def join(wx):
                dve.wait_ge(sem("a_ps"), A_BY(wx))
                if wx < D0:
                    dve.wait_ge(sem("a_added"), added)
                part = bigv(AW + wx * A_PITCH, [1, A_PITCH])
                v.tensor_tensor(part, part, bank(wx, 0, P, [1, A_PITCH]), ALU.add).then_inc(sem("A_done"), 1)

            def add_pending(pending):
                nonlocal added
                i, dx, dy = pending
                dve.wait_ge(sem("a_made"), i + 1)
                dve.wait_ge(sem("a_added"), added)
                dst = bigv(AW + dx * A_PITCH + dy * J * G0, [A_PITCH, 3], [J * G0, 3], [1, J * G0])
                v.tensor_tensor(dst, dst, V(ring, 0, SUM0 + J * GP0 * (i % 2), [[1, P], [3, 3], [1, 3], [K, J * G0]]),
                                ALU.add).then_inc(sem("a_added"), 1)
                added += 1

            for dx in range(D0):
                dve.wait_ge(sem("tentx"), dx + 1)
                pending = []
                for dy in range(D0):
                    if A_OWNER(dx, dy) == "sum":
                        if made >= 2:
                            dve.wait_ge(sem("a_added"), made - 1)
                        tent_product(v, dx, dy, SUM0 + J * GP0 * (made % 2)).then_inc(sem("a_made"), 1)
                        pending.append((made, dx, dy))
                        made += 1
                    elif A_OWNER(dx, dy) == "dve":
                        if to_pe >= 2:
                            dve.wait_ge(sem("a_ps"), A_COUNT("dve", to_pe - 2))
                        tent_product(v, dx, dy, J * GP0 * (to_pe % 2)).then_inc(sem("a_dve"), 1)
                        to_pe += 1
                        if pending:
                            add_pending(pending.pop(0))
                if dx:
                    join(dx - 1)
                while pending:
                    add_pending(pending.pop(0))
            for wx in range(D0 - 1, N0):
                join(wx)
            dve.wait_ge(sem("A_done"), N0)
            dve.wait_ge(sem("slab0"), 128)
            order = [w for w in DISPLACED if OWNER(w) == "dve"]
            own = [w for w in DISPLACED if OWNER(w) == "sum"]
            acc = V(ring, 0, SUM0, [[1, P], [1, 512]])

            def product(w, slot):
                return slab_product(v, w, slot)
            todo = list(order)
            k = 0
            for i in range(len(own) + 1):
                if i == FLAG_AT[0]:
                    dve.wait_ge(sem("off_abs"), 2)
                    v.tensor_reduce(flagf[:, 2:3], abx[:, :], AX.X, ALU.max).then_inc(sem("off_flag"), 1)
                if i == FLAG_AT[0] + 1:
                    v.tensor_reduce(flagf[:, 0:1], aby[:, :], AX.X, ALU.max).then_inc(sem("off_flag"), 1)
                if i == FLAG_AT[0] + 2:
                    v.tensor_tensor(abx[:, :], abx[:, :], aby[:, :], ALU.min).then_inc(sem("off_flag"), 1)
                if i == FLAG_AT[0] + 3:
                    dve.wait_ge(sem("off_flag"), 3)
                    step(v.tensor_reduce(flagf[:, 3:4], abx[:, :], AX.X, ALU.max))
                    step(v.tensor_tensor(flagf[:, 0:1], flagf[:, 0:1], flagf[:, 2:3], ALU.max))
                    v.scalar_tensor_tensor(flagf[:, 0:1], flagf[:, 0:1], 1.0 / WIN0, flagf[:, 3:4], ALU.mult, ALU.max
                                           ).then_inc(sem("off_max"), 1)
                if i == FLAG_AT[2]:
                    flag_finish(0, 2, 1.0, ALU.is_ge)
                    flag = dve.value_load(flagi[0:1, 0:1], min_val=0, max_val=1)
                if i < len(own):
                    if i >= 3:
                        dve.wait_ge(sem("own_sum"), i - 2)
                    product(own[i], SUM0 if i == 0 else OWN0 + 512 * ((i - 1) % 2)).then_inc(sem("own_pr0"), 1)
                while todo and k * len(own) <= i * len(order):
                    if k >= 4:
                        dve.wait_ge(sem("acc0"), PE_COUNT(order[k - 4]))
                    product(todo.pop(0), 512 * (k % 4)).then_inc(sem("dve_pr0"), 1)
                    k += 1
                if i >= 2:
                    dve.wait_ge(sem("own_pr0"), i)
                    if i >= 3:
                        dve.wait_ge(sem("own_sum"), i - 2)
                    v.tensor_tensor(acc, acc, V(ring, 0, OWN0 + 512 * ((i - 2) % 2), [[1, P], [1, 512]]), ALU.add
                                    ).then_inc(sem("own_sum"), 1)
            while todo:
                dve.wait_ge(sem("acc0"), PE_COUNT(order[k - 4]))
                product(todo.pop(0), 512 * (k % 4)).then_inc(sem("dve_pr0"), 1)
                k += 1
            step(v.tensor_reduce(m64[:, :], V(ml, 0, 0, [[1, P], [K, J * G0], [1, K]]), AX.X, ALU.add))
            step(v.reciprocal(r64[:, :], m64[:, :]))
            dve.wait_ge(sem("own_sum"), len(own) - 1)
            dve.wait_ge(sem("acc0"), len(PE_ORDER))
            step(v.tensor_tensor(acc, acc, bank(7, 0, P, [1, 512]), ALU.add))

            def tent_loop(tag, width, xs, ys, prepare, consume):
                prepare()
                m = [0]

                def fstep(ins):
                    m[0] += 1
                    ins.then_inc(sem("general_step"), 1)
                    dve.wait_ge(sem("general_step"), m[0])

                def tent(dst, src, count):
                    fstep(v.tensor_scalar(dst, src, count, None, ALU.subtract))
                    fstep(v.scalar_tensor_tensor(dst, dst, -1.0, dst, ALU.mult, ALU.min))
                    fstep(v.tensor_scalar(dst, dst, 1.0, 0.0, ALU.add, ALU.max))

                v.memset(fcnt[:, 0:1], float(-RB)).then_inc(sem(f"general_start{tag}"), 1)
                dve.wait_ge(sem(f"general_start{tag}"), 1)
                dve.sem_inc(sem(f"fslab_used{tag}"), 1)
                with dve.Fori(1, NB + 1) as i:
                    dve.sem_clear(sem("general_step"))
                    m[0] = 0
                    dve.wait_ge(sem(f"fslab_in{tag}"), i * 128)
                    tent(fy[:, 0:width], ys, fcnt[:, 0:1])
                    fstep(v.memset(fcnt[:, 1:2], float(-RB)))
                    with dve.Fori(0, NB) as k:
                        dve.sem_clear(sem("general_step"))
                        m[0] = 0
                        tent(fx[:, 0:width], xs, fcnt[:, 1:2])
                        fstep(v.tensor_tensor(fx[:, 0:width], fx[:, 0:width], fy[:, 0:width], ALU.mult))
                        consume(fstep, fslab[:, bass.ds(k * C, HC * C)])
                        fstep(v.tensor_scalar(fcnt[:, 1:2], fcnt[:, 1:2], 1.0, None, ALU.add))
                    dve.sem_clear(sem("general_step"))
                    m[0] = 0
                    fstep(v.tensor_scalar(fcnt[:, 0:1], fcnt[:, 0:1], 1.0, None, ALU.add))
                    dve.sem_inc(sem(f"fslab_used{tag}"), 1)

            with dve.If(flag > 0):
                def prepare0():
                    for ap_, px in ((ox, True), (oy, False)):
                        for t in range(3):
                            o = (3 * t if px else t)
                            vw = V(ap_, 0, o, [[1, P], [K, J * G0], [1 if px else 3, 3]])
                            v.tensor_scalar(vw, vw, float(t - 1), None, ALU.add).then_inc(sem("general_prep0"), 1)
                    v.memset(acc, 0.0).then_inc(sem("general_prep0"), 1)
                    dve.wait_ge(sem("general_prep0"), 7)

                def consume0(istep, slab):
                    istep(v.tensor_tensor(fx[:, :], fx[:, :], ml[:, :], ALU.mult))
                    istep(v.tensor_reduce(m64[:, :], V(fx, 0, 0, [[1, P], [K, J * G0], [1, K]]), AX.X, ALU.add))
                    istep(v.tensor_tensor(V(ring, 0, OWN0, [[1, P], [C0, J * G0], [1, C0]]),
                                          slab.rearrange("p (g c) -> p g c", c=C0),
                                          V(m64, 0, 0, [[1, P], [1, J * G0], [0, C0]]), ALU.mult))
                    istep(v.tensor_tensor(acc, acc, V(ring, 0, OWN0, [[1, P], [1, 512]]), ALU.add))
                tent_loop(0, J * GP0, ox[:, :], oy[:, :], prepare0, consume0)
            with dve.Else():
                dve.nop()
            for h in range(2):
                v.tensor_tensor(V(o_tok, 0, 256 * h, [[1, P], [C0, HJ * G0], [1, C0]]),
                                V(ring, 0, SUM0 + 256 * h, [[1, P], [C0, HJ * G0], [1, C0]]),
                                V(r64, 0, HJ * G0 * h, [[1, P], [1, HJ * G0], [0, C0]]), ALU.mult
                                ).then_inc(sem("o_tok"), 1)

            def je(t):
                return t[:, :, :]

            def bc(t):
                return V(t, 0, 0, [[1, P], [1, J], [0, E]])

            def first_of_max(src, m, dst):
                step(v.tensor_reduce(m[:, :], je(src), AX.X, ALU.max))
                step(v.tensor_tensor(je(t1), je(src), bc(m), ALU.is_equal))
                step(v.tensor_tensor(je(t1), je(t1), je(jneg), ALU.mult))
                step(v.tensor_reduce(den[:, :], je(t1), AX.X, ALU.max))
                step(v.tensor_tensor(je(dst), je(t1), bc(den), ALU.is_equal))

            for e in range(E):
                last = v.memset(jneg[:, :, e:e + 1], float(E - e))
            step(last)
            def residual1(h):
                dve.wait_ge(sem("x1_ps"), h + 1)
                cols = slice(HJ * h, HJ * h + HJ)
                step(v.tensor_tensor(x1[:, cols, :], x0[:, cols, :], bank(2 + h, 0, P, [1, 256]), ALU.add))
            layernorm(2, x1, 1e-5, 1, residual1)
            dve.wait_ge(sem("gate_ps"), 2)
            step(v.tensor_copy(V(lg, 0, 0, [[1, P], [HJ * E, 2], [1, HJ * E]]), bank(4, 0, P, [512, 2], [1, HJ * E])))
            first_of_max(lg, m1, oh1)
            v.tensor_tensor(je(lgw), je(lg), bc(m1), ALU.subtract).then_inc(sem("gate_in"), 1)
            step(v.tensor_scalar(je(t2), je(oh1), -BIGV, None, ALU.mult))
            step(v.tensor_tensor(je(t2), je(lg), je(t2), ALU.add))
            first_of_max(t2, m2, oh2)
            step(v.tensor_tensor(je(oh1), je(oh1), je(oh2), ALU.add))
            dve.wait_ge(sem("gate_ex"), 1)
            step(v.tensor_reduce(den[:, :], je(ex), AX.X, ALU.add))
            step(v.reciprocal(m2[:, :], den[:, :]))
            step(v.tensor_tensor(je(t1), je(oh1), je(ex), ALU.mult))
            step(v.tensor_tensor(je(cw), je(t1), bc(m2), ALU.mult))
            dve.wait_ge(sem("pads_zero"), 1)
            step(v.tensor_copy(cw_parts[:, :, 0:E], je(cw)))
            step(v.tensor_tensor(je(cw_rest), je(cw), cw_parts[:, :, 0:E], ALU.subtract))
            step(v.tensor_copy(cw_parts[:, :, E:2 * E], je(cw_rest)))
            step(v.tensor_tensor(je(cw_rest), je(cw_rest), cw_parts[:, :, E:2 * E], ALU.subtract))
            v.tensor_copy(cw_parts[:, :, 2 * E:3 * E], je(cw_rest)).then_inc(sem("cw"), 1)
            dve.wait_ge(sem("pidx"), 3)
            step(v.tensor_scalar(pidx[:, 1:2], pidx[:, 0:1], 1, 1, ALU.bitwise_and, ALU.bitwise_and))
            step(v.tensor_scalar(pidx[:, 2:3], pidx[:, 0:1], 1, 15, ALU.logical_shift_right, ALU.bitwise_and))
            step(v.tensor_scalar(pidx[:, 3:4], pidx[:, 0:1], 4, 3, ALU.logical_shift_right, ALU.bitwise_and))
            step(v.tensor_copy(pf[:, :], pidx[:, :]))
            step(v.tensor_scalar(pf[:, 1:2], pf[:, 1:2], float(HC), None, ALU.mult))
            v.tensor_scalar(gsel[:, :], e4[:, :], pf[:, 3:4], None, ALU.is_equal).then_inc(sem("gsel"), 1)
            for c0, col in ((0, 1), (GP1, 2)):
                vw = V(base1, 0, c0, [[1, P], [2 * GP1, J], [1, GP1]])
                step(v.tensor_scalar(vw, vw, pf[:, col:col + 1], None, ALU.add))
            def add_outputs(hf):
                dve.wait_ge(sem("y0_tok"), hf + 1)
                step(v.tensor_tensor(x2[:, 4 * hf:4 * hf + 4, :], x1[:, 4 * hf:4 * hf + 4, :],
                                     bank(6, 0, P, [1, 4 * C], off=4 * hf * C), ALU.add))

            for u in range(2 * E):
                dve.wait_ge(sem("h0"), u + 1)
                dve.wait_ge(sem("cwb_ps"), u + 1)
                hid = bigv((u % E) * 512, [1, 512])
                v.tensor_tensor(hid, hid, bank(2 + u % 2, 0, F0, [1, 512]), ALU.mult).then_inc(sem("hw"), 1)
                if u == E + 3:
                    add_outputs(0)
                    moments(x2, range(HJ))
                    inverse_std(slice(0, HJ), 1e-6)
                if u == E + 5:
                    dve.wait_ge(sem("rstd"), 5)
                    normalise(x2, 1, range(HJ))

            add_outputs(1)
            moments(x2, range(HJ, J))
            inverse_std(slice(HJ, J), 1e-6)
            dve.wait_ge(sem("rstd"), 6)
            normalise(x2, 1, range(HJ, J))
            dve.wait_ge(sem("imgT_ps"), 2)
            dve.wait_ge(sem("cpad1_zero"), 1)
            pad_image(v.tensor_copy, 1).then_inc(sem("cpad1"), 1)
            dve.wait_ge(sem("off1_ps"), 1)
            step(v.tensor_tensor(V(loc1, 0, 0, [[1, P], [2 * GP1, J], [1, 2 * GP1]]),
                                 bank(2, 0, P, [P, J], [1, 2 * GP1]),
                                 V(base1, 0, 0, [[1, P], [2 * GP1, J], [1, 2 * GP1]]), ALU.add))
            v.tensor_scalar(val1[:, :], loc1[:, :], W - 1.0, None, ALU.is_lt).then_inc(sem("val1"), 1)
            step(v.tensor_scalar(loc1[:, :], loc1[:, :], 0.0, W - 1.0, ALU.max, ALU.min))
            v.tensor_tensor(u1[:, :], loc1[:, :], base1[:, :], ALU.subtract).then_inc(sem("off1"), 1)
            dve.wait_ge(sem("off1"), 1)
            v.tensor_reduce(flagf[:, 1:2], u1[:, :], AX.X, ALU.max, apply_absolute_value=True
                            ).then_inc(sem("off_max"), 1)
            NT = J * 2 * GP1
            dve.wait_ge(sem("val1"), 1)
            v.scalar_tensor_tensor(bigv(T1 + 2 * NT, [1, NT]), u1[:, :], 0.0, val1[:, :], ALU.max, ALU.mult)
            dve.wait_ge(sem("neg_val1"), 1)
            v.scalar_tensor_tensor(bigv(T1, [1, NT]), u1[:, :], 0.0, ml[:, :], ALU.min, ALU.mult)
            dve.wait_ge(sem("tent1"), 2)
            v.tensor_tensor(bigv(T1 + NT, [1, NT]), loc1[:, :], val1[:, :], ALU.mult).then_inc(sem("tents1"), 1)
            dve.wait_ge(sem("tents1"), 1)
            flag_finish(1, 6, 1.0, ALU.is_gt)
            flag = dve.value_load(flagi[0:1, 1:2], min_val=0, max_val=1)
            for d in range(9 - POOL_PAIRS):
                pair_weights(v, d)
            dve.wait_ge(sem("pairs"), 9)
            with dve.If(flag > 0):
                seen = {"even": 0, "odd": 0}
                for k in range(POOL_TOTAL):
                    dve.wait_ge(sem("pool_pr1"), k + 1)
                    chain, count = POOL_USED(k)
                    dve.sem_inc(sem(chain), count - seen[chain])
                    seen[chain] = count

                def prepare1():
                    for c0 in (0, GP1):
                        for t in range(3):
                            for g in range(G1):
                                o = c0 + g * K + (t if c0 == 0 else 3 * t)
                                vw = V(u1, 0, o, [[1, P], [2 * GP1, J], [3 if c0 == 0 else 1, 3]])
                                v.tensor_scalar(vw, vw, float(t - 1), None, ALU.add).then_inc(sem("general_prep1"), 1)
                    dve.wait_ge(sem("general_prep1"), 24)
                    for c0, dst in ((0, ox), (GP1, oy)):
                        v.tensor_copy(V(dst, 0, 0, [[1, P], [GP1, J], [1, GP1]]),
                                      V(u1, 0, c0, [[1, P], [2 * GP1, J], [1, GP1]])).then_inc(sem("general_prep1"), 1)
                    v.tensor_tensor(V(ml, 0, 0, [[1, P], [GP1, J], [1, GP1]]),
                                    V(val1, 0, 0, [[1, P], [2 * GP1, J], [1, GP1]]),
                                    V(val1, 0, GP1, [[1, P], [2 * GP1, J], [1, GP1]]), ALU.mult
                                    ).then_inc(sem("general_prep1"), 1)
                    v.memset(bigv(SM, [1, J * K1 * C]), 0.0).then_inc(sem("general_prep1"), 1)
                    dve.wait_ge(sem("general_prep1"), 28)

                def consume1(istep, slab):
                    istep(v.tensor_tensor(fx[:, 0:J * GP1], fx[:, 0:J * GP1], ml[:, 0:J * GP1], ALU.mult))
                    for p in range(K):
                        istep(v.tensor_tensor(V(ring, 0, 3072, [[1, P], [C1, J * G1], [1, C1]]),
                                              slab.rearrange("p (g c) -> p g c", c=C1),
                                              V(fx, 0, p, [[1, P], [K, J * G1], [0, C1]]), ALU.mult))
                        for q in (p,) if p < K - 1 else (p, K):
                            smp = bigv(SM + q * C, [K1 * C, J], [1, C])
                            istep(v.tensor_tensor(smp, smp, V(ring, 0, 3072, [[1, P], [C, J], [1, C]]), ALU.add))
                tent_loop(1, J * GP1, ox[:, 0:J * GP1], oy[:, 0:J * GP1], prepare1, consume1)
                dve.sem_inc(sem("sampled"), 5)
            with dve.Else():
                dve.wait_ge(sem("slab1"), 128)
                def rv(slot, kt):
                    return V(product_slot(slot), 0, 0, [[1, P], [512, TAPS(kt)], [C, J], [1, C]])

                n_extra = 0
                for kt in range(5):
                    done = {"even": EVENS * kt, "odd": ODDS * kt}

                    def add(chain, source):
                        dve.wait_ge(sem(chain), done[chain])
                        done[chain] += 1
                        total = rv(CHAIN_SLOT[chain], kt)
                        v.tensor_tensor(total, total, rv(source, kt), ALU.add).then_inc(sem(chain), 1)

                    extra = kt not in POOL_MORE
                    if extra:
                        sample_product(v, EXTRA_SLOT, kt, DVE_D[2]).then_inc(sem("extra"), 1)
                        n_extra += 1
                    if kt:
                        dve.wait_ge(sem("even"), EVENS * kt)
                    for chain, d in (("even", DVE_D[0]), ("odd", DVE_D[1])):
                        sample_product(v, CHAIN_SLOT[chain], kt, d).then_inc(sem(chain), 1)
                        done[chain] += 1
                    for i, k in enumerate(TILE_ADDS[kt]):
                        chain = ("even", "odd")[i % 2]
                        if k is None:
                            dve.wait_ge(sem("extra"), n_extra)
                            add(chain, EXTRA_SLOT)
                        else:
                            dve.wait_ge(sem("pool_pr1"), k + 1)
                            add(chain, k % POOL_SLOTS)
                    dve.wait_ge(sem("even"), done["even"])
                    dve.wait_ge(sem("odd"), done["odd"])
                    if kt < 4:
                        dst = bigv(SM + kt * P, [C, TAPS(kt)], [K1 * C, J], [1, C])
                        ins = rv(CHAIN_SLOT["even"], kt), rv(CHAIN_SLOT["odd"], kt)
                    else:
                        dst = bigv(SM + kt * P, [K1 * C, J], [C, 2], [1, C])
                        ins = [V(ring, 0, CHAIN_SLOT[c] * 1024, [[1, P], [C, J], [0, 2], [1, C]])
                               for c in ("even", "odd")]
                    v.tensor_tensor(dst, ins[0], ins[1], ALU.add).then_inc(sem("even"), 1)
                    dve.wait_ge(sem("even"), EVENS * (kt + 1))
                    dve.sem_inc(sem("sampled"), 1)
            dve.wait_ge(sem("b_cv_ps"), 1)
            v.tensor_tensor(b_cv[:, :], b_pw[:, :], bank(7, 0, C, [1, 1]), ALU.add).then_inc(sem("b_cv"), 1)
            dve.wait_ge(sem("conv_ps"), 1)
            for b in range(B):
                v.tensor_copy(V(convT_of, C, b * H * W, [[1, C], [1, (H - 1) * W]]),
                                     bank(4, C, P, [1, (H - 1) * W], off=b * H * W + W)).then_inc(sem("convT_up"), 1)
            v.memset(V(convT_of, C, (H - 1) * W, [[1, C], [H * W, B], [1, W]]), 0.0).then_inc(sem("convT_up"), 1)

            def residual3(h):
                dve.wait_ge(sem("x3_ps"), h + 1)
                cols = slice(HJ * h, HJ * h + HJ)
                step(v.tensor_tensor(x3[:, cols, :], x2[:, cols, :], bank(2 + h, 0, P, [1, 256]), ALU.add))
            layernorm(4, x3, 1e-5, 1, residual3)
            dve.wait_ge(sem("gate_ps"), 4)
            step(v.tensor_copy(V(lg, 0, 0, [[1, P], [HJ * E, 2], [1, HJ * E]]), bank(4, 0, P, [512, 2], [1, HJ * E])))
            first_of_max(lg, m1, oh1)
            v.tensor_tensor(je(lgw), je(lg), bc(m1), ALU.subtract).then_inc(sem("gate_in"), 1)
            v.tensor_reduce(total1[:, :], V(oh1, 0, 0, [[1, P], [1, E], [E, J]]), AX.X, ALU.add).then_inc(sem("tot"), 1)
            step(v.tensor_copy(cum[:, 0, :], oh1[:, 0, :]))
            for j in range(1, J):
                step(v.tensor_tensor(cum[:, j, :], cum[:, j - 1, :], oh1[:, j, :], ALU.add))
            dve.wait_ge(sem("before"), 1)
            step(v.tensor_tensor(je(t2), je(cum), bank(5, 0, P, [0, J], [1, E]), ALU.add))
            step(v.tensor_tensor(je(t2), je(t2), je(oh1), ALU.mult))
            step(v.tensor_reduce(posf[:, :], je(t2), AX.X, ALU.add))
            step(v.tensor_scalar(slot[:, :], den[:, :], -float(CAP), float(E * CAP - 1), ALU.mult, ALU.add))
            step(v.scalar_tensor_tensor(slot[:, :], posf[:, :], float(CAP), slot[:, :], ALU.min, ALU.add))
            step(v.tensor_scalar(lost[:, :], posf[:, :], float(CAP), None, ALU.is_gt))
            step(v.tensor_tensor(posf[:, :], trash[:, :], slot[:, :], ALU.subtract))
            step(v.tensor_tensor(posf[:, :], posf[:, :], lost[:, :], ALU.mult))
            step(v.tensor_tensor(posf[:, :], posf[:, :], slot[:, :], ALU.add))
            v.tensor_copy(idx_in[:, :], posf[:, :]).then_inc(sem("idx"), 1)
            v.tensor_copy(idx_out[:, :], slot[:, :]).then_inc(sem("idx"), 1)
            step(v.tensor_scalar(lost[:, :], lost[:, :], -1.0, 1.0, ALU.mult, ALU.add))
            dve.wait_ge(sem("gate_ex"), 2)
            step(v.tensor_reduce(den[:, :], je(ex), AX.X, ALU.add))
            step(v.reciprocal(m2[:, :], den[:, :]))
            step(v.tensor_tensor(wtok[:, :], lost[:, :], m2[:, :], ALU.mult))
            v.memset(V(big, C, XST, [[1, C], [1, SLOTS]]), 0.0).then_inc(sem("xsT_zero"), 1)
            dve.wait_ge(sem("xsT_zero"), 1)
            v.memset(V(big, C, XST, [[1, 1], [1, SLOTS]]), 1.0).then_inc(sem("xsT"), 1)
            dve.wait_ge(sem("xs_ps"), 1)
            v.tensor_copy(bigv(XST + 1024, [1, SLOTS - 1024], p=C), bank(2, 0, C, [1, SLOTS - 1024])
                          ).then_inc(sem("xsT2"), 1)
            for nb in range(HB):
                if nb % 2:
                    dve.wait_ge(sem("h1_ps"), nb + 1)
                    w = min(3, 2 * E - 3 * nb) * CAP
                    v.tensor_scalar(bigv(HS + nb * 3 * CAP, [1, w]), bank(nb, 0, P, [1, w]), 0.0, None, ALU.max
                                    ).then_inc(sem("h1_dve"), 1)
            dve.wait_ge(sem("w_ffn1"), 64)
            for g in (0, 2):
                dve.wait_ge(sem("yT_ps"), g + 1)
                b, e0, ne = Y_GROUPS[g]
                for e in range(e0, e0 + ne):
                    last = v.tensor_scalar(bigv(YT + e * QE, [P, ST_N], [1, QE], p=C),
                                           bank(b, 0, C, [QE, ST_N], [1, QE], off=(e - e0) * CAP),
                                           b_21[:, e:e + 1], None, ALU.add)
                last.then_inc(sem("yT"), 1)
            dve.wait_ge(sem("ys_ps"), 1)
            v.tensor_copy(bigv(YS, [1, 8 * C]), bank(3, 0, P, [1, 8 * C])).then_inc(sem("ys"), 1)
            dve.wait_ge(sem("limits"), 1)
            for h, cols in enumerate(LAST):
                j0, nj = cols.start, cols.stop - cols.start
                dve.wait_ge(sem(f"gathered{h}"), 16 * nj)
                step(v.tensor_tensor(ysum[:, cols, :], bigv(YG + j0 * C, [C, nj], [1, C]),
                                     V(wtok, 0, j0, [[1, P], [1, nj], [0, C]]), ALU.mult))
                ys = V(ysum, 0, j0 * C, [[1, P], [1, nj * C]])
                masks = [nmask[:, (i * J + j0) * C:(i * J + j0 + nj) * C] for i in range(3)]
                v.tensor_scalar(masks[0], ys, BIGV, None, ALU.is_gt)
                v.tensor_scalar(masks[1], ys, -BIGV, None, ALU.is_lt)
                step(v.tensor_tensor(masks[2], ys, ys, ALU.not_equal))
                for i, mask in enumerate(masks):
                    step(v.copy_predicated(ys, mask, V(big1e4, 0, i, [[1, P], [0, nj * C]])))
                v.tensor_tensor(x0[:, cols, :], x3[:, cols, :], ysum[:, cols, :], ALU.add).then_inc(sem("x4"), 1)


def V2(t, dims, off=0):
    if isinstance(t, bass.AP):
        return bass.AP(tensor=t.tensor, offset=t.offset + off, ap=[list(d) for d in dims])
    return bass.AP(tensor=t, offset=off, ap=[list(d) for d in dims])


DISPLACED = [w for w in range(N0 * N0) if not (w // N0 in (0, N0 - 1) and w % N0 in (0, N0 - 1))]


def OWNER(w):
    return PATTERN[DISPLACED.index(w) % len(PATTERN)]


PATTERN = ("sum", "pool", "sum", "pool", "dve", "pool", "pool")


def A_OWNER(dx, dy):
    if dx in (0, D0 - 1) and dy in (0, D0 - 1):
        return None
    return ("sum", "pool", "pool" if dx % 2 else "dve", "sum", "pool")[dy]


A_ORDER = [(dx, dy) for dx in range(D0) for dy in range(D0) if A_OWNER(dx, dy) in ("pool", "dve")]
A_TOTAL = len(A_ORDER)


def A_BY(wx):
    return sum(dx <= wx for dx, _ in A_ORDER)


FLAG_AT = (4, 16, 11)
DVE_TENTS = 2


def A_ORDER_OF(who):
    return [c for c in A_ORDER if A_OWNER(*c) == who]


def A_COUNT(who, i):
    return A_ORDER.index(A_ORDER_OF(who)[i]) + 1


Y_GROUPS = ((6, 0, 3), (0, 3, 3), (1, 6, 2))
LAST = (slice(0, 5), slice(5, J))
POOL0, SUM0, OWN0 = 4 * 512, 8 * 512, 9 * 512
PE_ORDER = [w for w in DISPLACED if OWNER(w) != "sum"]


def PE_COUNT(w):
    return PE_ORDER.index(w) + 1


AHEAD = 6


def TAPS(kt):
    return 2 if kt < 4 else 1


DVE_D = (0, 3, 6)
POOL_MORE = (1, 3)
POOL_SLOTS, CHAIN_SLOT, EXTRA_SLOT = 4, {"even": 4, "odd": 5}, 6
EVENS, ODDS = 6, 4


def POOL_D(kt):
    return (1, 2, 6, 4, 5, 7, 8) if kt in POOL_MORE else (1, 2, 4, 5, 7, 8)


TILE_ADDS, POOL_TOTAL = [], 0
for _kt in range(5):
    _own = list(range(POOL_TOTAL, POOL_TOTAL + len(POOL_D(_kt))))
    POOL_TOTAL += len(_own)
    TILE_ADDS.append(_own if _kt in POOL_MORE else _own[:2] + [None] + _own[2:])


def POOL_USED(k):
    kt = next(t for t in range(5) if k in TILE_ADDS[t])
    i = TILE_ADDS[kt].index(k)
    return ("odd", ODDS * kt + 1 + (i + 1) // 2) if i % 2 else ("even", EVENS * kt + 2 + i // 2)


NEXT_TILE = (5, 5, 5, 3)
POOL_PAIRS = 4


INPUTS = ["x", "dc", "w_in", "om", "omb", "w_out", "w_g0", "w_10", "w_20", "b_20", "w_i1", "w_of_a", "w_of_b",
          "b_of", "w_dp_a", "w_dp_b", "b_pw", "w_g1", "w_11", "w_21", "b_21"]


def kernel(**inputs):
    import numpy as np
    import concourse.bacc as _bacc
    from concourse.bass_utils import run_bass_kernel_spmd as _run

    i = {k: np.asarray(v) for k, v in inputs.items()}

    def rows(*parts):
        return np.concatenate(parts, axis=0)

    om = i["L0_conv_off_w"].reshape(C, GP0, 2).transpose(0, 2, 1).reshape(C, 2 * GP0)
    omb = i["L0_conv_off_b"].reshape(GP0, 2).transpose(1, 0).reshape(2 * GP0)
    w_of = i["L1_conv_w_off"].reshape(G1, 3, 3, C1, K, 2).transpose(1, 0, 3, 2, 5, 4).reshape(3 * C, 54)
    b_of = i["L1_conv_b_off"].reshape(G1, K, 2).transpose(2, 0, 1).reshape(72, 1)
    w_dw = i["L1_conv_w_dw"].reshape(G1, K, K, C1).transpose(2, 0, 3, 1).reshape(K * C, K)
    w_pw = i["L1_conv_w_pw"].reshape(G1, K, C1, C1).transpose(1, 0, 2, 3).reshape(K * C, C1)
    b_dw = i["L1_conv_b_dw"].reshape(G1, K, C1).transpose(1, 0, 2).reshape(K * C, 1)
    w_dp = np.concatenate([w_dw, w_pw, b_dw], axis=1)
    data = {
        "x": i["x"],
        "dc": np.concatenate([i["L0_conv_dw_k"].reshape(C, K)] +
                             [i["L0_conv_bn_" + s].reshape(C, 1) for s in "gbmv"], axis=1),
        "w_in": rows(i["L0_conv_in_w"], i["L0_conv_in_b"][None]),
        "om": np.concatenate([om, i["L0_conv_mask_w"]], axis=1),
        "omb": np.concatenate([omb, i["L0_conv_mask_b"]]),
        "w_out": rows(i["L0_conv_out_w"], i["L0_conv_out_b"][None]),
        "w_g0": rows(i["L0_ffn_gate_w"], i["L0_ffn_gate_b"][None]),
        "w_10": rows(i["L0_ffn_W1"].transpose(1, 0, 2).reshape(C, E * F0), i["L0_ffn_b1"].reshape(1, E * F0)),
        "w_20": i["L0_ffn_W2"].transpose(1, 0, 2).reshape(F0, E * C),
        "b_20": rows(*[i["L0_ffn_b2"]] * NPART),
        "w_i1": rows(i["L1_conv_w_init"].reshape(C, C), i["L1_conv_b_init"][None]),
        "w_of_a": w_of[:P], "w_of_b": w_of[P:],
        "b_of": b_of,
        "w_dp_a": w_dp[:4 * P], "w_dp_b": w_dp[4 * P:],
        "b_pw": i["L1_conv_b_pw"].reshape(C, 1),
        "w_g1": rows(i["L1_ffn_gate_w"], i["L1_ffn_gate_b"][None]),
        "w_11": rows(i["L1_ffn_w1"].transpose(1, 0, 2).reshape(C, E * F1), i["L1_ffn_b1"].reshape(1, E * F1)),
        "w_21": i["L1_ffn_w2"].reshape(E * F1, C),
        "b_21": i["L1_ffn_b2"].T,
    }
    nc = _bacc.Bacc("TRN2", target_bir_lowering=False, num_devices=1)
    arrays, aps = {}, {}
    for name in INPUTS:
        v = np.ascontiguousarray(data[name])
        arrays[f"in_{name}_dram"] = v
        aps[name] = nc.dram_tensor(f"in_{name}_dram", v.shape, F32, kind="ExternalInput").ap()
    out = nc.dram_tensor("out_0_dram", (B, H, W, C), F32, kind="ExternalOutput").ap()
    program(nc, aps, out)
    r = _run(nc, [arrays], core_ids=[0])
    return r.results[0]["out_0_dram"]
```
